# Optimizing a Trainium2 kernel written in Bass

```python
import numpy as np
import jax
import jax.numpy as jnp

def _softmax(x, axis=-1):
    return jax.nn.softmax(x, axis=axis)

def _gelu(x):
    return jax.nn.gelu(x, approximate=True)

def _silu(x):
    return jax.nn.silu(x)

def _sigmoid(x):
    return jax.nn.sigmoid(x)

def _layernorm(x, axis=-1, eps=1e-05):
    m = jnp.mean(x, axis=axis, keepdims=True)
    v = jnp.var(x, axis=axis, keepdims=True)
    return (x - m) / jnp.sqrt(v + eps)

def _scatter_add(tgt, idx, src, axis=0):
    return tgt.at[idx].add(src)

def _segment_sum(src, seg, n):
    return jax.ops.segment_sum(src, seg, n)
kernel_name = 'mk_seq_postln_d2_jaxref_r4_0a384d'

def setup_inputs(seed: int=0):
    np.random.seed(seed)
    _w = jnp.asarray

    def _L0_attn_setup():
        import jax, jax.numpy as jnp
        import numpy as np
        B, T, D, H, NT = (2, 512, 256, 16, 7)
        HD = D // H
        TEMP = 0.5
        key = jax.random.key(seed)
        ks = jax.random.split(key, 6)
        x = jax.random.normal(ks[0], (B, T, D), jnp.float32)
        qkv_w = jax.random.normal(ks[1], (3 * D, D), jnp.float32) / np.sqrt(D)
        out_w = jax.random.normal(ks[2], (D, D), jnp.float32) / np.sqrt(D)
        hex_w = jax.random.normal(ks[3], (6, D), jnp.float32) * 0.02
        q6_w = jax.random.normal(ks[4], (6, D), jnp.float32) * 0.02
        tr = np.zeros((NT, 6, 6), dtype=np.float32)
        for i in range(6):
            tr[i] = np.eye(6)
            tr[i, i, i] = -1.0
        tr[6] = -np.eye(6)
        transforms = jnp.asarray(tr)
        transform_weights = jax.random.normal(ks[5], (H, NT), jnp.float32) * 0.01
        hamming_lambda_logit = jnp.asarray(np.log(0.1 / 0.9), jnp.float32)
        scale_logit = jnp.zeros((), jnp.float32)
        sips_alpha = jnp.ones((1,), jnp.float32)
        sips_beta = jnp.full((1,), np.sqrt(HD), jnp.float32)
        return {'x': x, 'qkv_w': qkv_w, 'out_w': out_w, 'hex_w': hex_w, 'hamming_lambda_logit': hamming_lambda_logit, 'q6_w': q6_w, 'transforms': transforms, 'transform_weights': transform_weights, 'scale_logit': scale_logit, 'sips_alpha': sips_alpha, 'sips_beta': sips_beta}
    _L0_attn_in = _L0_attn_setup()

    def _L0_ffn_setup():
        import jax, jax.numpy as jnp
        import numpy as np
        INT4_QMAX = 7.0

        def simulate_quantize_int4(w):
            scale = jnp.max(jnp.abs(w)) / INT4_QMAX
            q = jnp.clip(jnp.round(w / scale), -8.0, 7.0)
            return q * scale
        key = jax.random.key(seed)
        k_x, k_w, k_bias, k_a, k_b = jax.random.split(key, 5)
        d_in, features, rank = (256, 256, 16)
        x = jax.random.normal(k_x, (4, 2048, d_in), dtype=jnp.float32)
        kernel = jax.random.normal(k_w, (d_in, features), dtype=jnp.float32)
        bias = jax.random.normal(k_bias, (features,), dtype=jnp.float32)
        a = jax.random.normal(k_a, (d_in, rank), dtype=jnp.float32) * (1.0 / np.sqrt(d_in))
        b = jax.random.normal(k_b, (rank, features), dtype=jnp.float32) * 0.01
        return {'x': x, 'kernel': kernel, 'bias': bias, 'a': a, 'b': b}
    _L0_ffn_in = _L0_ffn_setup()

    def _L1_attn_setup():
        import jax, jax.numpy as jnp
        import numpy as np
        D_MODEL = 256
        N_HEADS = 16
        HEAD_DIM = D_MODEL // N_HEADS
        ROPE_BASE = 10000.0

        def _rope(q, k):
            S, Dh = (q.shape[1], q.shape[-1])
            inv_freq = 1.0 / ROPE_BASE ** (jnp.arange(0, Dh, 2, dtype=jnp.float32) / Dh)
            t = jnp.arange(S, dtype=jnp.float32)
            freqs = jnp.outer(t, inv_freq)
            emb = jnp.concatenate([freqs, freqs], axis=-1)
            cos = jnp.cos(emb)[None, :, None, :]
            sin = jnp.sin(emb)[None, :, None, :]

            def rotate_half(v):
                v1, v2 = (v[..., :Dh // 2], v[..., Dh // 2:])
                return jnp.concatenate([-v2, v1], axis=-1)
            return (q * cos + rotate_half(q) * sin, k * cos + rotate_half(k) * sin)
        key = jax.random.key(seed)
        ks = jax.random.split(key, 5)
        B, S = (1, 1024)
        scale = 1.0 / np.sqrt(D_MODEL)
        x = jax.random.normal(ks[0], (B, S, D_MODEL), dtype=jnp.float32)
        Wq = jax.random.normal(ks[1], (D_MODEL, D_MODEL), dtype=jnp.float32) * scale
        Wk = jax.random.normal(ks[2], (D_MODEL, D_MODEL), dtype=jnp.float32) * scale
        Wv = jax.random.normal(ks[3], (D_MODEL, D_MODEL), dtype=jnp.float32) * scale
        Wo = jax.random.normal(ks[4], (D_MODEL, D_MODEL), dtype=jnp.float32) * scale
        return {'x': x, 'Wq': Wq, 'Wk': Wk, 'Wv': Wv, 'Wo': Wo}
    _L1_attn_in = _L1_attn_setup()

    def _L1_ffn_setup():
        import jax, jax.numpy as jnp
        import numpy as np
        DIM = 256

        def _reference_tuple_inner(x, W_r, W_k, W_v, mu_r, mu_k):
            B, T, C = x.shape
            x_prev = jnp.concatenate([jnp.zeros((B, 1, C), x.dtype), x[:, :-1, :]], axis=1)
            xr = mu_r * x + (1.0 - mu_r) * x_prev
            xk = mu_k * x + (1.0 - mu_k) * x_prev
            r = jax.nn.sigmoid(jnp.einsum('btc,dc->btd', xr, W_r))
            k = jnp.einsum('btc,dc->btd', xk, W_k)
            k_act = jnp.square(jax.nn.relu(k))
            out = r * jnp.einsum('btc,dc->btd', k_act, W_v)
            new_state = x[:, -1, :]
            return (out, new_state)
        key = jax.random.key(seed)
        ks = jax.random.split(key, 6)
        B, T, C = (8, 512, DIM)
        x = jax.random.normal(ks[0], (B, T, C), dtype=jnp.float32)
        s = 1.0 / np.sqrt(C)
        W_r = jax.random.uniform(ks[1], (C, C), jnp.float32, -s, s)
        W_k = jax.random.uniform(ks[2], (C, C), jnp.float32, -s, s)
        W_v = jax.random.uniform(ks[3], (C, C), jnp.float32, -s, s)
        mu_r = jax.random.uniform(ks[4], (C,), jnp.float32)
        mu_k = jax.random.uniform(ks[5], (C,), jnp.float32)
        return {'x': x, 'W_r': W_r, 'W_k': W_k, 'W_v': W_v, 'mu_r': mu_r, 'mu_k': mu_k}
    _L1_ffn_in = _L1_ffn_setup()
    _d = {'L0_attn_x': _L0_attn_in['x'], 'L0_attn_qkv_w': _L0_attn_in['qkv_w'], 'L0_attn_out_w': _L0_attn_in['out_w'], 'L0_attn_hex_w': _L0_attn_in['hex_w'], 'L0_attn_hamming_lambda_logit': _L0_attn_in['hamming_lambda_logit'], 'L0_attn_q6_w': _L0_attn_in['q6_w'], 'L0_attn_transforms': _L0_attn_in['transforms'], 'L0_attn_transform_weights': _L0_attn_in['transform_weights'], 'L0_attn_scale_logit': _L0_attn_in['scale_logit'], 'L0_attn_sips_alpha': _L0_attn_in['sips_alpha'], 'L0_attn_sips_beta': _L0_attn_in['sips_beta'], 'L0_ffn_kernel': _L0_ffn_in['kernel'], 'L0_ffn_bias': _L0_ffn_in['bias'], 'L0_ffn_a': _L0_ffn_in['a'], 'L0_ffn_b': _L0_ffn_in['b'], 'L1_attn_Wq': _L1_attn_in['Wq'], 'L1_attn_Wk': _L1_attn_in['Wk'], 'L1_attn_Wv': _L1_attn_in['Wv'], 'L1_attn_Wo': _L1_attn_in['Wo'], 'L1_ffn_W_r': _L1_ffn_in['W_r'], 'L1_ffn_W_k': _L1_ffn_in['W_k'], 'L1_ffn_W_v': _L1_ffn_in['W_v'], 'L1_ffn_mu_r': _L1_ffn_in['mu_r'], 'L1_ffn_mu_k': _L1_ffn_in['mu_k']}
    _x0 = _d['L0_attn_x']
    _d['L0_attn_x'] = jax.random.normal(jax.random.fold_in(jax.random.key(seed), 1), (4, 2048, 256), dtype=_x0.dtype)
    del _x0
    return _d

def reference(L0_attn_x, L0_attn_qkv_w, L0_attn_out_w, L0_attn_hex_w, L0_attn_hamming_lambda_logit, L0_attn_q6_w, L0_attn_transforms, L0_attn_transform_weights, L0_attn_scale_logit, L0_attn_sips_alpha, L0_attn_sips_beta, L0_ffn_kernel, L0_ffn_bias, L0_ffn_a, L0_ffn_b, L1_attn_Wq, L1_attn_Wk, L1_attn_Wv, L1_attn_Wo, L1_ffn_W_r, L1_ffn_W_k, L1_ffn_W_v, L1_ffn_mu_r, L1_ffn_mu_k):

    def _L0_attn_ref(x, qkv_w, out_w, hex_w, hamming_lambda_logit, q6_w, transforms, transform_weights, scale_logit, sips_alpha, sips_beta):
        import jax, jax.numpy as jnp
        import numpy as np
        B, T, D, H, NT = (2, 512, 256, 16, 7)
        HD = D // H
        TEMP = 0.5
        b, t, _ = x.shape
        qkv = (x @ qkv_w.T).reshape(b, t, 3, H, HD)
        q = jnp.transpose(qkv[:, :, 0], (0, 2, 1, 3))
        k = jnp.transpose(qkv[:, :, 1], (0, 2, 1, 3))
        v = jnpp = jnp.transpose(qkv[:, :, 2], (0, 2, 1, 3))
        raw = jnp.einsum('bhid,bhjd->bhij', q, k)
        scores = sips_alpha[0] * jnp.tanh(raw / sips_beta[0])
        soft_bits = jnp.tanh(x @ hex_w.T)
        hamming = jnp.einsum('bid,bjd->bij', soft_bits, soft_bits) / 2.0
        lam = jax.nn.sigmoid(hamming_lambda_logit)
        scores = scores + lam * hamming[:, None, :, :]
        hexc = jnp.tanh(x @ q6_w.T)
        w = jax.nn.softmax(transform_weights / TEMP, axis=-1)
        Mh = jnp.einsum('ht,tde->hde', w, transforms)
        lat = jnp.einsum('bid,hde,bje->bhij', hexc, Mh, hexc) / 6.0
        lat = lat * (jax.nn.sigmoid(scale_logit) * 2.0)
        scores = scores + lat
        causal = jnp.tril(jnp.ones((t, t), bool))
        scores = jnp.where(causal[None, None], scores, -jnp.inf)
        attn = jax.nn.softmax(scores, axis=-1)
        out = jnp.einsum('bhij,bhjd->bhid', attn, v)
        out = jnp.transpose(out, (0, 2, 1, 3)).reshape(b, t, D)
        return out @ out_w.T

    def _L0_ffn_ref(x, kernel, bias, a, b):
        import jax, jax.numpy as jnp
        import numpy as np
        INT4_QMAX = 7.0

        def simulate_quantize_int4(w):
            scale = jnp.max(jnp.abs(w)) / INT4_QMAX
            q = jnp.clip(jnp.round(w / scale), -8.0, 7.0)
            return q * scale
        w = simulate_quantize_int4(kernel)
        y = jnp.einsum('bsd,df->bsf', x, w) + bias
        lora = jnp.einsum('bsr,rf->bsf', jnp.einsum('bsd,dr->bsr', x, a), b)
        return y + lora

    def _L1_attn_ref(x, Wq, Wk, Wv, Wo):
        import jax, jax.numpy as jnp
        import numpy as np
        D_MODEL = 256
        N_HEADS = 16
        HEAD_DIM = D_MODEL // N_HEADS
        ROPE_BASE = 10000.0

        def _rope(q, k):
            S, Dh = (q.shape[1], q.shape[-1])
            inv_freq = 1.0 / ROPE_BASE ** (jnp.arange(0, Dh, 2, dtype=jnp.float32) / Dh)
            t = jnp.arange(S, dtype=jnp.float32)
            freqs = jnp.outer(t, inv_freq)
            emb = jnp.concatenate([freqs, freqs], axis=-1)
            cos = jnp.cos(emb)[None, :, None, :]
            sin = jnp.sin(emb)[None, :, None, :]

            def rotate_half(v):
                v1, v2 = (v[..., :Dh // 2], v[..., Dh // 2:])
                return jnp.concatenate([-v2, v1], axis=-1)
            return (q * cos + rotate_half(q) * sin, k * cos + rotate_half(k) * sin)
        B, S, _ = x.shape
        H, Dh = (N_HEADS, HEAD_DIM)
        q = (x @ Wq.T).reshape(B, S, H, Dh)
        k = (x @ Wk.T).reshape(B, S, H, Dh)
        v = (x @ Wv.T).reshape(B, S, H, Dh)
        q, k = _rope(q, k)
        scale = 1.0 / np.sqrt(Dh)
        scores = jnp.einsum('bqhd,bkhd->bhqk', q, k) * scale
        causal = jnp.triu(jnp.ones((S, S), dtype=bool), k=1)
        scores = jnp.where(causal, -jnp.inf, scores)
        attn = jax.nn.softmax(scores, axis=-1)
        out = jnp.einsum('bhqk,bkhd->bqhd', attn, v).reshape(B, S, H * Dh)
        return out @ Wo.T

    def _L1_ffn_ref(x, W_r, W_k, W_v, mu_r, mu_k):
        import jax, jax.numpy as jnp
        import numpy as np
        DIM = 256

        def _reference_tuple_inner(x, W_r, W_k, W_v, mu_r, mu_k):
            B, T, C = x.shape
            x_prev = jnp.concatenate([jnp.zeros((B, 1, C), x.dtype), x[:, :-1, :]], axis=1)
            xr = mu_r * x + (1.0 - mu_r) * x_prev
            xk = mu_k * x + (1.0 - mu_k) * x_prev
            r = jax.nn.sigmoid(jnp.einsum('btc,dc->btd', xr, W_r))
            k = jnp.einsum('btc,dc->btd', xk, W_k)
            k_act = jnp.square(jax.nn.relu(k))
            out = r * jnp.einsum('btc,dc->btd', k_act, W_v)
            new_state = x[:, -1, :]
            return (out, new_state)
        return _reference_tuple_inner(x, W_r, W_k, W_v, mu_r, mu_k)[0]
    x = L0_attn_x
    x = _layernorm(x + _L0_attn_ref(x, L0_attn_qkv_w, L0_attn_out_w, L0_attn_hex_w, L0_attn_hamming_lambda_logit, L0_attn_q6_w, L0_attn_transforms, L0_attn_transform_weights, L0_attn_scale_logit, L0_attn_sips_alpha, L0_attn_sips_beta), axis=-1)
    x = _layernorm(x + _L0_ffn_ref(x, L0_ffn_kernel, L0_ffn_bias, L0_ffn_a, L0_ffn_b), axis=-1)
    x = _layernorm(x + _L1_attn_ref(x, L1_attn_Wq, L1_attn_Wk, L1_attn_Wv, L1_attn_Wo), axis=-1)
    x = _layernorm(x + _L1_ffn_ref(x, L1_ffn_W_r, L1_ffn_W_k, L1_ffn_W_v, L1_ffn_mu_r, L1_ffn_mu_k), axis=-1)
    return x

_drawn_inputs = setup_inputs


def setup_inputs(seed=0):
    import zlib

    import numpy as np

    out = dict(_drawn_inputs(seed))
    spreads = {}
    factors = {'L0_attn_hex_w': 51.062,
     'L0_attn_q6_w': 8.0,
     'L0_attn_transforms': 8.0,
     'L0_attn_transform_weights': 35.511,
     'L0_ffn_a': 8.0,
     'L0_ffn_b': 8.0,
     'L1_ffn_W_r': 2.78,
     'L1_ffn_mu_r': 6.572}
    for name, (base, spread) in spreads.items():
        noise = np.random.default_rng([zlib.crc32(name.encode()), seed]).standard_normal(out[name].shape)
        drawn = base * np.exp(spread * noise) if base else spread * noise
        out[name] = jnp.asarray(drawn.astype(out[name].dtype))
    for name, factor in factors.items():
        out[name] = (out[name] * factor).astype(out[name].dtype)
    return out
```

```python
from contextlib import ExitStack

import concourse.bass as bass
from concourse import mybir

F32 = mybir.dt.float32
BF16 = mybir.dt.bfloat16
I32 = mybir.dt.int32
ACT = mybir.ActivationFunctionType
ALU = mybir.AluOpType
AX = mybir.AxisListType

B, T, D = 4, 2048, 256
H, HD = 16, 16
P = 128
DC = D // P
TG = 512
GB = T // TG
TT = TG // P
KB = T // P
HQ = 4
NHQ = H // HQ
NF = 12
VW = 32
SLOTS_A = (0, 1, 2, 0, 1, 0)
SLOTS_B = (0, 0, 0, 1, 1, 2)
NS = len(SLOTS_A)
QROWS = NS * HD
FROWS = NS * NF
MASKED = -1.0e30
BOUND = 60.0
EPS = 1e-5


APART = (mybir.EngineType.Pool, mybir.EngineType.SP)


def wait(eng, sem, value, passed, apart=False):
    eng.wait_ge(sem, value)
    if apart or eng.engine in APART:
        eng.sem_inc(passed, 1)


class Count:

    CREDIT = 8

    def __init__(self, sem, passed, unit=1):
        self.sem, self.passed, self.unit = sem, passed, unit

    def start(self, eng):
        eng.sem_inc(self.sem, self.CREDIT * self.unit)

    def done(self, ins):
        ins.then_inc(self.sem, self.unit)

    def wait(self, eng, item, apart=False):
        wait(eng, self.sem, (item + (1 + self.CREDIT)) * self.unit, self.passed, apart)


class Stores:

    def __init__(self, sems, passed, n=1):
        self.sems, self.passed, self.unit = sems, passed, 16 * n

    def start(self, eng):
        for sem in self.sems:
            eng.sem_inc(sem, self.unit)

    def done(self, ins, slot):
        ins.then_inc(self.sems[slot], 16)

    def wait(self, eng, slot, use):
        wait(eng, self.sems[slot], (use + 2) * self.unit, self.passed)


class Chain:

    def __init__(self, sem, per_turn=0, turn=0):
        self.sem, self.per_turn, self.turn, self.n = sem, per_turn, turn, 0

    def link(self, eng, ins):
        ins.then_inc(self.sem, 1)
        self.n += 1
        eng.wait_ge(self.sem, self.turn * self.per_turn + self.n)

    def close(self):
        assert not self.per_turn or self.n == self.per_turn, (self.n, self.per_turn)


class Phase:

    def __init__(self, nc, ctx, name):
        self.nc, self.ctx, self.name, self.sems = nc, ctx, name, []
        ctx.callback(self.clear)
        self.passed = self.sem("passed")

    def sb(self, name, shape, dt=F32):
        return self.ctx.enter_context(self.nc.sbuf_tensor(f"{self.name}_{name}", shape, dt))

    def sem(self, name):
        self.sems.append(self.nc.alloc_semaphore(f"{self.name}_{name}"))
        return self.sems[-1]

    def clear(self):
        self.nc.clear_and_free_semaphores(self.sems)
        self.nc.all_engine_barrier()

    def count(self, name, unit=1):
        return Count(self.sem(name), self.passed, unit)

    def stores(self, name, slots, n=1):
        return Stores([self.sem(f"{name}{i}") for i in range(slots)], self.passed, n)


def setup_phase(nc, kn, ins):
    with ExitStack() as ctx:
        ph = Phase(nc, ctx, "setup")
        loaded, done, exps, pe_done, pool_done = (ph.sem(n) for n in ("loaded", "done", "exps", "pe_done", "pool_done"))
        tw = ph.sb("tw", [NF, H, 7])
        tr = ph.sb("tr", [NF, 6, 7])
        mx = ph.sb("mx", [NF, H])
        sm = ph.sb("sm", [NF, H])
        prod = ph.sb("prod", [NF, H, 6, 7])
        mh = ph.sb("mh", [NF, H, 6])
        mag = ph.sb("mag", [NF, H, NF])
        rowabs = ph.sb("rowabs", [NF, H])
        w = ph.sb("w", [P, DC, D])
        sc = ph.sb("sc", [P, 8])
        wmax = ph.sb("wmax", [P, 4])
        scale = ph.sb("scale", [P, 2])
        rows = ph.sb("rows", [P, 2])
        bnd = ph.sb("bnd", [P, 4])
        zero = ph.sb("zero", [P, T], BF16)
        zeroed = ph.sem("zeroed")
        block = ctx.enter_context(nc.Block())

        @block.sync
        def _(sp):
            sp.wait_ge(done, 1)
            with nc.allow_non_contiguous_dma(reason="small table"):
                for d in range(6):
                    sp.dma_start(tr[6 + d:7 + d, :, :], ins["tr"][:, d, :].rearrange("t (o e) -> o e t", o=1)).then_inc(loaded, 16)
            sp.dma_start(tw[:], ins["tw"]).then_inc(loaded, 16)
            sp.dma_start(w[:], ins["kernel0"]).then_inc(loaded, 16)
            sp.dma_start(sc[:, 0:4], ins["scalars"]).then_inc(loaded, 16)
            sp.wait_ge(zeroed, 1)
            n = 0
            for part in range(3):
                for half in range(B * H // 32):
                    sp.dma_start(kn["shift_d"][part, half * 32:half * 32 + 32, :], zero[0:32, :]).then_inc(zeroed, 16)
                    n += 16
            sp.wait_ge(zeroed, 1 + n)

        @block.gpsimd
        def _(pool):
            pool.memset(zero[:], 0.0).then_inc(zeroed, 1)
            pool.wait_ge(pool_done, 1)
            pool.partition_all_reduce(wmax[:, 1:2], wmax[:, 0:1], P, bass.bass_isa.ReduceOp.max).then_inc(pool_done, 1)

        @block.scalar
        def _(act):
            act.wait_ge(loaded, 16 * 9)
            act.activation(sc[:, 4:6], sc[:, 0:2], ACT.Exp, scale=-1.0).then_inc(exps, 1)
            act.wait_ge(exps, 2)
            act.activation(tw[:], tw[:], ACT.Exp, scale=2.0).then_inc(exps, 1)

        @block.tensor
        def _(pe):
            pe.wait_ge(exps, 4)
            pe.matmul(kn["ps"][:, 0, 0:H], kn["ones"][0:NF, :], rowabs[:], start=True, stop=True).then_inc(pe_done, 1)

        @block.vector
        def _(dve):
            ch = Chain(done)
            ch.link(dve, dve.memset(tr[:], 0.0))
            dve.wait_ge(loaded, 16 * 9)
            ch.link(dve, dve.tensor_reduce(mx[:], tw[:], AX.X, ALU.max))
            dve.tensor_tensor(tw[:], tw[:], mx[:].unsqueeze(2).to_broadcast([NF, H, 7]), ALU.subtract).then_inc(exps, 1)
            ch.link(dve, dve.tensor_reduce(wmax[:, 0:1], w[:], AX.XY, ALU.max))
            ch.link(dve, dve.tensor_reduce(wmax[:, 2:3], w[:], AX.XY, ALU.min))
            ch.link(dve, dve.tensor_scalar(wmax[:, 2:3], wmax[:, 2:3], -1.0, None, ALU.mult))
            dve.tensor_tensor(wmax[:, 0:1], wmax[:, 0:1], wmax[:, 2:3], ALU.max).then_inc(pool_done, 1)
            dve.wait_ge(exps, 3)
            ch.link(dve, dve.tensor_scalar(sc[:, 4:6], sc[:, 4:6], 1.0, None, ALU.add))
            ch.link(dve, dve.reciprocal(sc[:, 6:8], sc[:, 4:6]))
            ch.link(dve, dve.tensor_scalar(sc[:, 6:7], sc[:, 6:7], 0.5, None, ALU.mult))
            ch.link(dve, dve.tensor_scalar(sc[:, 7:8], sc[:, 7:8], 1.0 / 3.0, None, ALU.mult))
            ch.link(dve, dve.tensor_copy(kn["alpha"][:], sc[:, 2:3]))
            ch.link(dve, dve.reciprocal(kn["rbeta"][:], sc[:, 3:4]))
            ch.link(dve, dve.tensor_reduce(sm[:], tw[:], AX.X, ALU.add))
            ch.link(dve, dve.reciprocal(sm[:], sm[:]))
            ch.link(dve, dve.tensor_tensor(tw[:], tw[:], sm[:].unsqueeze(2).to_broadcast([NF, H, 7]), ALU.mult))
            for h in range(H):
                ch.link(dve, dve.tensor_tensor(prod[:, h], tr[:], tw[:, h:h + 1, :].to_broadcast([NF, 6, 7]), ALU.mult))
            ch.link(dve, dve.tensor_reduce(mh[:], prod[:], AX.X, ALU.add))
            for h in range(H):
                ch.link(dve, dve.tensor_scalar(kn["C"][:, h, 0:6], kn["ident"][0:NF, 0:6], sc[0:NF, 6:7], None, ALU.mult))
            ch.link(dve, dve.tensor_scalar(kn["C"][:, :, 6:12], mh[:], sc[0:NF, 7:8], None, ALU.mult))
            ch.link(dve, dve.tensor_scalar(mag[:], kn["C"][:], -1.0, None, ALU.mult))
            ch.link(dve, dve.tensor_tensor(mag[:], mag[:], kn["C"][:], ALU.max))
            dve.tensor_reduce(rowabs[:], mag[:], AX.X, ALU.add).then_inc(exps, 1)
            dve.wait_ge(pe_done, 1)
            ch.link(dve, dve.tensor_reduce(bnd[:, 0:1], kn["ps"][:, 0, 0:H], AX.X, ALU.max))
            ch.link(dve, dve.tensor_scalar(bnd[:, 1:2], kn["alpha"][:], -1.0, None, ALU.mult))
            ch.link(dve, dve.tensor_tensor(bnd[:, 1:2], bnd[:, 1:2], kn["alpha"][:], ALU.max))
            ch.link(dve, dve.tensor_tensor(bnd[:, 0:1], bnd[:, 1:2], bnd[:, 0:1], ALU.add))
            ch.link(dve, dve.tensor_scalar(bnd[:, 2:3], bnd[:, 0:1], BOUND, None, ALU.is_le))
            ch.link(dve, dve.tensor_scalar(kn["wide"][:, 0:1], bnd[:, 2:3], -1.0, 1.0, ALU.mult, ALU.add))
            dve.wait_ge(pool_done, 2)
            m, s0, rest = wmax[:, 1:2], scale[:, 0:1], scale[:, 1:2]
            ch.link(dve, dve.tensor_scalar(s0, m, 1.0 / 7.0, None, ALU.mult))
            ch.link(dve, dve.scalar_tensor_tensor(rest, s0, -8.0, m, ALU.mult, ALU.add))
            ch.link(dve, dve.tensor_tensor(rest, rest, s0, ALU.add))
            ch.link(dve, dve.scalar_tensor_tensor(s0, rest, 1.0 / 7.0, s0, ALU.mult, ALU.add))
            ch.link(dve, dve.reciprocal(rest, s0))
            wf = w[:].rearrange("p c n -> p (c n)")
            ch.link(dve, dve.tensor_scalar(wf, wf, rest, None, ALU.mult))
            magic = 12582912.0
            ch.link(dve, dve.tensor_scalar(wf, wf, magic, None, ALU.add))
            ch.link(dve, dve.tensor_scalar(wf, wf, -magic, -8.0, ALU.add, ALU.max))
            ch.link(dve, dve.tensor_scalar(kn["w4"][:].rearrange("p c n -> p (c n)"), wf, 7.0, scale[:, 0:1], ALU.min, ALU.mult))


def project_phase(nc, kn, layer, w, x_d):
    rope = layer == 1
    tiles = ([] if rope else [("g", 0)]) + [("q", 0), ("q", 1), ("k", 0), ("k", 1)] + ([] if rope else [("f", 0), ("f", 1)])
    NTL = len(tiles)
    NTB = GB * NTL
    R = 4
    assert NTB % R == 0
    rows_of = {"q": P, "k": P, "f": 96, "g": NF}
    V_AT = (NTL // 2 - 1, NTL - 1)
    XT0, PRJ0, NORM, VB = 0, 2, 6, 7
    with ExitStack() as ctx:
        ph = Phase(nc, ctx, f"proj{layer}")
        w_in, x_in = ph.sem("w_in"), [ph.sem(f"x_in{i}") for i in range(GB)]
        ones_set = ph.sem("ones_set")
        xt_ps, xt_sb = ph.count("xt_ps"), ph.count("xt_sb")
        prj = ph.count("prj")
        hi, rest, mid, low = (ph.count(n) for n in ("hi", "rest", "mid", "low"))
        parts_out = [ph.sem(f"parts_out{i}") for i in range(R)]
        v_ps, v_sb = ph.count("v_ps"), ph.count("v_sb")
        v_out = ph.stores("v_out", 2, NHQ)
        feat = ph.count("feat")
        raw, swapped, t_cos, t_sin, rot = (ph.count(n) for n in ("raw", "swapped", "t_cos", "t_sin", "rot"))
        sq, norm, nmax = (ph.count(n) for n in ("sq", "norm", "nmax"))
        fold, flag = ph.sem("fold"), ph.sem("flag")
        wq_s, wk_s, wv_s = (ph.sb(n, [P, DC, D]) for n in ("wq", "wk", "wv"))
        xs = ph.sb("xs", [P, GB, TT, D])
        xt = ph.sb("xt", [P, 2, DC, TG])
        parts = ph.sb("parts", [P, R, 3, TG], BF16)
        rem = ph.sb("rem", [P, R, TG])
        vs = ph.sb("vs", [P, 2, TT, H, VW])
        if rope:
            qraw, qrot, qsin = (ph.sb(n, [P, R, TG]) for n in ("qraw", "qrot", "qsin"))
            cos_s, sin_s = ph.sb("cos", [P, T]), ph.sb("sin", [P, T])
            sqr = ph.sb("sqr", [P, R, TG], BF16)
            nrm = ph.sb("nrm", [P, 2, 2 * GB])
            top = ph.sb("top", [P, 8])
        else:
            w12_s, f12 = ph.sb("w12", [P, DC, NF]), ph.sb("f12", [NF, 2, TG])
        n_w = 16 * (5 if rope else 4)
        ps = kn["ps"]
        block = ctx.enter_context(nc.Block())

        def tile_of(jb):
            gq, j = divmod(jb, NTL)
            kind, m = tiles[j]
            return gq, j, kind, m, rows_of[kind], jb % R

        n_stores = [NHQ if tiles[jb % NTL][0] == "g" else 1 for jb in range(NTB)]
        per_batch = [sum(n_stores[r::R]) for r in range(R)]

        def stored(eng, b, jb):
            before, jb = (0, jb) if jb >= 0 else (1, jb + NTB)
            upto = sum(n_stores[jb % R:jb + 1:R])
            wait(eng, parts_out[jb % R], (b * per_batch[jb % R] + (per_batch[jb % R] * (1 - before) + upto)) * 16, ph.passed)

        def x_rows(b, gq):
            return x_d[bass.ds(b * T + gq * TG, TG), :].rearrange("(t p) d -> p t d", p=P)

        @block.sync
        def _(sp):
            for gq in range(GB):
                sp.dma_start(xs[:, gq], x_rows(0, gq)).then_inc(x_in[gq], 16)
                if gq == 0:
                    for name, t in [("wq", wq_s), ("wk", wk_s), ("wv", wv_s)]:
                        sp.dma_start(t[:], w[name]).then_inc(w_in, 16)
                    if rope:
                        sp.dma_start(cos_s[:], w["cos"]).then_inc(w_in, 16)
                        sp.dma_start(sin_s[:], w["sin"]).then_inc(w_in, 16)
                    else:
                        sp.dma_start(w12_s[:], w["w12"]).then_inc(w_in, 16)
            for r in range(R):
                sp.sem_inc(parts_out[r], per_batch[r] * 16)
            v_out.start(sp)
            with sp.Fori(0, B) as b:
                for jb in range(NTB):
                    gq, j, kind, m, n, r = tile_of(jb)
                    low.wait(sp, b * NTB + jb)
                    if kind == "g":
                        for q in range(NHQ):
                            sp.dma_start(kn["g_d"][:, bass.ds((b * NHQ + q) * NF, NF), gq * TG:(gq + 1) * TG].rearrange("k r t -> r k t"),
                                         parts[0:n, r]).then_inc(parts_out[r], 16)
                    else:
                        rows = {"q": D, "k": D, "f": H * NF}[kind]
                        sp.dma_start(kn[f"{kind}_d"][:, bass.ds(b * rows + m * n, n), gq * TG:(gq + 1) * TG].rearrange("k r t -> r k t"),
                                     parts[0:n, r]).then_inc(parts_out[r], 16)
                    if j == NTL - 1:
                        g = b * GB + gq
                        v_sb.wait(sp, g * 2 + 1)
                        for q in range(NHQ):
                            v_out.done(sp.dma_start(
                                kn["v_d"][bass.ds(b * NHQ + q, 1), :, gq * TT:(gq + 1) * TT, :].rearrange("o p k n -> (o p) k n"),
                                vs[:, gq % 2, :, q * HQ:(q + 1) * HQ, :].rearrange("p t h n -> p t (h n)")), gq % 2)
                        xt_ps.wait(sp, g * DC + DC - 1)
                        sp.dma_start(xs[:, gq], x_rows((b + 1) % B, gq)).then_inc(x_in[gq], 16)
            for jb in range(NTB - R, NTB):
                stored(sp, B - 1, jb)
            for u in range(2):
                v_out.wait(sp, u, B * GB // 2 - 1)
            for gq in range(GB):
                sp.wait_ge(x_in[gq], 16 * (B + 1))

        @block.gpsimd
        def _(pool):
            for c in (mid, low, t_cos):
                c.start(pool)
            if rope:
                pool.wait_ge(w_in, n_w)
            LAG = 1 if rope else 0
            with pool.Fori(0, B) as b:
                for s in range(NTB + LAG):
                    if rope and s < NTB:
                        gq, j, kind, m, n, r = tile_of(s)
                        J = b * NTB + s
                        raw.wait(pool, J)
                        rest.wait(pool, J - R)
                        sq.wait(pool, J - R)
                        t_cos.done(pool.tensor_tensor(qrot[:, r], qraw[:, r], cos_s[:, gq * TG:(gq + 1) * TG], ALU.mult))
                    if s >= LAG:
                        gq, j, kind, m, n, r = tile_of(s - LAG)
                        J = b * NTB + s - LAG
                        rest.wait(pool, J)
                        mid.done(pool.tensor_copy(parts[0:n, r, 1], rem[0:n, r]))
                        mid.wait(pool, J)
                        low.done(pool.tensor_tensor(parts[0:n, r, 2], rem[0:n, r], parts[0:n, r, 1], ALU.subtract))
            if rope:
                pool.wait_ge(fold, B + 1)
                pool.partition_all_reduce(top[:, 2:4], top[:, 0:2], P, bass.bass_isa.ReduceOp.max).then_inc(flag, 1)

        @block.scalar
        def _(act):
            for c in (xt_sb, raw, hi, v_sb, feat, sq):
                c.start(act)
            LAG = 1 if rope else 0

            def v_half(b, gq, half):
                g = b * GB + gq
                v_ps.wait(act, g * 2 + half)
                if half == 0:
                    v_out.wait(act, gq % 2, b * (GB // 2) + gq // 2 - 1)
                v_sb.done(act.activation(vs[:, gq % 2, 2 * half:2 * half + 2, :, 0:HD],
                                         ps[:, VB].rearrange("p (t h d) -> p t h d", t=2, h=H), ACT.Copy))

            act.wait_ge(ones_set, 1)
            with act.Fori(0, B) as b:
                for s in range(NTB + LAG):
                    if s < NTB:
                        gq, j, kind, m, n, r = tile_of(s)
                        J, g = b * NTB + s, b * GB + gq
                        if j == 0:
                            v_ps.wait(act, (g - 2) * 2 + 1)
                            for c in range(DC):
                                xt_ps.wait(act, g * DC + c)
                                xt_sb.done(act.activation(xt[:, gq % 2, c], ps[:, XT0 + c], ACT.Copy))
                        if rope:
                            prj.wait(act, J)
                            swapped.wait(act, J - R)
                            t_cos.wait(act, J - R)
                            raw.done(act.activation(qraw[:, r], ps[:, PRJ0 + r], ACT.Copy))
                    if s >= LAG:
                        gq, j, kind, m, n, r = tile_of(s - LAG)
                        J, g = b * NTB + s - LAG, b * GB + gq
                        stored(act, b, s - LAG - R)
                        if rope:
                            rot.wait(act, J)
                            hi.done(act.activation(parts[0:n, r, 0], qrot[0:n, r], ACT.Copy))
                            norm.wait(act, J - R)
                            sq.done(act.activation(sqr[:, r], qrot[:, r], ACT.Square))
                        elif kind == "g":
                            prj.wait(act, J)
                            feat.done(act.activation(f12[:, gq % 2], ps[0:NF, PRJ0 + r], ACT.Tanh))
                            feat.wait(act, g)
                            hi.done(act.activation(parts[0:n, r, 0], f12[:, gq % 2], ACT.Copy))
                        else:
                            prj.wait(act, J)
                            hi.done(act.activation(parts[0:n, r, 0], ps[0:n, PRJ0 + r], ACT.Copy))
                        if j in V_AT:
                            v_half(b, gq, V_AT.index(j))

        @block.tensor
        def _(pe):
            for c in (xt_ps, prj, v_ps, swapped, norm):
                c.start(pe)
            pe.wait_ge(w_in, n_w)
            LAG_S, LAG_N = (1, 3) if rope else (0, 0)
            with pe.Fori(0, B) as b:
                for s in range(NTB + LAG_N):
                    if s < NTB:
                        gq, j, kind, m, n, r = tile_of(s)
                        J, g, u = b * NTB + s, b * GB + gq, gq % 2
                        if j == 0:
                            pe.wait_ge(x_in[gq], 16 * (b + 1))
                            for c in range(DC):
                                xt_sb.wait(pe, (g - 1) * DC + c)
                                for t in range(TT):
                                    mm = pe.transpose(ps[:, XT0 + c, t * P:(t + 1) * P], xs[:, gq, t, c * P:(c + 1) * P], kn["ident"][:])
                                xt_ps.done(mm)
                            xt_sb.wait(pe, g * DC + DC - 1)
                        (t_sin if rope else rest).wait(pe, J - R)
                        if kind == "f":
                            feat.wait(pe, g)
                            mm = pe.matmul(ps[0:n, PRJ0 + r], kn["C"][:].rearrange("p h e -> p (h e)")[:, m * n:(m + 1) * n], f12[:, u], start=True, stop=True)
                        else:
                            for c in range(DC):
                                lhs = w12_s[:, c, :] if kind == "g" else (wq_s if kind == "q" else wk_s)[:, c, m * P:(m + 1) * P]
                                mm = pe.matmul(ps[0:n, PRJ0 + r], lhs, xt[:, u, c], start=c == 0, stop=c == DC - 1)
                        prj.done(mm)
                    if rope and LAG_S <= s < NTB + LAG_S:
                        Js, rs = b * NTB + s - LAG_S, (s - LAG_S) % R
                        raw.wait(pe, Js)
                        swapped.done(pe.matmul(ps[:, PRJ0 + rs], kn["swap"][:], qraw[:, rs], start=True, stop=True))
                    if s < NTB and j in V_AT:
                        half = V_AT.index(j)
                        v_sb.wait(pe, g * 2 + half - 1)
                        for t in range(2 * half, 2 * half + 2):
                            for c in range(DC):
                                mm = pe.matmul(ps[:, VB, (t % 2) * D:(t % 2 + 1) * D], xt[:, u, c, t * P:(t + 1) * P], wv_s[:, c, :], start=c == 0, stop=c == DC - 1)
                        v_ps.done(mm)
                    if rope and s >= LAG_N:
                        J, r = b * NTB + s - LAG_N, (s - LAG_N) % R
                        sq.wait(pe, J)
                        nmax.wait(pe, J - 1)
                        norm.done(pe.matmul(ps[:, NORM], kn["headsum"][:], sqr[:, r], start=True, stop=True))

        @block.vector
        def _(dve):
            for c in (rest, t_sin, rot, nmax):
                c.start(dve)
            dve.memset(vs[:], 1.0).then_inc(ones_set, 1)
            if rope:
                dve.memset(top[:], 0.0).then_inc(fold, 1)
                dve.wait_ge(w_in, n_w)
            LAG, LAG_N = (1, 3) if rope else (0, 0)
            with dve.Fori(0, B) as b:
                for s in range(NTB + LAG_N):
                    if rope and s < NTB:
                        gq, j, kind, m, n, r = tile_of(s)
                        J = b * NTB + s
                        swapped.wait(dve, J)
                        t_sin.done(dve.tensor_tensor(qsin[:, r], ps[:, PRJ0 + r], sin_s[:, gq * TG:(gq + 1) * TG], ALU.mult))
                        t_sin.wait(dve, J)
                        t_cos.wait(dve, J)
                        rot.done(dve.tensor_tensor(qrot[:, r], qrot[:, r], qsin[:, r], ALU.add))
                    if LAG <= s < NTB + LAG:
                        gq, j, kind, m, n, r = tile_of(s - LAG)
                        J = b * NTB + s - LAG
                        hi.wait(dve, J)
                        low.wait(dve, J - R)
                        src = qrot[:, r] if rope else f12[:, gq % 2] if kind == "g" else ps[0:n, PRJ0 + r]
                        rest.done(dve.tensor_tensor(rem[0:n, r], src, parts[0:n, r, 0], ALU.subtract))
                    if rope and s >= LAG_N:
                        gq, j, kind, m, n, r = tile_of(s - LAG_N)
                        J = b * NTB + s - LAG_N
                        norm.wait(dve, J)
                        nmax.done(dve.tensor_reduce(nrm[:, 0 if kind == "q" else 1, gq * 2 + m:gq * 2 + m + 1], ps[:, NORM], AX.X, ALU.max))
                if rope:
                    nmax.wait(dve, b * NTB + NTB - 1)
                    dve.tensor_reduce(top[:, 4:6], nrm[:], AX.X, ALU.max).then_inc(ones_set, 1)
                    dve.wait_ge(ones_set, b + 2)
                    dve.wait_ge(fold, b + 1)
                    dve.tensor_tensor(top[:, 0:2], top[:, 0:2], top[:, 4:6], ALU.max).then_inc(fold, 1)
            if rope:
                dve.wait_ge(flag, 1)
                dve.tensor_tensor(top[:, 6:7], top[:, 2:3], top[:, 3:4], ALU.mult).then_inc(flag, 1)
                dve.wait_ge(flag, 2)
                dve.tensor_scalar(top[:, 7:8], top[:, 6:7], (BOUND * 4 / 1.05) ** 2, None, ALU.is_le).then_inc(flag, 1)
                dve.wait_ge(flag, 3)
                dve.tensor_scalar(kn["wide"][:, 1:2], top[:, 7:8], -1.0, 1.0, ALU.mult, ALU.add)


def load_stacks(eng, kn, layer, it, st, sem):
    n = 0

    def load(dst, src):
        nonlocal n
        eng.dma_start(dst, src).then_inc(sem, 16)
        n += 1

    for s in range(NS):
        load(st["q"][s * HD:(s + 1) * HD], kn["q_d"][SLOTS_A[s], bass.ds(it * HQ * HD, HQ * HD), :].rearrange("(h r) t -> r h t", r=HD))
        load(st["k"][s * HD:(s + 1) * HD], kn["k_d"][SLOTS_B[s], bass.ds(it * HQ * HD, HQ * HD), :].rearrange("(h r) t -> r h t", r=HD))
        if layer == 0:
            load(st["f"][s * NF:(s + 1) * NF], kn["f_d"][SLOTS_A[s], bass.ds(it * HQ * NF, HQ * NF), :].rearrange("(h r) t -> r h t", r=NF))
            load(st["g"][s * NF:(s + 1) * NF], kn["g_d"][SLOTS_B[s], bass.ds(it * NF, NF), :])
    return n


def attend_phase(nc, kn, layer):
    U = 2
    steps = [(g, kb) for g in range(GB) for kb in range((g + 1) * (TG // P))]
    NST = len(steps)
    body = [(u, s) for u in range(U) for s in range(NST)]
    NB = len(body)
    R = 4
    assert NB % R == 0
    QK0, E0, O0 = 0, 4, 6
    SR, FR = (QROWS, FROWS + 3) if layer == 0 else (QROWS + 3, 0)
    with ExitStack() as ctx:
        ph = Phase(nc, ctx, f"att{layer}")
        ones_set = ph.sem("ones_set")
        stacks_in = [ph.sem(f"stacks_in{u}") for u in range(U)]
        stacks_free = [ph.sem(f"stacks_free{u}") for u in range(U)]
        qk = ph.count("qk")
        th = ph.count("th")
        ex = ph.count("ex")
        sc = ph.count("sc")
        pr = ph.count("pr")
        pv = ph.count("pv")
        o_sb, l_ps, l_sb, o_n = (ph.count(n) for n in ("o_sb", "l_ps", "l_sb", "o_n"))
        o_out = ph.stores("o_out", 2, HQ)
        st = []
        for u in range(U):
            s = {"q": ph.sb(f"q{u}", [SR, HQ, T], BF16), "k": ph.sb(f"k{u}", [SR, HQ, T], BF16),
                 "v": ph.sb(f"v{u}", [P, KB, HQ * VW])}
            if layer == 0:
                s["f"], s["g"] = ph.sb(f"f{u}", [FR, HQ, T], BF16), ph.sb(f"g{u}", [FR, T], BF16)
            st.append(s)
        tanh_s = ph.sb("tanh", [P, 2, 2, TG]) if layer == 0 else None
        prob = ph.sb("prob", [P, R, HQ, TG])
        o_s, l_s, on_s = (ph.sb(n, [P, 2, TG]) for n in ("o", "l", "on"))
        ones_row = ph.sb("ones_row", [3, HQ * T if layer else T], BF16)
        ps = kn["ps"]
        N_LOAD = NS * (4 if layer == 0 else 2) + 2
        block = ctx.enter_context(nc.Block())

        def at(i):
            u, s = body[i]
            g, kb = steps[s]
            r = kb - g * (TG // P)
            off = r * P if r > 0 else 0
            return u, s, g, kb, off, r >= 0, kb == (g + 1) * (TG // P) - 1

        @block.sync
        def _(sp):
            sp.wait_ge(ones_set, 1)
            for u in range(U):
                if layer == 0:
                    sp.dma_start(st[u]["g"][FROWS:FROWS + 3], ones_row[:]).then_inc(ones_set, 16)
                else:
                    sp.dma_start(st[u]["k"][QROWS:QROWS + 3], ones_row[:].rearrange("p (h t) -> p h t", h=HQ)).then_inc(ones_set, 16)
            N_IT = B * NHQ

            def load(it, u):
                n = load_stacks(sp, kn, layer, it, st[u], stacks_in[u])
                shift = st[u]["f"][FROWS:FROWS + 3] if layer == 0 else st[u]["q"][QROWS:QROWS + 3]
                sp.dma_start(shift, kn["shift_d"][:, bass.ds(it * HQ, HQ), :]).then_inc(stacks_in[u], 16)
                sp.dma_start(st[u]["v"][:], kn["v_d"][bass.ds(it, 1)].rearrange("o p k n -> (o p) k n")).then_inc(stacks_in[u], 16)
                assert n + 2 == N_LOAD

            o_out.start(sp)
            load(0, 0)
            with sp.Fori(0, N_IT // U) as i:
                for u in range(U):
                    it = i * U + u
                    wait(sp, stacks_free[1 - u], i + 1 + u, ph.passed)
                    load((it + 1) % N_IT, 1 - u)
                    for g in range(GB):
                        o_n.wait(sp, it * GB + g)
                        for h in range(HQ):
                            o_out.done(sp.dma_start(kn["o_d"][bass.ds(it * HQ * HD + h * HD, HD), g * TG:(g + 1) * TG], on_s[VW * h:VW * h + HD, g % 2]), g % 2)
            for u in range(2):
                o_out.wait(sp, u, B * NHQ * GB // 2 - 1)
            sp.wait_ge(stacks_in[0], 16 * N_LOAD * (N_IT // U + 1))

        @block.tensor
        def _(pe):
            for c in (qk, ex, pv, l_ps):
                c.start(pe)
            for u in range(U):
                pe.sem_inc(stacks_free[u], 1)
            pe.wait_ge(ones_set, 1 + 16 * U)
            LAG = 2 if layer == 0 else 1
            with pe.Fori(0, B * NHQ // U) as i:

                def scores(k, pair):
                    u, s, g, kb, off, diag, _ = at(k)
                    S = i * NB + k
                    (th if layer == 0 else pr).wait(pe, S * 2 + pair - 2)
                    for h in (2 * pair, 2 * pair + 1):
                        out = ps[:, QK0 + h, off:TG]
                        mask = layer == 1 and diag
                        mm = pe.matmul(out, st[u]["k"][:, h, kb * P:(kb + 1) * P], st[u]["q"][:, h, g * TG + off:(g + 1) * TG], start=True, stop=not mask)
                        if mask:
                            mm = pe.matmul(ps[:, QK0 + h, off:off + P], kn["identb"][:], kn["mask_kq"][:], start=False, stop=True)
                    qk.done(mm)

                def extra(k, h):
                    u, s, g, kb, off, diag, _ = at(k)
                    S = i * NB + k
                    sc.wait(pe, S * HQ + h - 2)
                    mm = pe.matmul(ps[:, E0 + h % 2, off:TG], st[u]["g"][:, kb * P:(kb + 1) * P], st[u]["f"][:, h, g * TG + off:(g + 1) * TG], start=True, stop=not diag)
                    if diag:
                        mm = pe.matmul(ps[:, E0 + h % 2, off:off + P], kn["identb"][:], kn["mask_kq"][:], start=False, stop=True)
                    ex.done(mm)

                def weigh(k):
                    u, s, g, kb, off, diag, last = at(k)
                    S = i * NB + k
                    if layer == 0:
                        pr.wait(pe, S)
                    else:
                        pr.wait(pe, S * 2 + 1)
                    if kb == 0:
                        l_sb.wait(pe, (i * U + u) * GB + g - 2)
                    for h in range(HQ):
                        mm = pe.matmul(ps[VW * h:VW * (h + 1), O0 + g % 2, off:TG], st[u]["v"][:, kb, h * VW:(h + 1) * VW], prob[:, k % R, h, off:TG], start=kb == 0, stop=last)
                    pv.done(mm)

                def row_sums(k):
                    u, s, g, *_ = at(k)
                    G = (i * U + u) * GB + g
                    o_sb.wait(pe, G)
                    l_ps.done(pe.matmul(ps[:, O0 + g % 2], kn["pick"][:], o_s[:, g % 2], start=True, stop=True))

                for k in range(NB + LAG + 1):
                    if k < NB:
                        u, s, *_ = at(k)
                        if s == 0:
                            pe.wait_ge(stacks_in[u], (i + 1) * (16 * N_LOAD))
                        scores(k, 0)
                        if layer == 0:
                            extra(k, 0)
                            extra(k, 1)
                        scores(k, 1)
                    if LAG <= k < NB + LAG:
                        weigh(k - LAG)
                    if k > LAG and at(k - LAG - 1)[-1]:
                        row_sums(k - LAG - 1)
                    if k < NB and layer == 0:
                        extra(k, 2)
                        extra(k, 3)

        @block.scalar
        def _(act):
            for c in (th, pr):
                c.start(act)
            with act.Fori(0, B * NHQ // U) as i:
                for k in range(NB + 1):
                    if k < NB:
                        u, s, g, kb, off, *_ = at(k)
                        S = i * NB + k
                        for pair in range(2):
                            qk.wait(act, S * 2 + pair)
                            src = ps[:, QK0 + 2 * pair:QK0 + 2 * pair + 2, off:TG]
                            if layer == 0:
                                sc.wait(act, (S - 1) * HQ + 2 * pair + 1)
                                th.done(act.activation(tanh_s[:, pair, :, off:TG], src, ACT.Tanh, scale=kn["rbeta"][:, 0:1]))
                            else:
                                pv.wait(act, S - R)
                                pr.done(act.activation(prob[:, k % R, 2 * pair:2 * pair + 2, off:TG], src, ACT.Exp, scale=float(HD) ** -0.5))
                    if k > 0 and layer == 0:
                        u, s, g, kb, off, *_ = at(k - 1)
                        S = i * NB + k - 1
                        sc.wait(act, S * HQ + HQ - 1)
                        pr.done(act.activation(prob[:, (k - 1) % R, :, off:TG], prob[:, (k - 1) % R, :, off:TG], ACT.Exp))

        @block.vector
        def _(dve):
            dve.memset(ones_row[:], 1.0).then_inc(ones_set, 1)
            for c in (sc, o_sb, l_sb):
                c.start(dve)
            LAG = 2 if layer == 0 else 1
            with dve.Fori(0, B * NHQ // U) as i:
                for k in range(NB + LAG + 2):
                    if LAG < k <= NB + LAG and at(k - LAG - 1)[-1]:
                        u, s, g, *_ = at(k - LAG - 1)
                        G = (i * U + u) * GB + g
                        pv.wait(dve, i * NB + k - LAG - 1)
                        o_n.wait(dve, G - 2)
                        o_sb.done(dve.tensor_copy(o_s[:, g % 2], ps[:, O0 + g % 2]))
                    if k > LAG + 1 and at(k - LAG - 2)[-1]:
                        u, s, g, *_ = at(k - LAG - 2)
                        G = (i * U + u) * GB + g
                        l_ps.wait(dve, G)
                        o_n.wait(dve, G - 2)
                        l_sb.done(dve.reciprocal(l_s[:, g % 2], ps[:, O0 + g % 2]))
                    if k < NB and layer == 0:
                        u, s, g, kb, off, *_ = at(k)
                        S = i * NB + k
                        pv.wait(dve, S - R)
                        for h in range(HQ):
                            th.wait(dve, S * 2 + h // 2)
                            ex.wait(dve, S * HQ + h)
                            sc.done(dve.scalar_tensor_tensor(prob[:, k % R, h, off:TG], tanh_s[:, h // 2, h % 2, off:TG], kn["alpha"][:, 0:1],
                                                             ps[:, E0 + h % 2, off:TG], ALU.mult, ALU.add))

        @block.gpsimd
        def _(pool):
            o_n.start(pool)
            with pool.Fori(0, B * NHQ // U) as i:
                for u in range(U):
                    for g in range(GB):
                        it = i * U + u
                        G = it * GB + g
                        l_sb.wait(pool, G)
                        o_out.wait(pool, g % 2, it * (GB // 2) + g // 2 - 1)
                        o_n.done(pool.tensor_tensor(on_s[:, g % 2], o_s[:, g % 2], l_s[:, g % 2], ALU.mult))
                        if g == GB - 1:
                            pool.sem_inc(stacks_free[u], 1)


def row_max_phase(nc, kn, layer):
    SR, FR = QROWS, FROWS
    with ExitStack() as ctx:
        ph = Phase(nc, ctx, f"max{layer}")
        stacks_in, qk, th, sc, mx, nm, tp, out = (ph.sem(n) for n in ("stacks_in", "qk", "th", "sc", "mx", "nm", "tp", "out"))
        st = {"q": ph.sb("q", [SR, HQ, T], BF16), "k": ph.sb("k", [SR, HQ, T], BF16)}
        if layer == 0:
            st["f"], st["g"] = ph.sb("f", [FR, HQ, T], BF16), ph.sb("g", [FR, T], BF16)
        tanh_s = ph.sb("tanh", [P, TG])
        score = ph.sb("score", [P, TG])
        cmax = ph.sb("cmax", [P, GB])
        nmax = ph.sb("nmax", [P, HQ * KB])
        parts = ph.sb("parts", [HQ * KB, 3, P], BF16)
        rem = ph.sb("rem", [HQ * KB, P])
        flag = ph.sb("flag", [P, 1], I32)
        flagged = ph.sem("flagged")
        ps = kn["ps"]
        N_LOAD = NS * (4 if layer == 0 else 2)
        chunks = [(h, qb, c, min(TG, (qb + 1) * P - c * TG)) for h in range(HQ) for qb in range(KB) for c in range(qb // (TG // P) + 1)]
        NCH = len(chunks)
        NQB = HQ * KB
        with nc.Block() as block:
            @block.vector
            def _(dve):
                dve.tensor_copy(flag[:], kn["wide"][:, layer:layer + 1]).then_inc(flagged, 1)
                dve.wait_ge(flagged, 1)
        block = ctx.enter_context(nc.Block())

        @block.sync
        def _(sp):
            wide = sp.value_load(flag[0:1, 0:1], min_val=0, max_val=1)
            with sp.If(wide == 1):
                with sp.Fori(0, B * NHQ) as it:
                    wait(sp, nm, it + 1, ph.passed)
                    load_stacks(sp, kn, layer, it, st, stacks_in)
                    wait(sp, tp, it * 5 + 5, ph.passed)
                    sp.dma_start(kn["shift_d"][:, bass.ds(it * HQ, HQ), :].rearrange("k h (q p) -> (h q) k p", p=P), parts[:]).then_inc(out, 16)
                    wait(sp, out, (it + 1) * 16, ph.passed)
            sp.nop()

        @block.tensor
        def _(pe):
            wide = pe.value_load(flag[0:1, 0:1], min_val=0, max_val=1)
            with pe.If(wide == 1):
                with pe.Fori(0, B * NHQ) as it:
                    pe.wait_ge(stacks_in, (it + 1) * (16 * N_LOAD))
                    for n, (h, qb, c, w) in enumerate(chunks):
                        pe.wait_ge(mx, it * NCH + n + 1)
                        diag = c == qb // (TG // P)
                        if layer == 1:
                            mm = pe.matmul(ps[:, 0, 0:w], st["q"][:, h, qb * P:(qb + 1) * P], st["k"][:, h, c * TG:c * TG + w], start=True, stop=not diag)
                            if diag:
                                mm = pe.matmul(ps[:, 0, w - P:w], kn["identb"][:], kn["mask_qk"][:], start=False, stop=True)
                        else:
                            pe.matmul(ps[:, 1, 0:w], st["f"][:, h, qb * P:(qb + 1) * P], st["g"][:, c * TG:c * TG + w], start=True, stop=not diag)
                            if diag:
                                pe.matmul(ps[:, 1, w - P:w], kn["identb"][:], kn["mask_qk"][:], start=False, stop=True)
                            mm = pe.matmul(ps[:, 0, 0:w], st["q"][:, h, qb * P:(qb + 1) * P], st["k"][:, h, c * TG:c * TG + w], start=True, stop=True)
                        mm.then_inc(qk, 1)
                    wait(pe, nm, it + 2, ph.passed, apart=True)
                    pe.transpose(ps[0:NQB, 2, 0:P], nmax[:], kn["ident"][:]).then_inc(tp, 1)
            pe.nop()

        @block.scalar
        def _(act):
            wide = act.value_load(flag[0:1, 0:1], min_val=0, max_val=1)
            with act.If(wide == 1):
                if layer == 0:
                    with act.Fori(0, B * NHQ) as it:
                        for n, (h, qb, c, w) in enumerate(chunks):
                            act.wait_ge(qk, it * NCH + n + 1)
                            act.activation(tanh_s[:, 0:w], ps[:, 0, 0:w], ACT.Tanh, scale=kn["rbeta"][:, 0:1]).then_inc(th, 1)
                else:
                    act.nop()
            act.nop()

        @block.vector
        def _(dve):
            wide = dve.value_load(flag[0:1, 0:1], min_val=0, max_val=1)
            with dve.If(wide == 1):
                dve.sem_inc(mx, 1)
                dve.sem_inc(nm, 1)
                with dve.Fori(0, B * NHQ) as it:
                    n_row = 0
                    for n, (h, qb, c, w) in enumerate(chunks):
                        if layer == 0:
                            dve.wait_ge(th, it * NCH + n + 1)
                            dve.scalar_tensor_tensor(score[:, 0:w], tanh_s[:, 0:w], kn["alpha"][:, 0:1], ps[:, 1, 0:w], ALU.mult, ALU.add).then_inc(sc, 1)
                            dve.wait_ge(sc, it * (NCH + NQB) + n_row + n + 1)
                            src = score[:, 0:w]
                        else:
                            dve.wait_ge(qk, it * NCH + n + 1)
                            src = ps[:, 0, 0:w]
                        dve.tensor_reduce(cmax[:, c:c + 1], src, AX.X, ALU.max).then_inc(mx, 1)
                        dve.wait_ge(mx, it * NCH + n + 2)
                        if c == qb // (TG // P):
                            row = h * KB + qb
                            dve.tensor_reduce(nmax[:, row:row + 1], cmax[:, 0:c + 1], AX.X, ALU.max).then_inc(sc, 1)
                            n_row += 1
                            dve.wait_ge(sc, it * ((NCH if layer == 0 else 0) + NQB) + n_row + (n + 1 if layer == 0 else 0))
                    dve.tensor_scalar(nmax[:], nmax[:], -1.0, None, ALU.mult).then_inc(nm, 1)
                    dve.wait_ge(tp, it * 5 + 1)
                    ptile = ps[0:NQB, 2, 0:P]
                    dve.tensor_copy(parts[:, 0], ptile).then_inc(tp, 1)
                    dve.wait_ge(tp, it * 5 + 2)
                    dve.tensor_tensor(rem[:], ptile, parts[:, 0], ALU.subtract).then_inc(tp, 1)
                    dve.wait_ge(tp, it * 5 + 3)
                    dve.tensor_copy(parts[:, 1], rem[:]).then_inc(tp, 1)
                    dve.wait_ge(tp, it * 5 + 4)
                    dve.tensor_tensor(parts[:, 2], rem[:], parts[:, 1], ALU.subtract).then_inc(tp, 1)
            dve.nop()


class Norm:

    def __init__(self, ph, name, slots=2):
        self.slots = slots
        self.st = ph.sb(f"{name}_st", [P, slots, TT, 6])
        self.mv = ph.sb(f"{name}_mv", [P, slots, TT, 2])
        self.sd = ph.sb(f"{name}_sd", [P, slots, TT])
        self.rs = ph.sb(f"{name}_rs", [P, slots, TT])
        self.nb = ph.sb(f"{name}_nb", [P, slots, TT])
        self.stats, self.agg, self.root, self.inv, self.shift, self.out = (
            ph.count(f"{name}_{n}") for n in ("stats", "agg", "root", "inv", "shift", "out"))

    def start(self, dve=None, act=None, pool=None):
        for eng, counts in ((dve, (self.stats, self.agg, self.inv, self.shift)), (act, (self.root,)), (pool, (self.out,))):
            if eng is not None:
                for c in counts:
                    c.start(eng)

    def take(self, dve, g, u, rows, wait_row):
        self.out.wait(dve, g - self.slots)
        for t in range(TT):
            wait_row(t)
            ins = dve.bn_stats(self.st[:, u, t], rows(t))
        self.stats.done(ins)
        self.stats.wait(dve, g, apart=True)
        for t in range(TT):
            ins = dve.bn_aggr(self.mv[:, u, t], self.st[:, u, t])
        self.agg.done(ins)

    def take_root(self, act, g, u, eps):
        self.agg.wait(act, g)
        self.root.done(act.activation(self.sd[:, u], self.mv[:, u, :, 1], ACT.Sqrt, bias=eps))

    def invert(self, dve, g, u):
        self.root.wait(dve, g)
        self.inv.done(dve.reciprocal(self.rs[:, u], self.sd[:, u]))
        self.inv.wait(dve, g)
        self.shift.done(dve.scalar_tensor_tensor(self.nb[:, u], self.mv[:, u, :, 0], -1.0, self.rs[:, u], ALU.mult, ALU.mult))

    def apply(self, pool, g, u, dst, src):
        self.shift.wait(pool, g)
        for t in range(TT):
            ins = pool.tensor_scalar(dst(t), src(t), self.rs[:, u, t:t + 1], self.nb[:, u, t:t + 1], ALU.mult, ALU.add)
        self.out.done(ins)


def post0_phase(nc, kn, w, x_d, out_d):
    Y1, XT0, HB, Y2 = 0, 2, 4, 5
    STAGES = 2
    with ExitStack() as ctx:
        ph = Phase(nc, ctx, "post0")
        w_in, o_in, x_in = ph.sem("w_in"), [ph.sem(f"o_in{i}") for i in range(GB)], [ph.sem(f"x_in{i}") for i in range(GB)]
        y1, r1, y2, r2 = (ph.count(n) for n in ("y1", "r1", "y2", "r2"))
        xt_ps, xt_sb = ph.count("xt_ps"), ph.count("xt_sb")
        h_ps, h_sb, xb = (ph.count(n) for n in ("h_ps", "h_sb", "xb"))
        out = ph.stores("out_dma", 2)
        n1, n2 = Norm(ph, "n1"), Norm(ph, "n2")
        wo = ph.sb("wo", [P, DC, D])
        a_s = ph.sb("a", [P, DC, 16])
        b_s = ph.sb("b", [16, D])
        bias = ph.sb("bias", [P, D])
        o_s = ph.sb("o", [P, GB, DC, TG])
        xs = ph.sb("x", [P, GB, TT, D])
        rr = ph.sb("rr", [P, 2, TT, D])
        x1 = ph.sb("x1", [P, 2, TT, D])
        x1b = ph.sb("x1b", [P, 2, TT, D])
        xt = ph.sb("xt", [P, 2, DC, TG])
        h_s = ph.sb("h", [16, 2, TG])
        rr2 = ph.sb("rr2", [P, 2, TT, D])
        x2 = ph.sb("x2", [P, 2, TT, D])
        ps = kn["ps"]
        block = ctx.enter_context(nc.Block())

        def rows(d, b, gq):
            return d[bass.ds(b * T + gq * TG, TG), :].rearrange("(t p) d -> p t d", p=P)

        def load(sp, b, gq):
            sp.dma_start(o_s[:, gq], kn["o_d"][bass.ds(b * D, D), gq * TG:(gq + 1) * TG].rearrange("(c p) t -> p c t", p=P)).then_inc(o_in[gq], 16)
            sp.dma_start(xs[:, gq], rows(x_d, b, gq)).then_inc(x_in[gq], 16)

        def staged(b):
            for s in range(GB + STAGES - 1):
                for stage in range(STAGES):
                    if 0 <= s - stage < GB:
                        yield stage, s - stage, b * GB + s - stage

        @block.sync
        def _(sp):
            for dst, src in ((wo, w["wo"]), (a_s, w["a"]), (b_s, w["b"]), (bias, w["bias"])):
                sp.dma_start(dst[:], src).then_inc(w_in, 16)
            for gq in range(GB):
                load(sp, 0, gq)
            out.start(sp)
            with sp.Fori(0, B) as b:
                for gq in range(GB):
                    g = b * GB + gq
                    r1.wait(sp, g * 2 + 1)
                    load(sp, (b + 1) % B, gq)
                    n2.out.wait(sp, g)
                    out.done(sp.dma_start(rows(out_d, b, gq), x2[:, gq % 2]), gq % 2)
            for u in range(2):
                out.wait(sp, u, B * GB // 2 - 1)
            for gq in range(GB):
                sp.wait_ge(x_in[gq], 16 * (B + 1))
                sp.wait_ge(o_in[gq], 16 * (B + 1))

        @block.tensor
        def _(pe):
            for c in (y1, xt_ps, h_ps, y2):
                c.start(pe)
            pe.wait_ge(w_in, 64)
            with pe.Fori(0, B) as b:
                for stage, gq, g in staged(b):
                    u = gq % 2
                    if stage == 0:
                        pe.wait_ge(o_in[gq], 16 * (b + 1))
                        for half in range(2):
                            r1.wait(pe, (g - 1) * 2 + half)
                            for t in range(2 * half, 2 * half + 2):
                                for c in range(DC):
                                    mm = pe.matmul(ps[:, Y1 + half, (t % 2) * D:(t % 2 + 1) * D], o_s[:, gq, c, t * P:(t + 1) * P], wo[:, c, :], start=c == 0, stop=c == DC - 1)
                            y1.done(mm)
                    else:
                        n1.out.wait(pe, g)
                        for c in range(DC):
                            xt_sb.wait(pe, (g - 1) * DC + c)
                            for t in range(TT):
                                mm = pe.transpose(ps[:, XT0 + c, t * P:(t + 1) * P], x1[:, u, t, c * P:(c + 1) * P], kn["ident"][:])
                            xt_ps.done(mm)
                        xt_sb.wait(pe, g * DC + DC - 1)
                        h_sb.wait(pe, g - 1)
                        for c in range(DC):
                            mm = pe.matmul(ps[0:16, HB], a_s[:, c, :], xt[:, u, c], start=c == 0, stop=c == DC - 1)
                        h_ps.done(mm)
                        h_sb.wait(pe, g)
                        for half in range(2):
                            r2.wait(pe, (g - 1) * 2 + half)
                            for t in range(2 * half, 2 * half + 2):
                                y = ps[:, Y2 + half, (t % 2) * D:(t % 2 + 1) * D]
                                for c in range(DC):
                                    pe.matmul(y, xt[:, u, c, t * P:(t + 1) * P], kn["w4"][:, c, :], start=c == 0, stop=False)
                                mm = pe.matmul(y, h_s[:, u, t * P:(t + 1) * P], b_s[:], start=False, stop=True)
                            y2.done(mm)

        @block.scalar
        def _(act):
            for c in (xt_sb, h_sb):
                c.start(act)
            n1.start(act=act)
            n2.start(act=act)
            with act.Fori(0, B) as b:
                for stage, gq, g in staged(b):
                    u = gq % 2
                    if stage == 0:
                        n1.take_root(act, g, u, kn["eps"][:, 0:1])
                    else:
                        for c in range(DC):
                            xt_ps.wait(act, g * DC + c)
                            y2.wait(act, (g - 2) * 2 + 1)
                            xt_sb.done(act.activation(xt[:, u, c], ps[:, XT0 + c], ACT.Copy))
                        h_ps.wait(act, g)
                        h_sb.done(act.activation(h_s[:, u], ps[0:16, HB], ACT.Copy))
                        n2.take_root(act, g, u, kn["eps"][:, 0:1])

        @block.vector
        def _(dve):
            for c in (r1, r2):
                c.start(dve)
            n1.start(dve=dve)
            n2.start(dve=dve)
            with dve.Fori(0, B) as b:
                for stage, gq, g in staged(b):
                    u = gq % 2
                    if stage == 0:
                        dve.wait_ge(x_in[gq], 16 * (b + 1))
                        n1.out.wait(dve, g - 2)
                        for half in range(2):
                            y1.wait(dve, g * 2 + half)
                            ts = slice(2 * half, 2 * half + 2)
                            r1.done(dve.tensor_tensor(rr[:, u, ts], ps[:, Y1 + half].rearrange("p (t d) -> p t d", t=2), xs[:, gq, ts], ALU.add))
                        n1.take(dve, g, u, lambda t: rr[:, u, t], lambda t: r1.wait(dve, g * 2 + t // 2))
                        n1.invert(dve, g, u)
                    else:
                        xb.wait(dve, g)
                        n2.out.wait(dve, g - 2)
                        for half in range(2):
                            y2.wait(dve, g * 2 + half)
                            ts = slice(2 * half, 2 * half + 2)
                            r2.done(dve.tensor_tensor(rr2[:, u, ts], ps[:, Y2 + half].rearrange("p (t d) -> p t d", t=2), x1b[:, u, ts], ALU.add))
                        n2.take(dve, g, u, lambda t: rr2[:, u, t], lambda t: r2.wait(dve, g * 2 + t // 2))
                        n2.invert(dve, g, u)

        @block.gpsimd
        def _(pool):
            xb.start(pool)
            n1.start(pool=pool)
            n2.start(pool=pool)
            pool.wait_ge(w_in, 64)
            with pool.Fori(0, B) as b:
                for stage, gq, g in staged(b):
                    u = gq % 2
                    if stage == 0:
                        xt_ps.wait(pool, (g - 2) * DC + DC - 1)
                        n1.apply(pool, g, u, lambda t: x1[:, u, t], lambda t: rr[:, u, t])
                        n1.out.wait(pool, g)
                        r2.wait(pool, (g - 2) * 2 + 1)
                        for t in range(TT):
                            ins = pool.tensor_tensor(x1b[:, u, t], x1[:, u, t], bias[:], ALU.add)
                        xb.done(ins)
                    else:
                        out.wait(pool, u, b * (GB // 2) + gq // 2 - 1)
                        n2.apply(pool, g, u, lambda t: x2[:, u, t], lambda t: rr2[:, u, t])


def post1_phase(nc, kn, w, x_d, out_d):
    Y1, XT0, KK, VR = 0, 1, 3, 5
    STAGES = 3
    with ExitStack() as ctx:
        ph = Phase(nc, ctx, "post1")
        w_in, o_in, x_in = ph.sem("w_in"), [ph.sem(f"o_in{i}") for i in range(GB)], [ph.sem(f"x_in{i}") for i in range(GB)]
        y1, r1 = ph.count("y1"), ph.count("r1")
        xt_ps, xt_sb, edge = ph.count("xt_ps"), ph.count("xt_sb"), ph.count("edge")
        pr_, pk_, mr_, mk_ = (ph.count(n) for n in ("pr", "pk", "mr", "mk"))
        k_ps, k_re, k_sq = (ph.count(n) for n in ("k_ps", "k_re", "k_sq"))
        r_ps, r_sg, v_ps, rv, r2 = (ph.count(n) for n in ("r_ps", "r_sg", "v_ps", "rv", "r2"))
        omitted = ph.sem("one_minus")
        out = ph.stores("out_dma", 2)
        n1, n2 = Norm(ph, "n1"), Norm(ph, "n2")
        wo, wr, wk, wv = (ph.sb(n, [P, DC, D]) for n in ("wo", "wr", "wk", "wv"))
        mu = ph.sb("mu", [P, 2, DC])
        om = ph.sb("om", [P, 2, DC])
        o_s = ph.sb("o", [P, GB, DC, TG])
        xs = ph.sb("x", [P, GB, TT, D])
        rr = ph.sb("rr", [P, 2, TT, D])
        x3 = ph.sb("x3", [P, GB, TT, D])
        xt = ph.sb("xt", [P, 2, DC, TG + 1])
        prev = ph.sb("prev", [P, 2, DC, TG])
        mix = ph.sb("mix", [P, 2, 2, DC, TG])
        kr = ph.sb("kr", [P, DC, TG])
        ka = ph.sb("ka", [P, 2, DC, TG])
        sg = ph.sb("sg", [P, 2, TT, D])
        rr2 = ph.sb("rr2", [P, 2, TT, D])
        x4 = ph.sb("x4", [P, 2, TT, D])
        ps = kn["ps"]
        block = ctx.enter_context(nc.Block())

        def rows(d, b, gq):
            return d[bass.ds(b * T + gq * TG, TG), :].rearrange("(t p) d -> p t d", p=P)

        def load(sp, b, gq):
            sp.dma_start(o_s[:, gq], kn["o_d"][bass.ds(b * D, D), gq * TG:(gq + 1) * TG].rearrange("(c p) t -> p c t", p=P)).then_inc(o_in[gq], 16)
            sp.dma_start(xs[:, gq], rows(x_d, b, gq)).then_inc(x_in[gq], 16)

        def staged(b):
            for s in range(GB + STAGES - 1):
                for stage in range(STAGES):
                    if 0 <= s - stage < GB:
                        yield stage, s - stage, b * GB + s - stage

        @block.sync
        def _(sp):
            for dst, src in ((wo, w["wo"]), (wr, w["wr"]), (wk, w["wk"]), (wv, w["wv"]), (mu, w["mu"])):
                sp.dma_start(dst[:], src).then_inc(w_in, 16)
            for gq in range(GB):
                load(sp, 0, gq)
            out.start(sp)
            with sp.Fori(0, B) as b:
                for gq in range(GB):
                    g = b * GB + gq
                    r1.wait(sp, g * 2 + 1)
                    load(sp, (b + 1) % B, gq)
                    n2.out.wait(sp, g)
                    out.done(sp.dma_start(rows(out_d, b, gq), x4[:, gq % 2]), gq % 2)
            for u in range(2):
                out.wait(sp, u, B * GB // 2 - 1)
            for gq in range(GB):
                sp.wait_ge(x_in[gq], 16 * (B + 1))
                sp.wait_ge(o_in[gq], 16 * (B + 1))

        @block.tensor
        def _(pe):
            for c in (y1, xt_ps, k_ps, r_ps, v_ps):
                c.start(pe)
            pe.wait_ge(w_in, 80)

            def token_rows(bank, lhs, rhs):
                for t in range(2):
                    for c in range(DC):
                        mm = pe.matmul(ps[:, bank, t * D:(t + 1) * D], lhs(t, c), rhs[:, c, :], start=c == 0, stop=c == DC - 1)
                return mm

            with pe.Fori(0, B) as b:
                for stage, gq, g in staged(b):
                    u = gq % 2
                    if stage == 0:
                        pe.wait_ge(o_in[gq], 16 * (b + 1))
                        for half in range(2):
                            r1.wait(pe, g * 2 + half - 1)
                            y1.done(token_rows(Y1, lambda t, c: o_s[:, gq, c, (2 * half + t) * P:(2 * half + t + 1) * P], wo))
                    elif stage == 1:
                        n1.out.wait(pe, g)
                        for c in range(DC):
                            xt_sb.wait(pe, (g - 1) * DC + c)
                            for t in range(TT):
                                mm = pe.transpose(ps[:, XT0 + c, t * P:(t + 1) * P], x3[:, gq, t, c * P:(c + 1) * P], kn["ident"][:])
                            xt_ps.done(mm)
                    else:
                        mk_.wait(pe, g * DC + DC - 1)
                        for m in range(DC):
                            k_re.wait(pe, (g - 1) * DC + m)
                            for c in range(DC):
                                mm = pe.matmul(ps[:, KK + m], wk[:, c, m * P:(m + 1) * P], mix[:, u, 1, c], start=c == 0, stop=c == DC - 1)
                            k_ps.done(mm)
                        mr_.wait(pe, g * DC + DC - 1)
                        for half in range(2):
                            r_sg.wait(pe, (g - 1) * 2 + half)
                            r_ps.done(token_rows(VR + half, lambda t, c: mix[:, u, 0, c, (2 * half + t) * P:(2 * half + t + 1) * P], wr))
                        k_sq.wait(pe, g * DC + DC - 1)
                        for half in range(2):
                            rv.wait(pe, g * 2 + half - 1)
                            v_ps.done(token_rows(VR + 2, lambda t, c: ka[:, u, c, (2 * half + t) * P:(2 * half + t + 1) * P], wv))

        @block.scalar
        def _(act):
            for c in (xt_sb, k_re, r_sg):
                c.start(act)
            n1.start(act=act)
            n2.start(act=act)
            with act.Fori(0, B) as b:
                for stage, gq, g in staged(b):
                    u = gq % 2
                    if stage == 0:
                        n1.take_root(act, g, u, kn["eps"][:, 0:1])
                    elif stage == 1:
                        mr_.wait(act, (g - 2) * DC + DC - 1)
                        mk_.wait(act, (g - 2) * DC + DC - 1)
                        edge.wait(act, g - 1)
                        for c in range(DC):
                            xt_ps.wait(act, g * DC + c)
                            xt_sb.done(act.activation(xt[:, u, c, 1:TG + 1], ps[:, XT0 + c], ACT.Copy))
                    else:
                        for m in range(DC):
                            k_ps.wait(act, g * DC + m)
                            k_sq.wait(act, (g - 1) * DC + m)
                            k_re.done(act.activation(kr[:, m], ps[:, KK + m], ACT.Relu))
                        for half in range(2):
                            r_ps.wait(act, g * 2 + half)
                            rv.wait(act, (g - 2) * 2 + half)
                            r_sg.done(act.activation(sg[:, u, 2 * half:2 * half + 2], ps[:, VR + half].rearrange("p (t d) -> p t d", t=2), ACT.Sigmoid))
                        n2.take_root(act, g, u, kn["eps"][:, 0:1])

        @block.vector
        def _(dve):
            for c in (r1, rv, r2, edge, mr_, mk_):
                c.start(dve)
            n1.start(dve=dve)
            n2.start(dve=dve)
            dve.wait_ge(w_in, 80)
            dve.tensor_scalar(om[:], mu[:], -1.0, 1.0, ALU.mult, ALU.add).then_inc(omitted, 1)
            with dve.Fori(0, B) as b:
                for stage, gq, g in staged(b):
                    u = gq % 2
                    if stage == 0:
                        dve.wait_ge(x_in[gq], 16 * (b + 1))
                        n1.out.wait(dve, g - 2)
                        for half in range(2):
                            y1.wait(dve, g * 2 + half)
                            ts = slice(2 * half, 2 * half + 2)
                            r1.done(dve.tensor_tensor(rr[:, u, ts], ps[:, Y1].rearrange("p (t d) -> p t d", t=2), xs[:, gq, ts], ALU.add))
                        n1.take(dve, g, u, lambda t: rr[:, u, t], lambda t: r1.wait(dve, g * 2 + t // 2))
                        n1.invert(dve, g, u)
                    elif stage == 1:
                        pr_.wait(dve, (g - 2) * DC + DC - 1)
                        pk_.wait(dve, (g - 2) * DC + DC - 1)
                        if gq == 0:
                            ins = dve.memset(xt[:, u, :, 0:1], 0.0)
                        else:
                            xt_sb.wait(dve, g * DC - 1)
                            ins = dve.tensor_copy(xt[:, u, :, 0:1], xt[:, 1 - u, :, TG:TG + 1])
                        edge.done(ins)
                        for c in range(DC):
                            xt_sb.wait(dve, g * DC + c)
                            pk_.wait(dve, g * DC + c)
                            k_ps.wait(dve, (g - 2) * DC + DC - 1)
                            mk_.done(dve.scalar_tensor_tensor(mix[:, u, 1, c], xt[:, u, c, 1:TG + 1], mu[:, 1, c:c + 1], prev[:, 1, c], ALU.mult, ALU.add))
                        for c in range(DC):
                            pr_.wait(dve, g * DC + c)
                            r_ps.wait(dve, (g - 2) * 2 + 1)
                            mr_.done(dve.scalar_tensor_tensor(mix[:, u, 0, c], xt[:, u, c, 1:TG + 1], mu[:, 0, c:c + 1], prev[:, 0, c], ALU.mult, ALU.add))
                    else:
                        n2.out.wait(dve, g - 2)
                        for half in range(2):
                            ts = slice(2 * half, 2 * half + 2)
                            v_ps.wait(dve, g * 2 + half)
                            r_sg.wait(dve, g * 2 + half)
                            rv.done(dve.tensor_tensor(rr2[:, u, ts], ps[:, VR + 2].rearrange("p (t d) -> p t d", t=2), sg[:, u, ts], ALU.mult))
                            rv.wait(dve, g * 2 + half)
                            r2.done(dve.tensor_tensor(rr2[:, u, ts], rr2[:, u, ts], x3[:, gq, ts], ALU.add))
                        n2.take(dve, g, u, lambda t: rr2[:, u, t], lambda t: r2.wait(dve, g * 2 + t // 2))
                        n2.invert(dve, g, u)

        @block.gpsimd
        def _(pool):
            for c in (pr_, pk_, k_sq):
                c.start(pool)
            n1.start(pool=pool)
            n2.start(pool=pool)
            pool.wait_ge(omitted, 1)
            with pool.Fori(0, B) as b:
                for stage, gq, g in staged(b):
                    u = gq % 2
                    if stage == 0:
                        r2.wait(pool, (g - GB) * 2 + 1)
                        n1.apply(pool, g, u, lambda t: x3[:, gq, t], lambda t: rr[:, u, t])
                    elif stage == 1:
                        edge.wait(pool, g)
                        for which, cnt, mixed in ((1, pk_, mk_), (0, pr_, mr_)):
                            for c in range(DC):
                                xt_sb.wait(pool, g * DC + c)
                                mixed.wait(pool, (g - 1) * DC + c)
                                cnt.done(pool.tensor_scalar(prev[:, which, c], xt[:, u, c, 0:TG], om[:, which, c:c + 1], 0.0, ALU.mult, ALU.add))
                    else:
                        for m in range(DC):
                            k_re.wait(pool, g * DC + m)
                            v_ps.wait(pool, (g - 2) * 2 + 1)
                            k_sq.done(pool.tensor_tensor(ka[:, u, m], kr[:, m], kr[:, m], ALU.mult))
                        out.wait(pool, u, b * (GB // 2) + gq // 2 - 1)
                        n2.apply(pool, g, u, lambda t: x4[:, u, t], lambda t: rr2[:, u, t])


def two_blocks(nc, a, out):
    with ExitStack() as ctx:
        def sb(name, shape, dt=F32):
            return ctx.enter_context(nc.sbuf_tensor(name, shape, dt))

        def dram(name, shape, dt=F32):
            return nc.dram_tensor(name, shape, dt, kind="Internal").ap()

        kn = {
            "ps": ctx.enter_context(nc.psum_tensor("ps", [P, 8, TG], F32)),
            "ident": sb("ident", [P, P]), "ones": sb("ones", [P, P]), "swap": sb("swap", [P, P]),
            "pick": sb("pick", [P, P]), "identb": sb("identb", [P, P], BF16), "headsum": sb("headsum", [P, P], BF16),
            "mask_kq": sb("mask_kq", [P, P], BF16), "mask_qk": sb("mask_qk", [P, P], BF16),
            "C": sb("C", [NF, H, NF]), "w4": sb("w4", [P, DC, D]),
            "alpha": sb("alpha", [P, 1]), "rbeta": sb("rbeta", [P, 1]), "wide": sb("wide", [P, 2]), "eps": sb("eps", [P, 1]),
            "q_d": dram("q_parts", [3, B * D, T], BF16), "k_d": dram("k_parts", [3, B * D, T], BF16),
            "f_d": dram("f_parts", [3, B * H * NF, T], BF16), "g_d": dram("g_parts", [3, B * NHQ * NF, T], BF16),
            "v_d": dram("v_ones", [B * NHQ, P, KB, HQ * VW]), "shift_d": dram("shift", [3, B * H, T], BF16),
            "o_d": dram("o_t", [B * D, T]), "x2_d": dram("x2", [B * T, D]),
        }
        const_in, made = ctx.enter_context(nc.semaphore("const_in")), ctx.enter_context(nc.semaphore("made"))

        def chunked(ap):
            return ap.rearrange("(c p) n -> p c n", p=P)

        with nc.Block() as block:
            @block.sync
            def _(sp):
                for i, name in enumerate(("ident", "ones", "swap", "pick")):
                    sp.dma_start(kn[name][:], a["consts"][i]).then_inc(const_in, 16)
                for i, name in enumerate(("identb", "headsum", "mask_kq", "mask_qk")):
                    sp.dma_start(kn[name][:], a["constsb"][i]).then_inc(const_in, 16)
                sp.wait_ge(const_in, 16 * 8)

            @block.vector
            def _(dve):
                dve.memset(kn["eps"][:], EPS).then_inc(made, 1)
                dve.memset(kn["wide"][:], 0.0).then_inc(made, 1)

        setup_phase(nc, kn, {"tw": a["tw"], "tr": a["L0_attn_transforms"], "kernel0": chunked(a["L0_ffn_kernel"]), "scalars": a["scalars"]})
        x0 = a["L0_attn_x"]
        project_phase(nc, kn, 0, {"wq": chunked(a["wq0"]), "wk": chunked(a["wk0"]), "wv": chunked(a["wv0"]), "w12": chunked(a["w12"])}, x0)
        row_max_phase(nc, kn, 0)
        attend_phase(nc, kn, 0)
        post0_phase(nc, kn, {"wo": chunked(a["wo0"]), "a": chunked(a["L0_ffn_a"]), "b": a["L0_ffn_b"], "bias": a["bias"]}, x0, kn["x2_d"])
        project_phase(nc, kn, 1, {"wq": chunked(a["wq1"]), "wk": chunked(a["wk1"]), "wv": chunked(a["wv1"]), "cos": a["cos"], "sin": a["sin"]}, kn["x2_d"])
        row_max_phase(nc, kn, 1)
        attend_phase(nc, kn, 1)
        post1_phase(nc, kn, {"wo": chunked(a["wo1"]), "wr": chunked(a["wr1"]), "wk": chunked(a["wkf1"]), "wv": chunked(a["wvf1"]),
                             "mu": a["mu"]}, kn["x2_d"], out)


def kernel(**inputs):
    import ml_dtypes as _md
    import numpy as _np
    import concourse.bacc as _bacc
    from concourse import mybir as _mybir
    from concourse.bass_utils import run_bass_kernel_spmd as _run

    x = {k: _np.asarray(v) for k, v in inputs.items()}

    eye = _np.eye(P, dtype=_np.float32)
    r = _np.arange(P)
    swap = (r[:, None] == (r[None, :] // HD) * HD + (r[None, :] % HD + HD // 2) % HD).astype(_np.float32)
    pick = (r[:, None] == (r[None, :] // VW) * VW + HD).astype(_np.float32)
    headsum = (r[:, None] // HD == r[None, :] // HD).astype(_np.float32)
    behind = _np.where(r[:, None] > r[None, :], MASKED, 0.0).astype(_np.float32)
    inv_freq = _np.float32(1.0) / _np.power(_np.float32(10000.0), _np.arange(0, HD, 2, dtype=_np.float32) / _np.float32(HD))
    freqs = _np.arange(T, dtype=_np.float32)[:, None] * inv_freq[None, :].astype(_np.float32)
    emb = _np.concatenate([freqs, freqs], axis=1)[:, r % HD].T
    sign = _np.where(r % HD < HD // 2, -1.0, 1.0).astype(_np.float32)[:, None]

    def t(a):
        return _np.ascontiguousarray(_np.asarray(a).T)

    def spread(a, n):
        return _np.ascontiguousarray(_np.broadcast_to(_np.asarray(a), (n,) + _np.asarray(a).shape))

    qkv = x["L0_attn_qkv_w"]
    arrays = {
        "consts": _np.stack([eye, _np.ones((P, P), _np.float32), swap, pick]),
        "constsb": _np.stack([eye, headsum, behind, behind.T]).astype(_md.bfloat16),
        "cos": _np.cos(emb).astype(_np.float32), "sin": (_np.sin(emb) * sign).astype(_np.float32),
        "L0_attn_x": _np.ascontiguousarray(x["L0_attn_x"].reshape(B * T, D)),
        "wq0": t(qkv[:D]), "wk0": t(qkv[D:2 * D]), "wv0": t(qkv[2 * D:]), "wo0": t(x["L0_attn_out_w"]),
        "w12": t(_np.concatenate([x["L0_attn_hex_w"], x["L0_attn_q6_w"]])),
        "L0_attn_transforms": x["L0_attn_transforms"],
        "tw": spread(x["L0_attn_transform_weights"], NF),
        "scalars": spread(_np.stack([x["L0_attn_hamming_lambda_logit"].reshape(()), x["L0_attn_scale_logit"].reshape(()),
                                     x["L0_attn_sips_alpha"].reshape(()), x["L0_attn_sips_beta"].reshape(())]), P),
        "L0_ffn_kernel": x["L0_ffn_kernel"], "L0_ffn_a": x["L0_ffn_a"], "L0_ffn_b": x["L0_ffn_b"],
        "bias": spread(x["L0_ffn_bias"], P),
        "wq1": t(x["L1_attn_Wq"]), "wk1": t(x["L1_attn_Wk"]), "wv1": t(x["L1_attn_Wv"]), "wo1": t(x["L1_attn_Wo"]),
        "wr1": t(x["L1_ffn_W_r"]), "wkf1": t(x["L1_ffn_W_k"]), "wvf1": t(x["L1_ffn_W_v"]),
        "mu": _np.ascontiguousarray(_np.stack([x["L1_ffn_mu_r"], x["L1_ffn_mu_k"]]).reshape(2, DC, P).transpose(2, 0, 1)),
    }
    nc = _bacc.Bacc("TRN2", target_bir_lowering=False, num_devices=1)
    aps = {n: nc.dram_tensor(f"in_{n}", v.shape, _mybir.dt.from_np(v.dtype), kind="ExternalInput").ap() for n, v in arrays.items()}
    out = nc.dram_tensor("out", (B * T, D), _mybir.dt.float32, kind="ExternalOutput").ap()
    two_blocks(nc, aps, out)
    res = _run(nc, [{f"in_{n}": _np.ascontiguousarray(v) for n, v in arrays.items()}], core_ids=[0])
    return res.results[0]["out"].reshape(B, T, D)
```

```python
from contextlib import ExitStack

import concourse.bass as bass
from concourse import mybir

F32 = mybir.dt.float32
BF16 = mybir.dt.bfloat16
I32 = mybir.dt.int32
ACT = mybir.ActivationFunctionType
ALU = mybir.AluOpType
AX = mybir.AxisListType

B, T, D = 4, 2048, 256
H, HD = 16, 16
P = 128
DC = D // P
TG = 512
GB = T // TG
TT = TG // P
KB = T // P
HQ = 4
NHQ = H // HQ
BU = 2
NF = 12
VW = 32
SLOTS_A = (0, 1, 2, 0, 1, 0)
SLOTS_B = (0, 0, 0, 1, 1, 2)
NS = len(SLOTS_A)
QROWS = NS * HD
FROWS = NS * NF
MASKED = -1.0e30
BOUND = 60.0
EPS = 1e-5


APART = (mybir.EngineType.Pool, mybir.EngineType.SP)


def wait(eng, sem, value, passed, apart=False):
    eng.wait_ge(sem, value)
    if apart or eng.engine in APART:
        eng.sem_inc(passed, 1)


class Count:

    CREDIT = 8

    def __init__(self, sem, passed, unit=1):
        self.sem, self.passed, self.unit = sem, passed, unit

    def start(self, eng):
        eng.sem_inc(self.sem, self.CREDIT * self.unit)

    def done(self, ins):
        ins.then_inc(self.sem, self.unit)

    def wait(self, eng, item, apart=False):
        wait(eng, self.sem, (item + (1 + self.CREDIT)) * self.unit, self.passed, apart)


class Stores:

    def __init__(self, sems, passed, n=1):
        self.sems, self.passed, self.unit = sems, passed, 16 * n

    def start(self, eng):
        for sem in self.sems:
            eng.sem_inc(sem, self.unit)

    def done(self, ins, slot):
        ins.then_inc(self.sems[slot], 16)

    def wait(self, eng, slot, use):
        wait(eng, self.sems[slot], (use + 2) * self.unit, self.passed)


class Chain:

    def __init__(self, sem, per_turn=0, turn=0):
        self.sem, self.per_turn, self.turn, self.n = sem, per_turn, turn, 0

    def link(self, eng, ins):
        ins.then_inc(self.sem, 1)
        self.n += 1
        eng.wait_ge(self.sem, self.turn * self.per_turn + self.n)

    def close(self):
        assert not self.per_turn or self.n == self.per_turn, (self.n, self.per_turn)


class Phase:

    def __init__(self, nc, ctx, name):
        self.nc, self.ctx, self.name, self.sems = nc, ctx, name, []
        ctx.callback(self.clear)
        self.passed = self.sem("passed")

    def sb(self, name, shape, dt=F32):
        return self.ctx.enter_context(self.nc.sbuf_tensor(f"{self.name}_{name}", shape, dt))

    def sem(self, name):
        self.sems.append(self.nc.alloc_semaphore(f"{self.name}_{name}"))
        return self.sems[-1]

    def clear(self):
        self.nc.clear_and_free_semaphores(self.sems)
        self.nc.all_engine_barrier()

    def count(self, name, unit=1):
        return Count(self.sem(name), self.passed, unit)

    def stores(self, name, slots, n=1):
        return Stores([self.sem(f"{name}{i}") for i in range(slots)], self.passed, n)


def setup_phase(nc, kn, ins):
    with ExitStack() as ctx:
        ph = Phase(nc, ctx, "setup")
        loaded, done, exps, pe_done, pool_done = (ph.sem(n) for n in ("loaded", "done", "exps", "pe_done", "pool_done"))
        tw = ph.sb("tw", [NF, H, 7])
        tr = ph.sb("tr", [NF, 6, 7])
        mx = ph.sb("mx", [NF, H])
        sm = ph.sb("sm", [NF, H])
        prod = ph.sb("prod", [NF, H, 6, 7])
        mh = ph.sb("mh", [NF, H, 6])
        mag = ph.sb("mag", [NF, H, NF])
        rowabs = ph.sb("rowabs", [NF, H])
        w = ph.sb("w", [P, DC, D])
        sc = ph.sb("sc", [P, 8])
        wmax = ph.sb("wmax", [P, 4])
        scale = ph.sb("scale", [P, 2])
        rows = ph.sb("rows", [P, 2])
        bnd = ph.sb("bnd", [P, 4])
        zero = ph.sb("zero", [P, T], BF16)
        zeroed = ph.sem("zeroed")
        block = ctx.enter_context(nc.Block())

        @block.sync
        def _(sp):
            sp.wait_ge(done, 1)
            with nc.allow_non_contiguous_dma(reason="small table"):
                for d in range(6):
                    sp.dma_start(tr[6 + d:7 + d, :, :], ins["tr"][:, d, :].rearrange("t (o e) -> o e t", o=1)).then_inc(loaded, 16)
            sp.dma_start(tw[:], ins["tw"]).then_inc(loaded, 16)
            sp.dma_start(w[:], ins["kernel0"]).then_inc(loaded, 16)
            sp.dma_start(sc[:, 0:4], ins["scalars"]).then_inc(loaded, 16)
            sp.wait_ge(zeroed, 1)
            n = 0
            for part in range(3):
                for half in range(B * H // 32):
                    sp.dma_start(kn["shift_d"][part, half * 32:half * 32 + 32, :], zero[0:32, :]).then_inc(zeroed, 16)
                    n += 16
            sp.wait_ge(zeroed, 1 + n)

        @block.gpsimd
        def _(pool):
            pool.memset(zero[:], 0.0).then_inc(zeroed, 1)
            pool.wait_ge(pool_done, 1)
            pool.partition_all_reduce(wmax[:, 1:2], wmax[:, 0:1], P, bass.bass_isa.ReduceOp.max).then_inc(pool_done, 1)

        @block.scalar
        def _(act):
            act.wait_ge(loaded, 16 * 9)
            act.activation(sc[:, 4:6], sc[:, 0:2], ACT.Exp, scale=-1.0).then_inc(exps, 1)
            act.wait_ge(exps, 2)
            act.activation(tw[:], tw[:], ACT.Exp, scale=2.0).then_inc(exps, 1)

        @block.tensor
        def _(pe):
            pe.wait_ge(exps, 4)
            pe.matmul(kn["ps"][:, 0, 0:H], kn["ones"][0:NF, :], rowabs[:], start=True, stop=True).then_inc(pe_done, 1)

        @block.vector
        def _(dve):
            ch = Chain(done)
            ch.link(dve, dve.memset(tr[:], 0.0))
            dve.wait_ge(loaded, 16 * 9)
            ch.link(dve, dve.tensor_reduce(mx[:], tw[:], AX.X, ALU.max))
            dve.tensor_tensor(tw[:], tw[:], mx[:].unsqueeze(2).to_broadcast([NF, H, 7]), ALU.subtract).then_inc(exps, 1)
            ch.link(dve, dve.tensor_reduce(wmax[:, 0:1], w[:], AX.XY, ALU.max))
            ch.link(dve, dve.tensor_reduce(wmax[:, 2:3], w[:], AX.XY, ALU.min))
            ch.link(dve, dve.tensor_scalar(wmax[:, 2:3], wmax[:, 2:3], -1.0, None, ALU.mult))
            dve.tensor_tensor(wmax[:, 0:1], wmax[:, 0:1], wmax[:, 2:3], ALU.max).then_inc(pool_done, 1)
            dve.wait_ge(exps, 3)
            ch.link(dve, dve.tensor_scalar(sc[:, 4:6], sc[:, 4:6], 1.0, None, ALU.add))
            ch.link(dve, dve.reciprocal(sc[:, 6:8], sc[:, 4:6]))
            ch.link(dve, dve.tensor_scalar(sc[:, 6:7], sc[:, 6:7], 0.5, None, ALU.mult))
            ch.link(dve, dve.tensor_scalar(sc[:, 7:8], sc[:, 7:8], 1.0 / 3.0, None, ALU.mult))
            ch.link(dve, dve.tensor_copy(kn["alpha"][:], sc[:, 2:3]))
            ch.link(dve, dve.reciprocal(kn["rbeta"][:], sc[:, 3:4]))
            ch.link(dve, dve.tensor_reduce(sm[:], tw[:], AX.X, ALU.add))
            ch.link(dve, dve.reciprocal(sm[:], sm[:]))
            ch.link(dve, dve.tensor_tensor(tw[:], tw[:], sm[:].unsqueeze(2).to_broadcast([NF, H, 7]), ALU.mult))
            for h in range(H):
                ch.link(dve, dve.tensor_tensor(prod[:, h], tr[:], tw[:, h:h + 1, :].to_broadcast([NF, 6, 7]), ALU.mult))
            ch.link(dve, dve.tensor_reduce(mh[:], prod[:], AX.X, ALU.add))
            for h in range(H):
                ch.link(dve, dve.tensor_scalar(kn["C"][:, h, 0:6], kn["ident"][0:NF, 0:6], sc[0:NF, 6:7], None, ALU.mult))
            ch.link(dve, dve.tensor_scalar(kn["C"][:, :, 6:12], mh[:], sc[0:NF, 7:8], None, ALU.mult))
            ch.link(dve, dve.tensor_scalar(mag[:], kn["C"][:], -1.0, None, ALU.mult))
            ch.link(dve, dve.tensor_tensor(mag[:], mag[:], kn["C"][:], ALU.max))
            dve.tensor_reduce(rowabs[:], mag[:], AX.X, ALU.add).then_inc(exps, 1)
            dve.wait_ge(pe_done, 1)
            ch.link(dve, dve.tensor_reduce(bnd[:, 0:1], kn["ps"][:, 0, 0:H], AX.X, ALU.max))
            ch.link(dve, dve.tensor_scalar(bnd[:, 1:2], kn["alpha"][:], -1.0, None, ALU.mult))
            ch.link(dve, dve.tensor_tensor(bnd[:, 1:2], bnd[:, 1:2], kn["alpha"][:], ALU.max))
            ch.link(dve, dve.tensor_tensor(bnd[:, 0:1], bnd[:, 1:2], bnd[:, 0:1], ALU.add))
            ch.link(dve, dve.tensor_scalar(bnd[:, 2:3], bnd[:, 0:1], BOUND, None, ALU.is_le))
            ch.link(dve, dve.tensor_scalar(kn["wide"][:, 0:1], bnd[:, 2:3], -1.0, 1.0, ALU.mult, ALU.add))
            dve.wait_ge(pool_done, 2)
            m, s0, rest = wmax[:, 1:2], scale[:, 0:1], scale[:, 1:2]
            ch.link(dve, dve.tensor_scalar(s0, m, 1.0 / 7.0, None, ALU.mult))
            ch.link(dve, dve.scalar_tensor_tensor(rest, s0, -8.0, m, ALU.mult, ALU.add))
            ch.link(dve, dve.tensor_tensor(rest, rest, s0, ALU.add))
            ch.link(dve, dve.scalar_tensor_tensor(s0, rest, 1.0 / 7.0, s0, ALU.mult, ALU.add))
            ch.link(dve, dve.reciprocal(rest, s0))
            wf = w[:].rearrange("p c n -> p (c n)")
            ch.link(dve, dve.tensor_scalar(wf, wf, rest, None, ALU.mult))
            magic = 12582912.0
            ch.link(dve, dve.tensor_scalar(wf, wf, magic, None, ALU.add))
            ch.link(dve, dve.tensor_scalar(wf, wf, -magic, -8.0, ALU.add, ALU.max))
            ch.link(dve, dve.tensor_scalar(kn["w4"][:].rearrange("p c n -> p (c n)"), wf, 7.0, scale[:, 0:1], ALU.min, ALU.mult))


def project_phase(nc, kn, layer, w, x_d):
    rope = layer == 1
    tiles = ([] if rope else [("g", 0)]) + [("q", 0), ("q", 1), ("k", 0), ("k", 1)] + ([] if rope else [("f", 0), ("f", 1)])
    NTL = len(tiles)
    NTB = GB * NTL
    R = 4
    assert NTB % R == 0
    rows_of = {"q": P, "k": P, "f": 96, "g": NF}
    V_AT = (NTL // 2 - 1, NTL - 1)
    XT0, PRJ0, NORM, VB = 0, 2, 6, 7
    L_HI, L_REST = (2, 2) if rope else (0, 0)
    L_MID, L_LOW, L_NORM = L_REST + 1, L_REST + 1, 5 if rope else 0
    with ExitStack() as ctx:
        ph = Phase(nc, ctx, f"proj{layer}")
        w_in, x_in = ph.sem("w_in"), [ph.sem(f"x_in{i}") for i in range(GB)]
        ones_set = ph.sem("ones_set")
        xt_ps, xt_sb = ph.count("xt_ps"), ph.count("xt_sb")
        prj = ph.count("prj")
        hi, rest, mid, low = (ph.count(n) for n in ("hi", "rest", "mid", "low"))
        parts_out = [ph.sem(f"parts_out{i}") for i in range(R)]
        v_ps, v_sb = ph.count("v_ps"), ph.count("v_sb")
        v_out = ph.stores("v_out", 2, NHQ)
        feat = ph.count("feat")
        mul, rot = ph.count("mul"), ph.count("rot")
        sq, norm, nmax = (ph.count(n) for n in ("sq", "norm", "nmax"))
        fold, flag = ph.sem("fold"), ph.sem("flag")
        wq_s, wk_s, wv_s = (ph.sb(n, [P, DC, D]) for n in ("wq", "wk", "wv"))
        xs = ph.sb("xs", [P, GB, TT, D])
        xt = ph.sb("xt", [P, 2, DC, TG])
        parts = ph.sb("parts", [P, R, 3, TG], BF16)
        rem = ph.sb("rem", [P, R, TG])
        vs = ph.sb("vs", [P, 2, TT, H, VW])
        if rope:
            qcos, qsin = (ph.sb(n, [P, R, TG]) for n in ("qcos", "qsin"))
            cos_s, sin_s = ph.sb("cos", [P, T]), ph.sb("sin", [P, T])
            sqr = ph.sb("sqr", [P, R, TG], BF16)
            nrm = ph.sb("nrm", [P, 2, GB])
            top = ph.sb("top", [P, 8])
        else:
            w12_s, f12 = ph.sb("w12", [P, DC, NF]), ph.sb("f12", [NF, 2, TG])
        n_w = 16 * (5 if rope else 4)
        ps = kn["ps"]
        block = ctx.enter_context(nc.Block())

        def tile_of(jb):
            gq, j = divmod(jb, NTL)
            kind, m = tiles[j]
            return gq, j, kind, m, rows_of[kind], jb % R

        n_stores = [NHQ if tiles[jb % NTL][0] == "g" else 1 for jb in range(NTB)]
        per_batch = [sum(n_stores[r::R]) for r in range(R)]

        def stored(eng, b, jb):
            before, jb = (0, jb) if jb >= 0 else (1, jb + NTB)
            upto = sum(n_stores[jb % R:jb + 1:R])
            wait(eng, parts_out[jb % R], (b * per_batch[jb % R] + (per_batch[jb % R] * (1 - before) + upto)) * 16, ph.passed)

        def x_rows(b, gq):
            return x_d[bass.ds(b * T + gq * TG, TG), :].rearrange("(t p) d -> p t d", p=P)

        @block.sync
        def _(sp):
            for gq in range(GB):
                sp.dma_start(xs[:, gq], x_rows(0, gq)).then_inc(x_in[gq], 16)
                if gq == 0:
                    for name, t in [("wq", wq_s), ("wk", wk_s), ("wv", wv_s)]:
                        sp.dma_start(t[:], w[name]).then_inc(w_in, 16)
                    if rope:
                        sp.dma_start(cos_s[:], w["cos"]).then_inc(w_in, 16)
                        sp.dma_start(sin_s[:], w["sin"]).then_inc(w_in, 16)
                    else:
                        sp.dma_start(w12_s[:], w["w12"]).then_inc(w_in, 16)
            for r in range(R):
                sp.sem_inc(parts_out[r], per_batch[r] * 16)
            v_out.start(sp)
            with sp.Fori(0, B) as b:
                for jb in range(NTB):
                    gq, j, kind, m, n, r = tile_of(jb)
                    low.wait(sp, b * NTB + jb)
                    cols = slice(gq * TG, (gq + 1) * TG)
                    if kind == "g":
                        for q in range(NHQ):
                            sp.dma_start(kn["g_d"][:, bass.ds((b * NHQ + q) * NF, NF), cols].rearrange("k r t -> r k t"),
                                         parts[0:n, r]).then_inc(parts_out[r], 16)
                    else:
                        row = b * P + m * (B * P) if rope else b * (H * NF if kind == "f" else D) + m * n
                        sp.dma_start(kn[f"{kind}_d"][:, bass.ds(row, n), cols].rearrange("k r t -> r k t"),
                                     parts[0:n, r]).then_inc(parts_out[r], 16)
                    if j == NTL - 1:
                        g = b * GB + gq
                        v_sb.wait(sp, g * 2 + 1)
                        for q in range(NHQ):
                            v_out.done(sp.dma_start(
                                kn["v_d"][bass.ds(b * NHQ + q, 1), :, gq * TT:(gq + 1) * TT, :].rearrange("o p k n -> (o p) k n"),
                                vs[:, gq % 2, :, q * HQ:(q + 1) * HQ, :].rearrange("p t h n -> p t (h n)")), gq % 2)
                        xt_ps.wait(sp, g * DC + DC - 1)
                        sp.dma_start(xs[:, gq], x_rows((b + 1) % B, gq)).then_inc(x_in[gq], 16)
            for jb in range(NTB - R, NTB):
                stored(sp, B - 1, jb)
            for u in range(2):
                v_out.wait(sp, u, B * GB // 2 - 1)
            for gq in range(GB):
                sp.wait_ge(x_in[gq], 16 * (B + 1))

        @block.gpsimd
        def _(pool):
            for c in (low, rot):
                c.start(pool)
            with pool.Fori(0, B) as b:
                for s in range(NTB + L_LOW):
                    if rope and s < NTB:
                        gq, j, kind, m, n, r = tile_of(s)
                        J = b * NTB + s
                        mul.wait(pool, J)
                        rot.done(pool.tensor_tensor(qcos[:, r], qcos[:, r], qsin[:, r], ALU.subtract if m == 0 else ALU.add))
                    if s >= L_LOW:
                        gq, j, kind, m, n, r = tile_of(s - L_LOW)
                        mid.wait(pool, b * NTB + s - L_LOW)
                        low.done(pool.tensor_tensor(parts[0:n, r, 2], rem[0:n, r], parts[0:n, r, 1], ALU.subtract))
            if rope:
                pool.wait_ge(fold, B + 1)
                pool.partition_all_reduce(top[:, 2:4], top[:, 0:2], P, bass.bass_isa.ReduceOp.max).then_inc(flag, 1)

        @block.scalar
        def _(act):
            for c in (xt_sb, hi, v_sb, feat, sq):
                c.start(act)

            def v_half(b, gq, half):
                g = b * GB + gq
                v_ps.wait(act, g * 2 + half)
                if half == 0:
                    v_out.wait(act, gq % 2, b * (GB // 2) + gq // 2 - 1)
                v_sb.done(act.activation(vs[:, gq % 2, 2 * half:2 * half + 2, :, 0:HD],
                                         ps[:, VB].rearrange("p (t h d) -> p t h d", t=2, h=H), ACT.Copy))

            act.wait_ge(ones_set, 1)
            with act.Fori(0, B) as b:
                for s in range(NTB + L_HI):
                    if s < NTB:
                        gq, j, *_ = tile_of(s)
                        g = b * GB + gq
                        if j == 0:
                            v_ps.wait(act, (g - 2) * 2 + 1)
                            for c in range(DC):
                                xt_ps.wait(act, g * DC + c)
                                xt_sb.done(act.activation(xt[:, gq % 2, c], ps[:, XT0 + c], ACT.Copy))
                    if s >= L_HI:
                        gq, j, kind, m, n, r = tile_of(s - L_HI)
                        J, g = b * NTB + s - L_HI, b * GB + gq
                        stored(act, b, s - L_HI - R)
                        if rope:
                            rot.wait(act, J)
                            hi.done(act.activation(parts[0:n, r, 0], qcos[0:n, r], ACT.Copy))
                            norm.wait(act, b * (NTB // 2) + (s - L_HI - R) // 2)
                            sq.done(act.activation(sqr[:, r], qcos[:, r], ACT.Square))
                        elif kind == "g":
                            prj.wait(act, J)
                            feat.done(act.activation(f12[:, gq % 2], ps[0:NF, PRJ0 + r], ACT.Tanh))
                            feat.wait(act, g)
                            hi.done(act.activation(parts[0:n, r, 0], f12[:, gq % 2], ACT.Copy))
                        else:
                            prj.wait(act, J)
                            hi.done(act.activation(parts[0:n, r, 0], ps[0:n, PRJ0 + r], ACT.Copy))
                        if j in V_AT:
                            v_half(b, gq, V_AT.index(j))

        @block.tensor
        def _(pe):
            for c in (xt_ps, prj, v_ps, norm):
                c.start(pe)
            pe.wait_ge(w_in, n_w)
            with pe.Fori(0, B) as b:

                def transposes(gq):
                    g = b * GB + gq
                    pe.wait_ge(x_in[gq], 16 * (b + 1))
                    for c in range(DC):
                        xt_sb.wait(pe, (g - 1) * DC + c)
                        for t in range(TT):
                            mm = pe.transpose(ps[:, XT0 + c, t * P:(t + 1) * P], xs[:, gq, t, c * P:(c + 1) * P], kn["ident"][:])
                        xt_ps.done(mm)

                transposes(0)
                for s in range(NTB + L_NORM):
                    if s < NTB:
                        gq, j, kind, m, n, r = tile_of(s)
                        J, g, u = b * NTB + s, b * GB + gq, gq % 2
                        if j == 0:
                            xt_sb.wait(pe, g * DC + DC - 1)
                        if rope:
                            mul.wait(pe, J - R + 1 - m)
                        else:
                            rest.wait(pe, J - R)
                        if kind == "f":
                            feat.wait(pe, g)
                            mm = pe.matmul(ps[0:n, PRJ0 + r], kn["C"][:].rearrange("p h e -> p (h e)")[:, m * n:(m + 1) * n], f12[:, u], start=True, stop=True)
                        else:
                            for c in range(DC):
                                lhs = w12_s[:, c, :] if kind == "g" else (wq_s if kind == "q" else wk_s)[:, c, m * P:(m + 1) * P]
                                mm = pe.matmul(ps[0:n, PRJ0 + r], lhs, xt[:, u, c], start=c == 0, stop=c == DC - 1)
                        prj.done(mm)
                        if j in V_AT:
                            half = V_AT.index(j)
                            if half == 1 and gq + 1 < GB:
                                transposes(gq + 1)
                            v_sb.wait(pe, g * 2 + half - 1)
                            for t in range(2 * half, 2 * half + 2):
                                for c in range(DC):
                                    mm = pe.matmul(ps[:, VB, (t % 2) * D:(t % 2 + 1) * D], xt[:, u, c, t * P:(t + 1) * P], wv_s[:, c, :], start=c == 0, stop=c == DC - 1)
                            v_ps.done(mm)
                    if rope and s >= L_NORM and s % 2 == 1:
                        pair = b * (NTB // 2) + (s - L_NORM) // 2
                        nmax.wait(pe, pair - 1)
                        sq.wait(pe, b * NTB + s - L_NORM + 1)
                        for m in range(2):
                            mm = pe.matmul(ps[:, NORM], kn["headsum"][:], sqr[:, (s - L_NORM + m) % R], start=m == 0, stop=m == 1)
                        norm.done(mm)

        @block.vector
        def _(dve):
            for c in (rest, mid, mul, nmax):
                c.start(dve)
            dve.memset(vs[:], 1.0).then_inc(ones_set, 1)
            if rope:
                dve.memset(top[:], 0.0).then_inc(fold, 1)
                dve.wait_ge(w_in, n_w)
            with dve.Fori(0, B) as b:
                for s in range(NTB + max(L_MID, L_NORM + 1)):
                    if rope and s < NTB and s % 2 == 1:
                        gq = s // NTL
                        cols = slice(gq * TG, (gq + 1) * TG)
                        prj.wait(dve, b * NTB + s)
                        for jb in (s - 1, s):
                            J, r, other = b * NTB + jb, jb % R, (jb ^ 1) % R
                            hi.wait(dve, J - R)
                            rest.wait(dve, J - R)
                            sq.wait(dve, J - R)
                            dve.tensor_tensor(qcos[:, r], ps[:, PRJ0 + r], cos_s[:, cols], ALU.mult)
                            mul.done(dve.tensor_tensor(qsin[:, r], ps[:, PRJ0 + other], sin_s[:, cols], ALU.mult))
                    if L_REST <= s < NTB + L_REST:
                        gq, j, kind, m, n, r = tile_of(s - L_REST)
                        J = b * NTB + s - L_REST
                        hi.wait(dve, J)
                        low.wait(dve, J - R)
                        src = qcos[:, r] if rope else f12[:, gq % 2] if kind == "g" else ps[0:n, PRJ0 + r]
                        rest.done(dve.tensor_tensor(rem[0:n, r], src, parts[0:n, r, 0], ALU.subtract))
                    if L_MID <= s < NTB + L_MID:
                        gq, j, kind, m, n, r = tile_of(s - L_MID)
                        rest.wait(dve, b * NTB + s - L_MID)
                        mid.done(dve.tensor_copy(parts[0:n, r, 1], rem[0:n, r]))
                    if rope and s > L_NORM and s % 2 == 0:
                        jb = s - 1 - L_NORM
                        gq, j, kind, *_ = tile_of(jb)
                        norm.wait(dve, b * (NTB // 2) + jb // 2)
                        nmax.done(dve.tensor_reduce(nrm[:, 0 if kind == "q" else 1, gq:gq + 1], ps[:, NORM], AX.X, ALU.max))
                if rope:
                    nmax.wait(dve, b * (NTB // 2) + NTB // 2 - 1)
                    dve.tensor_reduce(top[:, 4:6], nrm[:], AX.X, ALU.max).then_inc(ones_set, 1)
                    dve.wait_ge(ones_set, b + 2)
                    dve.wait_ge(fold, b + 1)
                    dve.tensor_tensor(top[:, 0:2], top[:, 0:2], top[:, 4:6], ALU.max).then_inc(fold, 1)
            if rope:
                dve.wait_ge(flag, 1)
                dve.tensor_tensor(top[:, 6:7], top[:, 2:3], top[:, 3:4], ALU.mult).then_inc(flag, 1)
                dve.wait_ge(flag, 2)
                dve.tensor_scalar(top[:, 7:8], top[:, 6:7], (BOUND * 4 / 1.05) ** 2, None, ALU.is_le).then_inc(flag, 1)
                dve.wait_ge(flag, 3)
                dve.tensor_scalar(kn["wide"][:, 1:2], top[:, 7:8], -1.0, 1.0, ALU.mult, ALU.add)


def load_stacks(eng, kn, layer, it, st, sem):
    n = 0

    def load(dst, src):
        nonlocal n
        eng.dma_start(dst, src).then_inc(sem, 16)
        n += 1

    nh = 1 if layer == 0 else 2
    hd = HD // nh
    for s in range(NS):
        for m in range(nh):
            r0 = s * HD + m * hd
            rows = bass.ds(it * HQ * hd + m * (B * H * hd), HQ * hd)
            load(st["q"][r0:r0 + hd], kn["q_d"][SLOTS_A[s], rows, :].rearrange("(h r) t -> r h t", r=hd))
            load(st["k"][r0:r0 + hd], kn["k_d"][SLOTS_B[s], rows, :].rearrange("(h r) t -> r h t", r=hd))
        if layer == 0:
            load(st["f"][s * NF:(s + 1) * NF], kn["f_d"][SLOTS_A[s], bass.ds(it * HQ * NF, HQ * NF), :].rearrange("(h r) t -> r h t", r=NF))
            load(st["g"][s * NF:(s + 1) * NF], kn["g_d"][SLOTS_B[s], bass.ds(it * NF, NF), :])
    return n


def attend_phase(nc, kn, layer):
    U = 2
    steps = [(g, kb) for g in range(GB) for kb in range((g + 1) * (TG // P))]
    NST = len(steps)
    body = [(u, s) for u in range(U) for s in range(NST)]
    NB = len(body)
    R = 4
    assert NB % R == 0
    QK0, E0, O0 = 0, 4, 6
    RQ = 2 if layer == 0 else 3
    SR, FR = (QROWS, FROWS + 3) if layer == 0 else (QROWS + 3, 0)
    with ExitStack() as ctx:
        ph = Phase(nc, ctx, f"att{layer}")
        ones_set = ph.sem("ones_set")
        stacks_in = [ph.sem(f"stacks_in{u}") for u in range(U)]
        stacks_free = [ph.sem(f"stacks_free{u}") for u in range(U)]
        qk = ph.count("qk")
        th = ph.count("th")
        ex = ph.count("ex")
        sc = ph.count("sc")
        pr = ph.count("pr")
        pv = ph.count("pv")
        o_sb, l_ps, l_sb, o_n = (ph.count(n) for n in ("o_sb", "l_ps", "l_sb", "o_n"))
        o_out = ph.stores("o_out", 2, HQ)
        st = []
        for u in range(U):
            s = {"q": ph.sb(f"q{u}", [SR, HQ, T], BF16), "k": ph.sb(f"k{u}", [SR, HQ, T], BF16),
                 "v": ph.sb(f"v{u}", [P, KB, HQ * VW])}
            if layer == 0:
                s["f"], s["g"] = ph.sb(f"f{u}", [FR, HQ, T], BF16), ph.sb(f"g{u}", [FR, T], BF16)
            st.append(s)
        tanh_s = ph.sb("tanh", [P, 2, 2, TG]) if layer == 0 else None
        prob = ph.sb("prob", [P, R, HQ, TG])
        o_s, l_s, on_s = (ph.sb(n, [P, 2, TG]) for n in ("o", "l", "on"))
        ones_row = ph.sb("ones_row", [3, HQ * T if layer else T], BF16)
        ps = kn["ps"]
        N_LOAD = NS * 4 + 2
        block = ctx.enter_context(nc.Block())

        def banks(q):
            return QK0 + 2 * (q % RQ)

        def had_banks(q):
            if q >= RQ:
                return q - RQ
            return max(x for x in range(2 * NB) if x % RQ == q) - 2 * NB

        def at(i):
            u, s = body[i]
            g, kb = steps[s]
            r = kb - g * (TG // P)
            off = r * P if r > 0 else 0
            return u, s, g, kb, off, r >= 0, kb == (g + 1) * (TG // P) - 1

        @block.sync
        def _(sp):
            sp.wait_ge(ones_set, 1)
            for u in range(U):
                if layer == 0:
                    sp.dma_start(st[u]["g"][FROWS:FROWS + 3], ones_row[:]).then_inc(ones_set, 16)
                else:
                    sp.dma_start(st[u]["k"][QROWS:QROWS + 3], ones_row[:].rearrange("p (h t) -> p h t", h=HQ)).then_inc(ones_set, 16)
            N_IT = B * NHQ

            def load(it, u):
                n = load_stacks(sp, kn, layer, it, st[u], stacks_in[u])
                shift = st[u]["f"][FROWS:FROWS + 3] if layer == 0 else st[u]["q"][QROWS:QROWS + 3]
                sp.dma_start(shift, kn["shift_d"][:, bass.ds(it * HQ, HQ), :]).then_inc(stacks_in[u], 16)
                sp.dma_start(st[u]["v"][:], kn["v_d"][bass.ds(it, 1)].rearrange("o p k n -> (o p) k n")).then_inc(stacks_in[u], 16)
                assert n + 2 == N_LOAD

            o_out.start(sp)
            load(0, 0)
            with sp.Fori(0, N_IT // U) as i:
                for u in range(U):
                    it = i * U + u
                    wait(sp, stacks_free[1 - u], i + 1 + u, ph.passed)
                    load((it + 1) % N_IT, 1 - u)
                    for g in range(GB):
                        o_n.wait(sp, it * GB + g)
                        for h in range(HQ):
                            o_out.done(sp.dma_start(kn["o_d"][bass.ds(it * HQ * HD + h * HD, HD), g * TG:(g + 1) * TG], on_s[VW * h:VW * h + HD, g % 2]), g % 2)
            for u in range(2):
                o_out.wait(sp, u, B * NHQ * GB // 2 - 1)
            sp.wait_ge(stacks_in[0], 16 * N_LOAD * (N_IT // U + 1))

        @block.tensor
        def _(pe):
            for c in (qk, ex, pv, l_ps):
                c.start(pe)
            for u in range(U):
                pe.sem_inc(stacks_free[u], 1)
            pe.wait_ge(ones_set, 1 + 16 * U)
            LAG = 2 if layer == 0 else 1
            with pe.Fori(0, B * NHQ // U) as i:

                def scores(k, pair):
                    u, s, g, kb, off, diag, _ = at(k)
                    S = i * NB + k
                    (th if layer == 0 else pr).wait(pe, i * (2 * NB) + had_banks(2 * k + pair))
                    for h in (2 * pair, 2 * pair + 1):
                        bank = banks(2 * k + pair) + h % 2
                        out = ps[:, bank, off:TG]
                        mask = layer == 1 and diag
                        mm = pe.matmul(out, st[u]["k"][:, h, kb * P:(kb + 1) * P], st[u]["q"][:, h, g * TG + off:(g + 1) * TG], start=True, stop=not mask)
                        if mask:
                            mm = pe.matmul(ps[:, bank, off:off + P], kn["identb"][:], kn["mask_kq"][:], start=False, stop=True)
                    qk.done(mm)

                def extra(k, h):
                    u, s, g, kb, off, diag, _ = at(k)
                    S = i * NB + k
                    sc.wait(pe, S * HQ + h - 2)
                    mm = pe.matmul(ps[:, E0 + h % 2, off:TG], st[u]["g"][:, kb * P:(kb + 1) * P], st[u]["f"][:, h, g * TG + off:(g + 1) * TG], start=True, stop=not diag)
                    if diag:
                        mm = pe.matmul(ps[:, E0 + h % 2, off:off + P], kn["identb"][:], kn["mask_kq"][:], start=False, stop=True)
                    ex.done(mm)

                def weigh(k):
                    u, s, g, kb, off, diag, last = at(k)
                    S = i * NB + k
                    if layer == 0:
                        pr.wait(pe, S)
                    else:
                        pr.wait(pe, S * 2 + 1)
                    if kb == 0:
                        l_sb.wait(pe, (i * U + u) * GB + g - 2)
                    for h in range(HQ):
                        mm = pe.matmul(ps[VW * h:VW * (h + 1), O0 + g % 2, off:TG], st[u]["v"][:, kb, h * VW:(h + 1) * VW], prob[:, k % R, h, off:TG], start=kb == 0, stop=last)
                    pv.done(mm)

                def row_sums(k):
                    u, s, g, *_ = at(k)
                    G = (i * U + u) * GB + g
                    o_sb.wait(pe, G)
                    l_ps.done(pe.matmul(ps[:, O0 + g % 2], kn["pick"][:], o_s[:, g % 2], start=True, stop=True))

                def first_pair(k):
                    u, s, *_ = at(k)
                    if s == 0:
                        pe.wait_ge(stacks_in[u], (i + 1) * (16 * N_LOAD))
                    scores(k, 0)

                first_pair(0)
                if layer == 1:
                    scores(0, 1)
                for k in range(NB + LAG + 1):
                    if layer == 0:
                        if k < NB:
                            scores(k, 1)
                            extra(k, 0)
                            extra(k, 1)
                    elif k + 1 < NB:
                        first_pair(k + 1)
                    if LAG <= k < NB + LAG:
                        weigh(k - LAG)
                    if k > LAG and at(k - LAG - 1)[-1]:
                        row_sums(k - LAG - 1)
                    if layer == 0:
                        if k + 1 < NB:
                            first_pair(k + 1)
                        if k < NB:
                            extra(k, 2)
                            extra(k, 3)
                    elif k + 1 < NB:
                        scores(k + 1, 1)

        @block.scalar
        def _(act):
            for c in (th, pr):
                c.start(act)
            with act.Fori(0, B * NHQ // U) as i:
                for k in range(NB + 1):
                    if k < NB:
                        u, s, g, kb, off, *_ = at(k)
                        S = i * NB + k
                        for pair in range(2):
                            qk.wait(act, S * 2 + pair)
                            bank = banks(2 * k + pair)
                            src = ps[:, bank:bank + 2, off:TG]
                            if layer == 0:
                                sc.wait(act, (S - 1) * HQ + 2 * pair + 1)
                                th.done(act.activation(tanh_s[:, pair, :, off:TG], src, ACT.Tanh, scale=kn["rbeta"][:, 0:1]))
                            else:
                                pv.wait(act, S - R)
                                pr.done(act.activation(prob[:, k % R, 2 * pair:2 * pair + 2, off:TG], src, ACT.Exp, scale=float(HD) ** -0.5))
                    if k > 0 and layer == 0:
                        u, s, g, kb, off, *_ = at(k - 1)
                        S = i * NB + k - 1
                        sc.wait(act, S * HQ + HQ - 1)
                        pr.done(act.activation(prob[:, (k - 1) % R, :, off:TG], prob[:, (k - 1) % R, :, off:TG], ACT.Exp))

        @block.vector
        def _(dve):
            dve.memset(ones_row[:], 1.0).then_inc(ones_set, 1)
            for c in (sc, o_sb, l_sb):
                c.start(dve)
            LAG = 2 if layer == 0 else 1
            with dve.Fori(0, B * NHQ // U) as i:
                for k in range(NB + LAG + 2):
                    if LAG < k <= NB + LAG and at(k - LAG - 1)[-1]:
                        u, s, g, *_ = at(k - LAG - 1)
                        G = (i * U + u) * GB + g
                        pv.wait(dve, i * NB + k - LAG - 1)
                        o_n.wait(dve, G - 2)
                        o_sb.done(dve.tensor_copy(o_s[:, g % 2], ps[:, O0 + g % 2]))
                    if k > LAG + 1 and at(k - LAG - 2)[-1]:
                        u, s, g, *_ = at(k - LAG - 2)
                        G = (i * U + u) * GB + g
                        l_ps.wait(dve, G)
                        o_n.wait(dve, G - 2)
                        l_sb.done(dve.reciprocal(l_s[:, g % 2], ps[:, O0 + g % 2]))
                    if k < NB and layer == 0:
                        u, s, g, kb, off, *_ = at(k)
                        S = i * NB + k
                        pv.wait(dve, S - R)
                        for h in range(HQ):
                            th.wait(dve, S * 2 + h // 2)
                            ex.wait(dve, S * HQ + h)
                            sc.done(dve.scalar_tensor_tensor(prob[:, k % R, h, off:TG], tanh_s[:, h // 2, h % 2, off:TG], kn["alpha"][:, 0:1],
                                                             ps[:, E0 + h % 2, off:TG], ALU.mult, ALU.add))

        @block.gpsimd
        def _(pool):
            o_n.start(pool)
            with pool.Fori(0, B * NHQ // U) as i:
                for u in range(U):
                    for g in range(GB):
                        it = i * U + u
                        G = it * GB + g
                        l_sb.wait(pool, G)
                        o_out.wait(pool, g % 2, it * (GB // 2) + g // 2 - 1)
                        o_n.done(pool.tensor_tensor(on_s[:, g % 2], o_s[:, g % 2], l_s[:, g % 2], ALU.mult))
                        if g == GB - 1:
                            pool.sem_inc(stacks_free[u], 1)


def row_max_phase(nc, kn, layer):
    SR, FR = QROWS, FROWS
    with ExitStack() as ctx:
        ph = Phase(nc, ctx, f"max{layer}")
        stacks_in, qk, th, sc, mx, nm, tp, out = (ph.sem(n) for n in ("stacks_in", "qk", "th", "sc", "mx", "nm", "tp", "out"))
        st = {"q": ph.sb("q", [SR, HQ, T], BF16), "k": ph.sb("k", [SR, HQ, T], BF16)}
        if layer == 0:
            st["f"], st["g"] = ph.sb("f", [FR, HQ, T], BF16), ph.sb("g", [FR, T], BF16)
        tanh_s = ph.sb("tanh", [P, TG])
        score = ph.sb("score", [P, TG])
        cmax = ph.sb("cmax", [P, GB])
        nmax = ph.sb("nmax", [P, HQ * KB])
        parts = ph.sb("parts", [HQ * KB, 3, P], BF16)
        rem = ph.sb("rem", [HQ * KB, P])
        flag = ph.sb("flag", [P, 1], I32)
        flagged = ph.sem("flagged")
        ps = kn["ps"]
        N_LOAD = NS * 4
        chunks = [(h, qb, c, min(TG, (qb + 1) * P - c * TG)) for h in range(HQ) for qb in range(KB) for c in range(qb // (TG // P) + 1)]
        NCH = len(chunks)
        NQB = HQ * KB
        with nc.Block() as block:
            @block.vector
            def _(dve):
                dve.tensor_copy(flag[:], kn["wide"][:, layer:layer + 1]).then_inc(flagged, 1)
                dve.wait_ge(flagged, 1)
        block = ctx.enter_context(nc.Block())

        @block.sync
        def _(sp):
            wide = sp.value_load(flag[0:1, 0:1], min_val=0, max_val=1)
            with sp.If(wide == 1):
                with sp.Fori(0, B * NHQ) as it:
                    wait(sp, nm, it + 1, ph.passed)
                    load_stacks(sp, kn, layer, it, st, stacks_in)
                    wait(sp, tp, it * 5 + 5, ph.passed)
                    sp.dma_start(kn["shift_d"][:, bass.ds(it * HQ, HQ), :].rearrange("k h (q p) -> (h q) k p", p=P), parts[:]).then_inc(out, 16)
                    wait(sp, out, (it + 1) * 16, ph.passed)
            sp.nop()

        @block.tensor
        def _(pe):
            wide = pe.value_load(flag[0:1, 0:1], min_val=0, max_val=1)
            with pe.If(wide == 1):
                with pe.Fori(0, B * NHQ) as it:
                    pe.wait_ge(stacks_in, (it + 1) * (16 * N_LOAD))
                    for n, (h, qb, c, w) in enumerate(chunks):
                        pe.wait_ge(mx, it * NCH + n + 1)
                        diag = c == qb // (TG // P)
                        if layer == 1:
                            mm = pe.matmul(ps[:, 0, 0:w], st["q"][:, h, qb * P:(qb + 1) * P], st["k"][:, h, c * TG:c * TG + w], start=True, stop=not diag)
                            if diag:
                                mm = pe.matmul(ps[:, 0, w - P:w], kn["identb"][:], kn["mask_qk"][:], start=False, stop=True)
                        else:
                            pe.matmul(ps[:, 1, 0:w], st["f"][:, h, qb * P:(qb + 1) * P], st["g"][:, c * TG:c * TG + w], start=True, stop=not diag)
                            if diag:
                                pe.matmul(ps[:, 1, w - P:w], kn["identb"][:], kn["mask_qk"][:], start=False, stop=True)
                            mm = pe.matmul(ps[:, 0, 0:w], st["q"][:, h, qb * P:(qb + 1) * P], st["k"][:, h, c * TG:c * TG + w], start=True, stop=True)
                        mm.then_inc(qk, 1)
                    wait(pe, nm, it + 2, ph.passed, apart=True)
                    pe.transpose(ps[0:NQB, 2, 0:P], nmax[:], kn["ident"][:]).then_inc(tp, 1)
            pe.nop()

        @block.scalar
        def _(act):
            wide = act.value_load(flag[0:1, 0:1], min_val=0, max_val=1)
            with act.If(wide == 1):
                if layer == 0:
                    with act.Fori(0, B * NHQ) as it:
                        for n, (h, qb, c, w) in enumerate(chunks):
                            act.wait_ge(qk, it * NCH + n + 1)
                            act.activation(tanh_s[:, 0:w], ps[:, 0, 0:w], ACT.Tanh, scale=kn["rbeta"][:, 0:1]).then_inc(th, 1)
                else:
                    act.nop()
            act.nop()

        @block.vector
        def _(dve):
            wide = dve.value_load(flag[0:1, 0:1], min_val=0, max_val=1)
            with dve.If(wide == 1):
                dve.sem_inc(mx, 1)
                dve.sem_inc(nm, 1)
                with dve.Fori(0, B * NHQ) as it:
                    n_row = 0
                    for n, (h, qb, c, w) in enumerate(chunks):
                        if layer == 0:
                            dve.wait_ge(th, it * NCH + n + 1)
                            dve.scalar_tensor_tensor(score[:, 0:w], tanh_s[:, 0:w], kn["alpha"][:, 0:1], ps[:, 1, 0:w], ALU.mult, ALU.add).then_inc(sc, 1)
                            dve.wait_ge(sc, it * (NCH + NQB) + n_row + n + 1)
                            src = score[:, 0:w]
                        else:
                            dve.wait_ge(qk, it * NCH + n + 1)
                            src = ps[:, 0, 0:w]
                        dve.tensor_reduce(cmax[:, c:c + 1], src, AX.X, ALU.max).then_inc(mx, 1)
                        dve.wait_ge(mx, it * NCH + n + 2)
                        if c == qb // (TG // P):
                            row = h * KB + qb
                            dve.tensor_reduce(nmax[:, row:row + 1], cmax[:, 0:c + 1], AX.X, ALU.max).then_inc(sc, 1)
                            n_row += 1
                            dve.wait_ge(sc, it * ((NCH if layer == 0 else 0) + NQB) + n_row + (n + 1 if layer == 0 else 0))
                    dve.tensor_scalar(nmax[:], nmax[:], -1.0, None, ALU.mult).then_inc(nm, 1)
                    dve.wait_ge(tp, it * 5 + 1)
                    ptile = ps[0:NQB, 2, 0:P]
                    dve.tensor_copy(parts[:, 0], ptile).then_inc(tp, 1)
                    dve.wait_ge(tp, it * 5 + 2)
                    dve.tensor_tensor(rem[:], ptile, parts[:, 0], ALU.subtract).then_inc(tp, 1)
                    dve.wait_ge(tp, it * 5 + 3)
                    dve.tensor_copy(parts[:, 1], rem[:]).then_inc(tp, 1)
                    dve.wait_ge(tp, it * 5 + 4)
                    dve.tensor_tensor(parts[:, 2], rem[:], parts[:, 1], ALU.subtract).then_inc(tp, 1)
            dve.nop()


class Norm:

    def __init__(self, ph, name, slots=2):
        self.slots = slots
        self.st = ph.sb(f"{name}_st", [P, slots, TT, 6])
        self.mv = ph.sb(f"{name}_mv", [P, slots, TT, 2])
        self.sd = ph.sb(f"{name}_sd", [P, slots, TT])
        self.rs = ph.sb(f"{name}_rs", [P, slots, TT])
        self.nb = ph.sb(f"{name}_nb", [P, slots, TT])
        self.stats, self.agg, self.root, self.inv, self.shift, self.out = (
            ph.count(f"{name}_{n}") for n in ("stats", "agg", "root", "inv", "shift", "out"))

    def start(self, dve=None, act=None):
        for eng, counts in ((dve, (self.stats, self.agg, self.inv, self.shift, self.out)), (act, (self.root,))):
            if eng is not None:
                for c in counts:
                    c.start(eng)

    def take(self, dve, g, u, rows, wait_row):
        self.out.wait(dve, g - self.slots)
        for t in range(TT):
            wait_row(t)
            ins = dve.bn_stats(self.st[:, u, t], rows(t))
        self.stats.done(ins)
        self.stats.wait(dve, g, apart=True)
        for t in range(TT):
            ins = dve.bn_aggr(self.mv[:, u, t], self.st[:, u, t])
        self.agg.done(ins)

    def take_root(self, act, g, u, eps):
        self.agg.wait(act, g)
        self.root.done(act.activation(self.sd[:, u], self.mv[:, u, :, 1], ACT.Sqrt, bias=eps))

    def invert(self, dve, g, u):
        self.root.wait(dve, g)
        self.inv.done(dve.reciprocal(self.rs[:, u], self.sd[:, u]))
        self.inv.wait(dve, g)
        self.shift.done(dve.scalar_tensor_tensor(self.nb[:, u], self.mv[:, u, :, 0], -1.0, self.rs[:, u], ALU.mult, ALU.mult))

    def apply(self, dve, g, u, dst, src):
        self.shift.wait(dve, g)
        for t in range(TT):
            ins = dve.tensor_scalar(dst(t), src(t), self.rs[:, u, t:t + 1], self.nb[:, u, t:t + 1], ALU.mult, ALU.add)
        self.out.done(ins)


def post0_phase(nc, kn, w, x_d, out_d):
    Y1, XT0, HB, Y2 = 0, 2, 4, 5
    STAGES = 2
    with ExitStack() as ctx:
        ph = Phase(nc, ctx, "post0")
        w_in, o_in, x_in = ph.sem("w_in"), [ph.sem(f"o_in{i}") for i in range(GB)], [ph.sem(f"x_in{i}") for i in range(GB)]
        y1, r1, y2, r2 = (ph.count(n) for n in ("y1", "r1", "y2", "r2"))
        xt_ps, xt_sb = ph.count("xt_ps"), ph.count("xt_sb")
        h_ps, h_sb, xb = (ph.count(n) for n in ("h_ps", "h_sb", "xb"))
        out = ph.stores("out_dma", 2)
        n1, n2 = Norm(ph, "n1"), Norm(ph, "n2")
        wo = ph.sb("wo", [P, DC, D])
        a_s = ph.sb("a", [P, DC, 16])
        b_s = ph.sb("b", [16, D])
        bias = ph.sb("bias", [P, D])
        o_s = ph.sb("o", [P, GB, DC, TG])
        xs = ph.sb("x", [P, GB, TT, D])
        rr = ph.sb("rr", [P, 2, TT, D])
        x1 = ph.sb("x1", [P, 2, TT, D])
        x1b = ph.sb("x1b", [P, 2, TT, D])
        xt = ph.sb("xt", [P, 2, DC, TG])
        h_s = ph.sb("h", [16, 2, TG])
        rr2 = ph.sb("rr2", [P, 2, TT, D])
        x2 = ph.sb("x2", [P, 2, TT, D])
        ps = kn["ps"]
        block = ctx.enter_context(nc.Block())

        def rows(d, b, gq):
            return d[bass.ds(b * T + gq * TG, TG), :].rearrange("(t p) d -> p t d", p=P)

        def load(sp, b, gq):
            sp.dma_start(o_s[:, gq], kn["o_d"][bass.ds(b * D, D), gq * TG:(gq + 1) * TG].rearrange("(c p) t -> p c t", p=P)).then_inc(o_in[gq], 16)
            sp.dma_start(xs[:, gq], rows(x_d, b, gq)).then_inc(x_in[gq], 16)

        def staged(turn, order):
            for s in range(BU * GB + STAGES - 1):
                for stage in order:
                    n = s - int(stage)
                    if 0 <= n < BU * GB:
                        yield stage, turn * BU + n // GB, n % GB, turn * (BU * GB) + n

        @block.sync
        def _(sp):
            for dst, src in ((wo, w["wo"]), (a_s, w["a"]), (b_s, w["b"]), (bias, w["bias"])):
                sp.dma_start(dst[:], src).then_inc(w_in, 16)
            for gq in range(GB):
                load(sp, 0, gq)
            out.start(sp)
            with sp.Fori(0, B // BU) as turn:
                for n in range(BU * GB):
                    b, gq, g = turn * BU + n // GB, n % GB, turn * (BU * GB) + n
                    r1.wait(sp, g * 2 + 1)
                    load(sp, (b + 1) % B, gq)
                    n2.out.wait(sp, g)
                    out.done(sp.dma_start(rows(out_d, b, gq), x2[:, gq % 2]), gq % 2)
            for u in range(2):
                out.wait(sp, u, B * GB // 2 - 1)
            for gq in range(GB):
                sp.wait_ge(x_in[gq], 16 * (B + 1))
                sp.wait_ge(o_in[gq], 16 * (B + 1))

        @block.tensor
        def _(pe):
            for c in (y1, xt_ps, h_ps, y2):
                c.start(pe)
            pe.wait_ge(w_in, 64)
            with pe.Fori(0, B // BU) as turn:
                for stage, b, gq, g in staged(turn, "01"):
                    u = gq % 2
                    if stage == "0":
                        pe.wait_ge(o_in[gq], 16 * (b + 1))
                        for half in range(2):
                            r1.wait(pe, (g - 1) * 2 + half)
                            for t in range(2 * half, 2 * half + 2):
                                for c in range(DC):
                                    mm = pe.matmul(ps[:, Y1 + half, (t % 2) * D:(t % 2 + 1) * D], o_s[:, gq, c, t * P:(t + 1) * P], wo[:, c, :], start=c == 0, stop=c == DC - 1)
                            y1.done(mm)
                    else:
                        n1.out.wait(pe, g)
                        for c in range(DC):
                            xt_sb.wait(pe, (g - 1) * DC + c)
                            for t in range(TT):
                                mm = pe.transpose(ps[:, XT0 + c, t * P:(t + 1) * P], x1[:, u, t, c * P:(c + 1) * P], kn["ident"][:])
                            xt_ps.done(mm)
                        xt_sb.wait(pe, g * DC + DC - 1)
                        h_sb.wait(pe, g - 1)
                        for c in range(DC):
                            mm = pe.matmul(ps[0:16, HB], a_s[:, c, :], xt[:, u, c], start=c == 0, stop=c == DC - 1)
                        h_ps.done(mm)
                        h_sb.wait(pe, g)
                        for half in range(2):
                            r2.wait(pe, (g - 1) * 2 + half)
                            for t in range(2 * half, 2 * half + 2):
                                y = ps[:, Y2 + half, (t % 2) * D:(t % 2 + 1) * D]
                                for c in range(DC):
                                    pe.matmul(y, xt[:, u, c, t * P:(t + 1) * P], kn["w4"][:, c, :], start=c == 0, stop=False)
                                mm = pe.matmul(y, h_s[:, u, t * P:(t + 1) * P], b_s[:], start=False, stop=True)
                            y2.done(mm)

        @block.scalar
        def _(act):
            for c in (xt_sb, h_sb):
                c.start(act)
            n1.start(act=act)
            n2.start(act=act)
            with act.Fori(0, B // BU) as turn:
                for stage, b, gq, g in staged(turn, "01"):
                    u = gq % 2
                    if stage == "0":
                        n1.take_root(act, g, u, kn["eps"][:, 0:1])
                    else:
                        for c in range(DC):
                            xt_ps.wait(act, g * DC + c)
                            y2.wait(act, (g - 2) * 2 + 1)
                            xt_sb.done(act.activation(xt[:, u, c], ps[:, XT0 + c], ACT.Copy))
                        h_ps.wait(act, g)
                        h_sb.done(act.activation(h_s[:, u], ps[0:16, HB], ACT.Copy))
                        n2.take_root(act, g, u, kn["eps"][:, 0:1])

        @block.vector
        def _(dve):
            for c in (r1, r2):
                c.start(dve)
            n1.start(dve=dve)
            n2.start(dve=dve)
            with dve.Fori(0, B // BU) as turn:
                for stage, b, gq, g in staged(turn, (0, 1, 0.5, 1.5)):
                    u = gq % 2
                    if stage == 0:
                        dve.wait_ge(x_in[gq], 16 * (b + 1))
                        for half in range(2):
                            y1.wait(dve, g * 2 + half)
                            ts = slice(2 * half, 2 * half + 2)
                            r1.done(dve.tensor_tensor(rr[:, u, ts], ps[:, Y1 + half].rearrange("p (t d) -> p t d", t=2), xs[:, gq, ts], ALU.add))
                        n1.take(dve, g, u, lambda t: rr[:, u, t], lambda t: r1.wait(dve, g * 2 + t // 2))
                    elif stage == 0.5:
                        n1.invert(dve, g, u)
                        xt_ps.wait(dve, (g - 2) * DC + DC - 1)
                        xb.wait(dve, g - 2)
                        n1.apply(dve, g, u, lambda t: x1[:, u, t], lambda t: rr[:, u, t])
                    elif stage == 1:
                        xb.wait(dve, g)
                        for half in range(2):
                            y2.wait(dve, g * 2 + half)
                            ts = slice(2 * half, 2 * half + 2)
                            r2.done(dve.tensor_tensor(rr2[:, u, ts], ps[:, Y2 + half].rearrange("p (t d) -> p t d", t=2), x1b[:, u, ts], ALU.add))
                        n2.take(dve, g, u, lambda t: rr2[:, u, t], lambda t: r2.wait(dve, g * 2 + t // 2))
                    else:
                        n2.invert(dve, g, u)
                        out.wait(dve, u, b * (GB // 2) + gq // 2 - 1)
                        n2.apply(dve, g, u, lambda t: x2[:, u, t], lambda t: rr2[:, u, t])

        @block.gpsimd
        def _(pool):
            xb.start(pool)
            pool.wait_ge(w_in, 64)
            with pool.Fori(0, B // BU) as turn:
                for stage, b, gq, g in staged(turn, "0"):
                    u = gq % 2
                    n1.out.wait(pool, g)
                    r2.wait(pool, (g - 2) * 2 + 1)
                    for t in range(TT):
                        ins = pool.tensor_tensor(x1b[:, u, t], x1[:, u, t], bias[:], ALU.add)
                    xb.done(ins)


def post1_phase(nc, kn, w, x_d, out_d):
    Y1, XT0, KK, VR = 0, 1, 3, 5
    STAGES = 3
    with ExitStack() as ctx:
        ph = Phase(nc, ctx, "post1")
        w_in, o_in, x_in = ph.sem("w_in"), [ph.sem(f"o_in{i}") for i in range(GB)], [ph.sem(f"x_in{i}") for i in range(GB)]
        y1, r1 = ph.count("y1"), ph.count("r1")
        xt_ps, xt_sb, edge = ph.count("xt_ps"), ph.count("xt_sb"), ph.count("edge")
        pr_, pk_, mr_, mk_ = (ph.count(n) for n in ("pr", "pk", "mr", "mk"))
        k_ps, k_re, k_sq = (ph.count(n) for n in ("k_ps", "k_re", "k_sq"))
        r_ps, r_sg, v_ps, rv, r2 = (ph.count(n) for n in ("r_ps", "r_sg", "v_ps", "rv", "r2"))
        omitted = ph.sem("one_minus")
        out = ph.stores("out_dma", 2)
        n1, n2 = Norm(ph, "n1"), Norm(ph, "n2")
        wo, wr, wk, wv = (ph.sb(n, [P, DC, D]) for n in ("wo", "wr", "wk", "wv"))
        mu = ph.sb("mu", [P, 2, DC])
        om = ph.sb("om", [P, 2, DC])
        o_s = ph.sb("o", [P, GB, DC, TG])
        xs = ph.sb("x", [P, GB, TT, D])
        rr = ph.sb("rr", [P, 2, TT, D])
        x3 = ph.sb("x3", [P, GB, TT, D])
        xt = ph.sb("xt", [P, 2, DC, TG + 1])
        prev = ph.sb("prev", [P, 2, DC, TG])
        mix = ph.sb("mix", [P, 2, 2, DC, TG])
        kr = ph.sb("kr", [P, DC, TG])
        ka = ph.sb("ka", [P, 2, DC, TG])
        sg = ph.sb("sg", [P, 2, TT, D])
        rr2 = ph.sb("rr2", [P, 2, TT, D])
        x4 = ph.sb("x4", [P, 2, TT, D])
        ps = kn["ps"]
        block = ctx.enter_context(nc.Block())

        def rows(d, b, gq):
            return d[bass.ds(b * T + gq * TG, TG), :].rearrange("(t p) d -> p t d", p=P)

        def load(sp, b, gq):
            sp.dma_start(o_s[:, gq], kn["o_d"][bass.ds(b * D, D), gq * TG:(gq + 1) * TG].rearrange("(c p) t -> p c t", p=P)).then_inc(o_in[gq], 16)
            sp.dma_start(xs[:, gq], rows(x_d, b, gq)).then_inc(x_in[gq], 16)

        def staged(turn, order):
            for s in range(BU * GB + STAGES - 1):
                for stage in order:
                    n = s - int(stage)
                    if 0 <= n < BU * GB:
                        yield stage, turn * BU + n // GB, n % GB, turn * (BU * GB) + n

        @block.sync
        def _(sp):
            for dst, src in ((wo, w["wo"]), (wr, w["wr"]), (wk, w["wk"]), (wv, w["wv"]), (mu, w["mu"])):
                sp.dma_start(dst[:], src).then_inc(w_in, 16)
            for gq in range(GB):
                load(sp, 0, gq)
            out.start(sp)
            with sp.Fori(0, B // BU) as turn:
                for n in range(BU * GB):
                    b, gq, g = turn * BU + n // GB, n % GB, turn * (BU * GB) + n
                    r1.wait(sp, g * 2 + 1)
                    load(sp, (b + 1) % B, gq)
                    n2.out.wait(sp, g)
                    out.done(sp.dma_start(rows(out_d, b, gq), x4[:, gq % 2]), gq % 2)
            for u in range(2):
                out.wait(sp, u, B * GB // 2 - 1)
            for gq in range(GB):
                sp.wait_ge(x_in[gq], 16 * (B + 1))
                sp.wait_ge(o_in[gq], 16 * (B + 1))

        @block.tensor
        def _(pe):
            for c in (y1, xt_ps, k_ps, r_ps, v_ps):
                c.start(pe)
            pe.wait_ge(w_in, 80)

            def token_rows(bank, lhs, rhs):
                for t in range(2):
                    for c in range(DC):
                        mm = pe.matmul(ps[:, bank, t * D:(t + 1) * D], lhs(t, c), rhs[:, c, :], start=c == 0, stop=c == DC - 1)
                return mm

            with pe.Fori(0, B // BU) as turn:
                for stage, b, gq, g in staged(turn, "012"):
                    u = gq % 2
                    if stage == "0":
                        pe.wait_ge(o_in[gq], 16 * (b + 1))
                        for half in range(2):
                            r1.wait(pe, g * 2 + half - 1)
                            y1.done(token_rows(Y1, lambda t, c: o_s[:, gq, c, (2 * half + t) * P:(2 * half + t + 1) * P], wo))
                    elif stage == "1":
                        n1.out.wait(pe, g)
                        for c in range(DC):
                            xt_sb.wait(pe, (g - 1) * DC + c)
                            for t in range(TT):
                                mm = pe.transpose(ps[:, XT0 + c, t * P:(t + 1) * P], x3[:, gq, t, c * P:(c + 1) * P], kn["ident"][:])
                            xt_ps.done(mm)
                    else:
                        mk_.wait(pe, g * DC + DC - 1)
                        for m in range(DC):
                            k_re.wait(pe, (g - 1) * DC + m)
                            for c in range(DC):
                                mm = pe.matmul(ps[:, KK + m], wk[:, c, m * P:(m + 1) * P], mix[:, u, 1, c], start=c == 0, stop=c == DC - 1)
                            k_ps.done(mm)
                        mr_.wait(pe, g * DC + DC - 1)
                        for half in range(2):
                            r_sg.wait(pe, (g - 1) * 2 + half)
                            r_ps.done(token_rows(VR + half, lambda t, c: mix[:, u, 0, c, (2 * half + t) * P:(2 * half + t + 1) * P], wr))
                        k_sq.wait(pe, g * DC + DC - 1)
                        for half in range(2):
                            rv.wait(pe, g * 2 + half - 1)
                            v_ps.done(token_rows(VR + 2, lambda t, c: ka[:, u, c, (2 * half + t) * P:(2 * half + t + 1) * P], wv))

        @block.scalar
        def _(act):
            for c in (xt_sb, k_re, r_sg):
                c.start(act)
            n1.start(act=act)
            n2.start(act=act)
            with act.Fori(0, B // BU) as turn:
                for stage, b, gq, g in staged(turn, "012"):
                    u = gq % 2
                    if stage == "0":
                        n1.take_root(act, g, u, kn["eps"][:, 0:1])
                    elif stage == "1":
                        mr_.wait(act, (g - 2) * DC + DC - 1)
                        mk_.wait(act, (g - 2) * DC + DC - 1)
                        edge.wait(act, g - 1)
                        for c in range(DC):
                            xt_ps.wait(act, g * DC + c)
                            xt_sb.done(act.activation(xt[:, u, c, 1:TG + 1], ps[:, XT0 + c], ACT.Copy))
                    else:
                        for m in range(DC):
                            k_ps.wait(act, g * DC + m)
                            k_sq.wait(act, (g - 1) * DC + m)
                            k_re.done(act.activation(kr[:, m], ps[:, KK + m], ACT.Relu))
                        for half in range(2):
                            r_ps.wait(act, g * 2 + half)
                            rv.wait(act, (g - 2) * 2 + half)
                            r_sg.done(act.activation(sg[:, u, 2 * half:2 * half + 2], ps[:, VR + half].rearrange("p (t d) -> p t d", t=2), ACT.Sigmoid))
                        n2.take_root(act, g, u, kn["eps"][:, 0:1])

        @block.vector
        def _(dve):
            for c in (r1, rv, r2, edge, mr_, mk_):
                c.start(dve)
            n1.start(dve=dve)
            n2.start(dve=dve)
            dve.wait_ge(w_in, 80)
            dve.tensor_scalar(om[:], mu[:], -1.0, 1.0, ALU.mult, ALU.add).then_inc(omitted, 1)
            with dve.Fori(0, B // BU) as turn:
                for stage, b, gq, g in staged(turn, (0, 1, 2, 0.5, 2.5)):
                    u = gq % 2
                    if stage == 0:
                        dve.wait_ge(x_in[gq], 16 * (b + 1))
                        for half in range(2):
                            y1.wait(dve, g * 2 + half)
                            ts = slice(2 * half, 2 * half + 2)
                            r1.done(dve.tensor_tensor(rr[:, u, ts], ps[:, Y1].rearrange("p (t d) -> p t d", t=2), xs[:, gq, ts], ALU.add))
                        n1.take(dve, g, u, lambda t: rr[:, u, t], lambda t: r1.wait(dve, g * 2 + t // 2))
                    elif stage == 0.5:
                        n1.invert(dve, g, u)
                        r2.wait(dve, (g - GB) * 2 + 1)
                        n1.apply(dve, g, u, lambda t: x3[:, gq, t], lambda t: rr[:, u, t])
                    elif stage == 1:
                        pr_.wait(dve, (g - 2) * DC + DC - 1)
                        pk_.wait(dve, (g - 2) * DC + DC - 1)
                        if gq == 0:
                            ins = dve.memset(xt[:, u, :, 0:1], 0.0)
                        else:
                            xt_sb.wait(dve, g * DC - 1)
                            ins = dve.tensor_copy(xt[:, u, :, 0:1], xt[:, 1 - u, :, TG:TG + 1])
                        edge.done(ins)
                        for c in range(DC):
                            xt_sb.wait(dve, g * DC + c)
                            pk_.wait(dve, g * DC + c)
                            k_ps.wait(dve, (g - 2) * DC + DC - 1)
                            mk_.done(dve.scalar_tensor_tensor(mix[:, u, 1, c], xt[:, u, c, 1:TG + 1], mu[:, 1, c:c + 1], prev[:, 1, c], ALU.mult, ALU.add))
                        for c in range(DC):
                            pr_.wait(dve, g * DC + c)
                            r_ps.wait(dve, (g - 2) * 2 + 1)
                            mr_.done(dve.scalar_tensor_tensor(mix[:, u, 0, c], xt[:, u, c, 1:TG + 1], mu[:, 0, c:c + 1], prev[:, 0, c], ALU.mult, ALU.add))
                    elif stage == 2:
                        for half in range(2):
                            ts = slice(2 * half, 2 * half + 2)
                            v_ps.wait(dve, g * 2 + half)
                            r_sg.wait(dve, g * 2 + half)
                            rv.done(dve.tensor_tensor(rr2[:, u, ts], ps[:, VR + 2].rearrange("p (t d) -> p t d", t=2), sg[:, u, ts], ALU.mult))
                            rv.wait(dve, g * 2 + half)
                            r2.done(dve.tensor_tensor(rr2[:, u, ts], rr2[:, u, ts], x3[:, gq, ts], ALU.add))
                        n2.take(dve, g, u, lambda t: rr2[:, u, t], lambda t: r2.wait(dve, g * 2 + t // 2))
                    else:
                        n2.invert(dve, g, u)
                        out.wait(dve, u, b * (GB // 2) + gq // 2 - 1)
                        n2.apply(dve, g, u, lambda t: x4[:, u, t], lambda t: rr2[:, u, t])

        @block.gpsimd
        def _(pool):
            for c in (pr_, pk_, k_sq):
                c.start(pool)
            pool.wait_ge(omitted, 1)
            with pool.Fori(0, B // BU) as turn:
                for stage, b, gq, g in staged(turn, "12"):
                    u = gq % 2
                    if stage == "1":
                        edge.wait(pool, g)
                        for which, cnt, mixed in ((1, pk_, mk_), (0, pr_, mr_)):
                            for c in range(DC):
                                xt_sb.wait(pool, g * DC + c)
                                mixed.wait(pool, (g - 1) * DC + c)
                                cnt.done(pool.tensor_scalar(prev[:, which, c], xt[:, u, c, 0:TG], om[:, which, c:c + 1], 0.0, ALU.mult, ALU.add))
                    else:
                        for m in range(DC):
                            k_re.wait(pool, g * DC + m)
                            v_ps.wait(pool, (g - 2) * 2 + 1)
                            k_sq.done(pool.tensor_tensor(ka[:, u, m], kr[:, m], kr[:, m], ALU.mult))


def two_blocks(nc, a, out):
    with ExitStack() as ctx:
        def sb(name, shape, dt=F32):
            return ctx.enter_context(nc.sbuf_tensor(name, shape, dt))

        def dram(name, shape, dt=F32):
            return nc.dram_tensor(name, shape, dt, kind="Internal").ap()

        kn = {
            "ps": ctx.enter_context(nc.psum_tensor("ps", [P, 8, TG], F32)),
            "ident": sb("ident", [P, P]), "ones": sb("ones", [P, P]), 
            "pick": sb("pick", [P, P]), "identb": sb("identb", [P, P], BF16), "headsum": sb("headsum", [P, P], BF16),
            "mask_kq": sb("mask_kq", [P, P], BF16), "mask_qk": sb("mask_qk", [P, P], BF16),
            "C": sb("C", [NF, H, NF]), "w4": sb("w4", [P, DC, D]),
            "alpha": sb("alpha", [P, 1]), "rbeta": sb("rbeta", [P, 1]), "wide": sb("wide", [P, 2]), "eps": sb("eps", [P, 1]),
            "q_d": dram("q_parts", [3, B * D, T], BF16), "k_d": dram("k_parts", [3, B * D, T], BF16),
            "f_d": dram("f_parts", [3, B * H * NF, T], BF16), "g_d": dram("g_parts", [3, B * NHQ * NF, T], BF16),
            "v_d": dram("v_ones", [B * NHQ, P, KB, HQ * VW]), "shift_d": dram("shift", [3, B * H, T], BF16),
            "o_d": dram("o_t", [B * D, T]), "x2_d": dram("x2", [B * T, D]),
        }
        const_in, made = ctx.enter_context(nc.semaphore("const_in")), ctx.enter_context(nc.semaphore("made"))

        def chunked(ap):
            return ap.rearrange("(c p) n -> p c n", p=P)

        with nc.Block() as block:
            @block.sync
            def _(sp):
                for i, name in enumerate(("ident", "ones", "pick")):
                    sp.dma_start(kn[name][:], a["consts"][i]).then_inc(const_in, 16)
                for i, name in enumerate(("identb", "headsum", "mask_kq", "mask_qk")):
                    sp.dma_start(kn[name][:], a["constsb"][i]).then_inc(const_in, 16)
                sp.wait_ge(const_in, 16 * 7)

            @block.vector
            def _(dve):
                dve.memset(kn["eps"][:], EPS).then_inc(made, 1)
                dve.memset(kn["wide"][:], 0.0).then_inc(made, 1)

        setup_phase(nc, kn, {"tw": a["tw"], "tr": a["L0_attn_transforms"], "kernel0": chunked(a["L0_ffn_kernel"]), "scalars": a["scalars"]})
        x0 = a["L0_attn_x"]
        project_phase(nc, kn, 0, {"wq": chunked(a["wq0"]), "wk": chunked(a["wk0"]), "wv": chunked(a["wv0"]), "w12": chunked(a["w12"])}, x0)
        row_max_phase(nc, kn, 0)
        attend_phase(nc, kn, 0)
        post0_phase(nc, kn, {"wo": chunked(a["wo0"]), "a": chunked(a["L0_ffn_a"]), "b": a["L0_ffn_b"], "bias": a["bias"]}, x0, kn["x2_d"])
        project_phase(nc, kn, 1, {"wq": chunked(a["wq1"]), "wk": chunked(a["wk1"]), "wv": chunked(a["wv1"]), "cos": a["cos"], "sin": a["sin"]}, kn["x2_d"])
        row_max_phase(nc, kn, 1)
        attend_phase(nc, kn, 1)
        post1_phase(nc, kn, {"wo": chunked(a["wo1"]), "wr": chunked(a["wr1"]), "wk": chunked(a["wkf1"]), "wv": chunked(a["wvf1"]),
                             "mu": a["mu"]}, kn["x2_d"], out)


def kernel(**inputs):
    import ml_dtypes as _md
    import numpy as _np
    import concourse.bacc as _bacc
    from concourse import mybir as _mybir
    from concourse.bass_utils import run_bass_kernel_spmd as _run

    x = {k: _np.asarray(v) for k, v in inputs.items()}

    eye = _np.eye(P, dtype=_np.float32)
    r = _np.arange(P)
    pick = (r[:, None] == (r[None, :] // VW) * VW + HD).astype(_np.float32)
    headsum = (r[:, None] // (HD // 2) == r[None, :] // (HD // 2)).astype(_np.float32)
    behind = _np.where(r[:, None] > r[None, :], MASKED, 0.0).astype(_np.float32)
    inv_freq = _np.float32(1.0) / _np.power(_np.float32(10000.0), _np.arange(0, HD, 2, dtype=_np.float32) / _np.float32(HD))
    freqs = _np.arange(T, dtype=_np.float32)[:, None] * inv_freq[None, :].astype(_np.float32)
    emb = freqs[:, r % (HD // 2)].T

    def t(a):
        return _np.ascontiguousarray(_np.asarray(a).T)

    def halves(a):
        return a.reshape(H, 2, HD // 2, D).transpose(1, 0, 2, 3).reshape(D, D)

    def spread(a, n):
        return _np.ascontiguousarray(_np.broadcast_to(_np.asarray(a), (n,) + _np.asarray(a).shape))

    qkv = x["L0_attn_qkv_w"]
    arrays = {
        "consts": _np.stack([eye, _np.ones((P, P), _np.float32), pick]),
        "constsb": _np.stack([eye, headsum, behind, behind.T]).astype(_md.bfloat16),
        "cos": _np.cos(emb).astype(_np.float32), "sin": _np.sin(emb).astype(_np.float32),
        "L0_attn_x": _np.ascontiguousarray(x["L0_attn_x"].reshape(B * T, D)),
        "wq0": t(qkv[:D]), "wk0": t(qkv[D:2 * D]), "wv0": t(qkv[2 * D:]), "wo0": t(x["L0_attn_out_w"]),
        "w12": t(_np.concatenate([x["L0_attn_hex_w"], x["L0_attn_q6_w"]])),
        "L0_attn_transforms": x["L0_attn_transforms"],
        "tw": spread(x["L0_attn_transform_weights"], NF),
        "scalars": spread(_np.stack([x["L0_attn_hamming_lambda_logit"].reshape(()), x["L0_attn_scale_logit"].reshape(()),
                                     x["L0_attn_sips_alpha"].reshape(()), x["L0_attn_sips_beta"].reshape(())]), P),
        "L0_ffn_kernel": x["L0_ffn_kernel"], "L0_ffn_a": x["L0_ffn_a"], "L0_ffn_b": x["L0_ffn_b"],
        "bias": spread(x["L0_ffn_bias"], P),
        "wq1": t(halves(x["L1_attn_Wq"])), "wk1": t(halves(x["L1_attn_Wk"])), "wv1": t(x["L1_attn_Wv"]), "wo1": t(x["L1_attn_Wo"]),
        "wr1": t(x["L1_ffn_W_r"]), "wkf1": t(x["L1_ffn_W_k"]), "wvf1": t(x["L1_ffn_W_v"]),
        "mu": _np.ascontiguousarray(_np.stack([x["L1_ffn_mu_r"], x["L1_ffn_mu_k"]]).reshape(2, DC, P).transpose(2, 0, 1)),
    }
    nc = _bacc.Bacc("TRN2", target_bir_lowering=False, num_devices=1)
    aps = {n: nc.dram_tensor(f"in_{n}", v.shape, _mybir.dt.from_np(v.dtype), kind="ExternalInput").ap() for n, v in arrays.items()}
    out = nc.dram_tensor("out", (B * T, D), _mybir.dt.float32, kind="ExternalOutput").ap()
    two_blocks(nc, aps, out)
    res = _run(nc, [{f"in_{n}": _np.ascontiguousarray(v) for n, v in arrays.items()}], core_ids=[0])
    return res.results[0]["out"].reshape(B, T, D)
```

```python
from contextlib import ExitStack

import concourse.bass as bass
from concourse import mybir

F32 = mybir.dt.float32
BF16 = mybir.dt.bfloat16
I32 = mybir.dt.int32
ACT = mybir.ActivationFunctionType
ALU = mybir.AluOpType
AX = mybir.AxisListType

B, T, D = 4, 2048, 256
H, HD = 16, 16
P = 128
DC = D // P
TG = 512
GB = T // TG
TT = TG // P
KB = T // P
HQ = 4
NHQ = H // HQ
NF = 12
VW = 32
SLOTS_A = (0, 1, 2, 0, 1, 0)
SLOTS_B = (0, 0, 0, 1, 1, 2)
NS = len(SLOTS_A)
QROWS = NS * HD
FROWS = NS * NF
MASKED = -1.0e30
BOUND = 60.0
EPS = 1e-5


APART = (mybir.EngineType.Pool, mybir.EngineType.SP)


def wait(eng, sem, value, passed, apart=False):
    eng.wait_ge(sem, value)
    if apart or eng.engine in APART:
        eng.sem_inc(passed, 1)


class Count:

    CREDIT = 8

    def __init__(self, sem, passed, unit=1):
        self.sem, self.passed, self.unit = sem, passed, unit

    def start(self, eng):
        eng.sem_inc(self.sem, self.CREDIT * self.unit)

    def done(self, ins):
        ins.then_inc(self.sem, self.unit)

    def wait(self, eng, item, apart=False):
        wait(eng, self.sem, (item + (1 + self.CREDIT)) * self.unit, self.passed, apart)


class Stores:

    def __init__(self, sems, passed, n=1):
        self.sems, self.passed, self.unit = sems, passed, 16 * n

    def start(self, eng):
        for sem in self.sems:
            eng.sem_inc(sem, self.unit)

    def done(self, ins, slot):
        ins.then_inc(self.sems[slot], 16)

    def wait(self, eng, slot, use):
        wait(eng, self.sems[slot], (use + 2) * self.unit, self.passed)


class Chain:

    def __init__(self, sem, per_turn=0, turn=0):
        self.sem, self.per_turn, self.turn, self.n = sem, per_turn, turn, 0

    def link(self, eng, ins):
        ins.then_inc(self.sem, 1)
        self.n += 1
        eng.wait_ge(self.sem, self.turn * self.per_turn + self.n)

    def close(self):
        assert not self.per_turn or self.n == self.per_turn, (self.n, self.per_turn)


class Phase:

    def __init__(self, nc, ctx, name):
        self.nc, self.ctx, self.name, self.sems = nc, ctx, name, []
        ctx.callback(self.clear)
        self.passed = self.sem("passed")

    def sb(self, name, shape, dt=F32):
        return self.ctx.enter_context(self.nc.sbuf_tensor(f"{self.name}_{name}", shape, dt))

    def sem(self, name):
        self.sems.append(self.nc.alloc_semaphore(f"{self.name}_{name}"))
        return self.sems[-1]

    def clear(self):
        self.nc.clear_and_free_semaphores(self.sems)
        self.nc.all_engine_barrier()

    def count(self, name, unit=1):
        return Count(self.sem(name), self.passed, unit)

    def stores(self, name, slots, n=1):
        return Stores([self.sem(f"{name}{i}") for i in range(slots)], self.passed, n)


def setup_phase(nc, kn, ins):
    with ExitStack() as ctx:
        ph = Phase(nc, ctx, "setup")
        loaded, done, exps, pe_done, pool_done = (ph.sem(n) for n in ("loaded", "done", "exps", "pe_done", "pool_done"))
        tw = ph.sb("tw", [NF, H, 7])
        tr = ph.sb("tr", [NF, 6, 7])
        mx = ph.sb("mx", [NF, H])
        sm = ph.sb("sm", [NF, H])
        prod = ph.sb("prod", [NF, H, 6, 7])
        mh = ph.sb("mh", [NF, H, 6])
        mag = ph.sb("mag", [NF, H, NF])
        rowabs = ph.sb("rowabs", [NF, H])
        w = ph.sb("w", [P, DC, D])
        sc = ph.sb("sc", [P, 8])
        wmax = ph.sb("wmax", [P, 4])
        scale = ph.sb("scale", [P, 2])
        rows = ph.sb("rows", [P, 2])
        bnd = ph.sb("bnd", [P, 4])
        zero = ph.sb("zero", [P, T], BF16)
        zeroed = ph.sem("zeroed")
        block = ctx.enter_context(nc.Block())

        @block.sync
        def _(sp):
            sp.wait_ge(done, 1)
            with nc.allow_non_contiguous_dma(reason="small table"):
                for d in range(6):
                    sp.dma_start(tr[6 + d:7 + d, :, :], ins["tr"][:, d, :].rearrange("t (o e) -> o e t", o=1)).then_inc(loaded, 16)
            sp.dma_start(tw[:], ins["tw"]).then_inc(loaded, 16)
            sp.dma_start(w[:], ins["kernel0"]).then_inc(loaded, 16)
            sp.dma_start(sc[:, 0:4], ins["scalars"]).then_inc(loaded, 16)
            sp.wait_ge(zeroed, 1)
            n = 0
            for part in range(3):
                for half in range(B * H // 32):
                    sp.dma_start(kn["shift_d"][part, half * 32:half * 32 + 32, :], zero[0:32, :]).then_inc(zeroed, 16)
                    n += 16
            sp.wait_ge(zeroed, 1 + n)

        @block.gpsimd
        def _(pool):
            pool.memset(zero[:], 0.0).then_inc(zeroed, 1)
            pool.wait_ge(pool_done, 1)
            pool.partition_all_reduce(wmax[:, 1:2], wmax[:, 0:1], P, bass.bass_isa.ReduceOp.max).then_inc(pool_done, 1)

        @block.scalar
        def _(act):
            act.wait_ge(loaded, 16 * 9)
            act.activation(sc[:, 4:6], sc[:, 0:2], ACT.Exp, scale=-1.0).then_inc(exps, 1)
            act.wait_ge(exps, 2)
            act.activation(tw[:], tw[:], ACT.Exp, scale=2.0).then_inc(exps, 1)

        @block.tensor
        def _(pe):
            pe.wait_ge(exps, 4)
            pe.matmul(kn["ps"][:, 0, 0:H], kn["ones"][0:NF, :], rowabs[:], start=True, stop=True).then_inc(pe_done, 1)

        @block.vector
        def _(dve):
            ch = Chain(done)
            ch.link(dve, dve.memset(tr[:], 0.0))
            dve.wait_ge(loaded, 16 * 9)
            ch.link(dve, dve.tensor_reduce(mx[:], tw[:], AX.X, ALU.max))
            dve.tensor_tensor(tw[:], tw[:], mx[:].unsqueeze(2).to_broadcast([NF, H, 7]), ALU.subtract).then_inc(exps, 1)
            ch.link(dve, dve.tensor_reduce(wmax[:, 0:1], w[:], AX.XY, ALU.max))
            ch.link(dve, dve.tensor_reduce(wmax[:, 2:3], w[:], AX.XY, ALU.min))
            ch.link(dve, dve.tensor_scalar(wmax[:, 2:3], wmax[:, 2:3], -1.0, None, ALU.mult))
            dve.tensor_tensor(wmax[:, 0:1], wmax[:, 0:1], wmax[:, 2:3], ALU.max).then_inc(pool_done, 1)
            dve.wait_ge(exps, 3)
            ch.link(dve, dve.tensor_scalar(sc[:, 4:6], sc[:, 4:6], 1.0, None, ALU.add))
            ch.link(dve, dve.reciprocal(sc[:, 6:8], sc[:, 4:6]))
            ch.link(dve, dve.tensor_scalar(sc[:, 6:7], sc[:, 6:7], 0.5, None, ALU.mult))
            ch.link(dve, dve.tensor_scalar(sc[:, 7:8], sc[:, 7:8], 1.0 / 3.0, None, ALU.mult))
            ch.link(dve, dve.tensor_copy(kn["alpha"][:], sc[:, 2:3]))
            ch.link(dve, dve.reciprocal(kn["rbeta"][:], sc[:, 3:4]))
            ch.link(dve, dve.tensor_reduce(sm[:], tw[:], AX.X, ALU.add))
            ch.link(dve, dve.reciprocal(sm[:], sm[:]))
            ch.link(dve, dve.tensor_tensor(tw[:], tw[:], sm[:].unsqueeze(2).to_broadcast([NF, H, 7]), ALU.mult))
            for h in range(H):
                ch.link(dve, dve.tensor_tensor(prod[:, h], tr[:], tw[:, h:h + 1, :].to_broadcast([NF, 6, 7]), ALU.mult))
            ch.link(dve, dve.tensor_reduce(mh[:], prod[:], AX.X, ALU.add))
            for h in range(H):
                ch.link(dve, dve.tensor_scalar(kn["C"][:, h, 0:6], kn["ident"][0:NF, 0:6], sc[0:NF, 6:7], None, ALU.mult))
            ch.link(dve, dve.tensor_scalar(kn["C"][:, :, 6:12], mh[:], sc[0:NF, 7:8], None, ALU.mult))
            ch.link(dve, dve.tensor_scalar(mag[:], kn["C"][:], -1.0, None, ALU.mult))
            ch.link(dve, dve.tensor_tensor(mag[:], mag[:], kn["C"][:], ALU.max))
            dve.tensor_reduce(rowabs[:], mag[:], AX.X, ALU.add).then_inc(exps, 1)
            dve.wait_ge(pe_done, 1)
            ch.link(dve, dve.tensor_reduce(bnd[:, 0:1], kn["ps"][:, 0, 0:H], AX.X, ALU.max))
            ch.link(dve, dve.tensor_scalar(bnd[:, 1:2], kn["alpha"][:], -1.0, None, ALU.mult))
            ch.link(dve, dve.tensor_tensor(bnd[:, 1:2], bnd[:, 1:2], kn["alpha"][:], ALU.max))
            ch.link(dve, dve.tensor_tensor(bnd[:, 0:1], bnd[:, 1:2], bnd[:, 0:1], ALU.add))
            ch.link(dve, dve.tensor_scalar(bnd[:, 2:3], bnd[:, 0:1], BOUND, None, ALU.is_le))
            ch.link(dve, dve.tensor_scalar(kn["wide"][:, 0:1], bnd[:, 2:3], -1.0, 1.0, ALU.mult, ALU.add))
            dve.wait_ge(pool_done, 2)
            m, s0, rest = wmax[:, 1:2], scale[:, 0:1], scale[:, 1:2]
            ch.link(dve, dve.tensor_scalar(s0, m, 1.0 / 7.0, None, ALU.mult))
            ch.link(dve, dve.scalar_tensor_tensor(rest, s0, -8.0, m, ALU.mult, ALU.add))
            ch.link(dve, dve.tensor_tensor(rest, rest, s0, ALU.add))
            ch.link(dve, dve.scalar_tensor_tensor(s0, rest, 1.0 / 7.0, s0, ALU.mult, ALU.add))
            ch.link(dve, dve.reciprocal(rest, s0))
            wf = w[:].rearrange("p c n -> p (c n)")
            ch.link(dve, dve.tensor_scalar(wf, wf, rest, None, ALU.mult))
            magic = 12582912.0
            ch.link(dve, dve.tensor_scalar(wf, wf, magic, None, ALU.add))
            ch.link(dve, dve.tensor_scalar(wf, wf, -magic, -8.0, ALU.add, ALU.max))
            ch.link(dve, dve.tensor_scalar(kn["w4"][:].rearrange("p c n -> p (c n)"), wf, 7.0, scale[:, 0:1], ALU.min, ALU.mult))


def project_phase(nc, kn, layer, w, x_d):
    rope = layer == 1
    tiles = ([] if rope else [("g", 0)]) + [("q", 0), ("q", 1), ("k", 0), ("k", 1)] + ([] if rope else [("f", 0), ("f", 1)])
    NTL = len(tiles)
    NTB = GB * NTL
    R = 4
    RP = 8 if rope else NTL
    assert NTB % R == 0 and NTB % RP == 0
    rows_of = {"q": P, "k": P, "f": 96, "g": NF}
    V_AT = (NTL // 2 - 1, NTL - 1)
    XT0, PRJ0, NORM, VB = 0, 2, 6, 7
    L_HI, L_REST = (2, 2) if rope else (0, 0)
    L_MID, L_LOW, L_NORM = L_REST + 1, L_REST + 1, 5 if rope else 0
    with ExitStack() as ctx:
        ph = Phase(nc, ctx, f"proj{layer}")
        w_in, x_in = ph.sem("w_in"), [ph.sem(f"x_in{i}") for i in range(GB)]
        ones_set = ph.sem("ones_set")
        xt_ps, xt_sb = ph.count("xt_ps"), ph.count("xt_sb")
        prj = ph.count("prj")
        hi, rest, mid, low = (ph.count(n) for n in ("hi", "rest", "mid", "low"))
        parts_out = [ph.sem(f"parts_out{i}") for i in range(RP)]
        v_ps, v_sb = ph.count("v_ps"), ph.count("v_sb")
        v_out = ph.stores("v_out", 2, NHQ)
        feat = ph.count("feat")
        mul, rot = ph.count("mul"), ph.count("rot")
        sq, norm, nmax = (ph.count(n) for n in ("sq", "norm", "nmax"))
        fold, flag = ph.sem("fold"), ph.sem("flag")
        wq_s, wk_s, wv_s = (ph.sb(n, [P, DC, D]) for n in ("wq", "wk", "wv"))
        xs = ph.sb("xs", [P, GB, TT, D])
        xt = ph.sb("xt", [P, 2, DC, TG])
        parts = ph.sb("parts", [P, RP, 3, TG], BF16)
        rem = ph.sb("rem", [P, R, TG])
        vs = ph.sb("vs", [P, 2, TT, H, VW])
        if rope:
            qcos, qsin = (ph.sb(n, [P, R, TG]) for n in ("qcos", "qsin"))
            cos_s, sin_s = ph.sb("cos", [P, T]), ph.sb("sin", [P, T])
            sqr = ph.sb("sqr", [P, R, TG], BF16)
            nrm = ph.sb("nrm", [P, 2, GB])
            top = ph.sb("top", [P, 8])
        else:
            w12_s, f12 = ph.sb("w12", [P, DC, NF]), ph.sb("f12", [NF, 2, TG])
        n_w = 16 * (5 if rope else 4)
        ps = kn["ps"]
        block = ctx.enter_context(nc.Block())

        def tile_of(jb):
            gq, j = divmod(jb, NTL)
            kind, m = tiles[j]
            return gq, j, kind, m, rows_of[kind], jb % R

        n_stores = [NHQ if tiles[jb % NTL][0] == "g" else 1 for jb in range(NTB)]
        per_batch = [sum(n_stores[r::RP]) for r in range(RP)]

        def stored(eng, b, jb):
            before, jb = (0, jb) if jb >= 0 else (1, jb + NTB)
            rp = jb % RP
            upto = sum(n_stores[rp:jb + 1:RP])
            wait(eng, parts_out[rp], (b * per_batch[rp] + (per_batch[rp] * (1 - before) + upto)) * 16, ph.passed)

        def x_rows(b, gq):
            return x_d[bass.ds(b * T + gq * TG, TG), :].rearrange("(t p) d -> p t d", p=P)

        @block.sync
        def _(sp):
            for gq in range(GB):
                sp.dma_start(xs[:, gq], x_rows(0, gq)).then_inc(x_in[gq], 16)
                if gq == 0:
                    for name, t in [("wq", wq_s), ("wk", wk_s), ("wv", wv_s)]:
                        sp.dma_start(t[:], w[name]).then_inc(w_in, 16)
                    if rope:
                        sp.dma_start(cos_s[:], w["cos"]).then_inc(w_in, 16)
                        sp.dma_start(sin_s[:], w["sin"]).then_inc(w_in, 16)
                    else:
                        sp.dma_start(w12_s[:], w["w12"]).then_inc(w_in, 16)
            for r in range(RP):
                sp.sem_inc(parts_out[r], per_batch[r] * 16)
            v_out.start(sp)
            with sp.Fori(0, B) as b:
                for jb in range(NTB):
                    gq, j, kind, m, n, _ = tile_of(jb)
                    rp = jb % RP
                    low.wait(sp, b * NTB + jb)
                    cols = slice(gq * TG, (gq + 1) * TG)
                    if kind == "g":
                        for q in range(NHQ):
                            sp.dma_start(kn["g_d"][:, bass.ds((b * NHQ + q) * NF, NF), cols].rearrange("k r t -> r k t"),
                                         parts[0:n, rp]).then_inc(parts_out[rp], 16)
                    else:
                        row = b * P + m * (B * P) if rope else b * (H * NF if kind == "f" else D) + m * n
                        sp.dma_start(kn[f"{kind}_d"][:, bass.ds(row, n), cols].rearrange("k r t -> r k t"),
                                     parts[0:n, rp]).then_inc(parts_out[rp], 16)
                    if j == NTL - 1:
                        g = b * GB + gq
                        v_sb.wait(sp, g * 2 + 1)
                        for q in range(NHQ):
                            v_out.done(sp.dma_start(
                                kn["v_d"][bass.ds(b * NHQ + q, 1), :, gq * TT:(gq + 1) * TT, :].rearrange("o p k n -> (o p) k n"),
                                vs[:, gq % 2, :, q * HQ:(q + 1) * HQ, :].rearrange("p t h n -> p t (h n)")), gq % 2)
                        xt_ps.wait(sp, g * DC + DC - 1)
                        sp.dma_start(xs[:, gq], x_rows((b + 1) % B, gq)).then_inc(x_in[gq], 16)
            for jb in range(NTB - RP, NTB):
                stored(sp, B - 1, jb)
            for u in range(2):
                v_out.wait(sp, u, B * GB // 2 - 1)
            for gq in range(GB):
                sp.wait_ge(x_in[gq], 16 * (B + 1))

        @block.gpsimd
        def _(pool):
            for c in (low, rot):
                c.start(pool)
            with pool.Fori(0, B) as b:
                for s in range(NTB + L_LOW):
                    if rope and s < NTB:
                        gq, j, kind, m, n, r = tile_of(s)
                        J = b * NTB + s
                        mul.wait(pool, J)
                        rot.done(pool.tensor_tensor(qcos[:, r], qcos[:, r], qsin[:, r], ALU.subtract if m == 0 else ALU.add))
                    if s >= L_LOW:
                        gq, j, kind, m, n, r = tile_of(s - L_LOW)
                        mid.wait(pool, b * NTB + s - L_LOW)
                        rp = (s - L_LOW) % RP
                        low.done(pool.tensor_tensor(parts[0:n, rp, 2], rem[0:n, r], parts[0:n, rp, 1], ALU.subtract))
            if rope:
                pool.wait_ge(fold, B + 1)
                pool.partition_all_reduce(top[:, 2:4], top[:, 0:2], P, bass.bass_isa.ReduceOp.max).then_inc(flag, 1)

        @block.scalar
        def _(act):
            for c in (xt_sb, hi, v_sb, feat, sq):
                c.start(act)

            def v_half(b, gq, half):
                g = b * GB + gq
                v_ps.wait(act, g * 2 + half)
                if half == 0:
                    v_out.wait(act, gq % 2, b * (GB // 2) + gq // 2 - 1)
                v_sb.done(act.activation(vs[:, gq % 2, 2 * half:2 * half + 2, :, 0:HD],
                                         ps[:, VB].rearrange("p (t h d) -> p t h d", t=2, h=H), ACT.Copy))

            def x_t(b, gq):
                g = b * GB + gq
                v_ps.wait(act, (g - 2) * 2 + 1)
                for c in range(DC):
                    xt_ps.wait(act, g * DC + c)
                    xt_sb.done(act.activation(xt[:, gq % 2, c], ps[:, XT0 + c], ACT.Copy))

            def others(b, gq, j):
                if j in V_AT:
                    v_half(b, gq, V_AT.index(j))
                if j == V_AT[0]:
                    x_t(b, gq + 1)

            act.wait_ge(ones_set, 1)
            x_t(0, 0)
            with act.Fori(0, B) as b:
                for s in range(NTB + L_HI):
                    if rope and 1 <= s <= NTB:
                        others(b, *divmod(s - 1, NTL))
                    if s >= L_HI:
                        gq, j, kind, m, n, r = tile_of(s - L_HI)
                        J, g = b * NTB + s - L_HI, b * GB + gq
                        rp = (s - L_HI) % RP
                        stored(act, b, s - L_HI - RP)
                        if rope:
                            rot.wait(act, J)
                            hi.done(act.activation(parts[0:n, rp, 0], qcos[0:n, r], ACT.Copy))
                            norm.wait(act, b * (NTB // 2) + (s - L_HI - R) // 2)
                            sq.done(act.activation(sqr[:, r], qcos[:, r], ACT.Square))
                        elif kind == "g":
                            prj.wait(act, J)
                            feat.done(act.activation(f12[:, gq % 2], ps[0:NF, PRJ0 + r], ACT.Tanh))
                            feat.wait(act, g)
                            hi.done(act.activation(parts[0:n, rp, 0], f12[:, gq % 2], ACT.Copy))
                        else:
                            prj.wait(act, J)
                            hi.done(act.activation(parts[0:n, rp, 0], ps[0:n, PRJ0 + r], ACT.Copy))
                        if not rope:
                            others(b, gq, j)

        @block.tensor
        def _(pe):
            for c in (xt_ps, prj, v_ps, norm):
                c.start(pe)
            pe.wait_ge(w_in, n_w)

            def transposes(b, gq):
                g = b * GB + gq
                pe.wait_ge(x_in[gq % GB], 16 * (b + (gq // GB + 1)))
                for c in range(DC):
                    xt_sb.wait(pe, (g - 1) * DC + c)
                    for t in range(TT):
                        mm = pe.transpose(ps[:, XT0 + c, t * P:(t + 1) * P], xs[:, gq % GB, t, c * P:(c + 1) * P], kn["ident"][:])
                    xt_ps.done(mm)

            transposes(0, 0)
            with pe.Fori(0, B) as b:
                for s in range(NTB + L_NORM):
                    if s < NTB:
                        gq, j, kind, m, n, r = tile_of(s)
                        J, g, u = b * NTB + s, b * GB + gq, gq % 2
                        if j == 0:
                            xt_sb.wait(pe, g * DC + DC - 1)
                        if rope:
                            mul.wait(pe, J - R + 1 - m)
                        else:
                            rest.wait(pe, J - R)
                        if kind == "f":
                            feat.wait(pe, g)
                            mm = pe.matmul(ps[0:n, PRJ0 + r], kn["C"][:].rearrange("p h e -> p (h e)")[:, m * n:(m + 1) * n], f12[:, u], start=True, stop=True)
                        else:
                            for c in range(DC):
                                lhs = w12_s[:, c, :] if kind == "g" else (wq_s if kind == "q" else wk_s)[:, c, m * P:(m + 1) * P]
                                mm = pe.matmul(ps[0:n, PRJ0 + r], lhs, xt[:, u, c], start=c == 0, stop=c == DC - 1)
                        prj.done(mm)
                        if j in V_AT:
                            half = V_AT.index(j)
                            v_sb.wait(pe, g * 2 + half - 1)
                            for t in range(2 * half, 2 * half + 2):
                                for c in range(DC):
                                    mm = pe.matmul(ps[:, VB, (t % 2) * D:(t % 2 + 1) * D], xt[:, u, c, t * P:(t + 1) * P], wv_s[:, c, :], start=c == 0, stop=c == DC - 1)
                            v_ps.done(mm)
                            if half == 0:
                                transposes(b, gq + 1)
                    if rope and s >= L_NORM and s % 2 == 1:
                        pair = b * (NTB // 2) + (s - L_NORM) // 2
                        nmax.wait(pe, pair - 1)
                        sq.wait(pe, b * NTB + s - L_NORM + 1)
                        for m in range(2):
                            mm = pe.matmul(ps[:, NORM], kn["headsum"][:], sqr[:, (s - L_NORM + m) % R], start=m == 0, stop=m == 1)
                        norm.done(mm)

        @block.vector
        def _(dve):
            for c in (rest, mid, mul, nmax):
                c.start(dve)
            dve.memset(vs[:], 1.0).then_inc(ones_set, 1)
            if rope:
                dve.memset(top[:], 0.0).then_inc(fold, 1)
                dve.wait_ge(w_in, n_w)
            with dve.Fori(0, B) as b:
                for s in range(NTB + max(L_MID, L_NORM + 1)):
                    if rope and s < NTB and s % 2 == 1:
                        gq = s // NTL
                        cols = slice(gq * TG, (gq + 1) * TG)
                        prj.wait(dve, b * NTB + s)
                        for jb in (s - 1, s):
                            J, r, other = b * NTB + jb, jb % R, (jb ^ 1) % R
                            hi.wait(dve, J - R)
                            rest.wait(dve, J - R)
                            sq.wait(dve, J - R)
                            dve.tensor_tensor(qcos[:, r], ps[:, PRJ0 + r], cos_s[:, cols], ALU.mult)
                            mul.done(dve.tensor_tensor(qsin[:, r], ps[:, PRJ0 + other], sin_s[:, cols], ALU.mult))
                    if L_REST <= s < NTB + L_REST:
                        gq, j, kind, m, n, r = tile_of(s - L_REST)
                        J = b * NTB + s - L_REST
                        hi.wait(dve, J)
                        low.wait(dve, J - R)
                        src = qcos[:, r] if rope else f12[:, gq % 2] if kind == "g" else ps[0:n, PRJ0 + r]
                        rest.done(dve.tensor_tensor(rem[0:n, r], src, parts[0:n, (s - L_REST) % RP, 0], ALU.subtract))
                    if L_MID <= s < NTB + L_MID:
                        gq, j, kind, m, n, r = tile_of(s - L_MID)
                        rest.wait(dve, b * NTB + s - L_MID)
                        mid.done(dve.tensor_copy(parts[0:n, (s - L_MID) % RP, 1], rem[0:n, r]))
                    if rope and s > L_NORM and s % 2 == 0:
                        jb = s - 1 - L_NORM
                        gq, j, kind, *_ = tile_of(jb)
                        norm.wait(dve, b * (NTB // 2) + jb // 2)
                        nmax.done(dve.tensor_reduce(nrm[:, 0 if kind == "q" else 1, gq:gq + 1], ps[:, NORM], AX.X, ALU.max))
                if rope:
                    nmax.wait(dve, b * (NTB // 2) + NTB // 2 - 1)
                    dve.tensor_reduce(top[:, 4:6], nrm[:], AX.X, ALU.max).then_inc(ones_set, 1)
                    dve.wait_ge(ones_set, b + 2)
                    dve.wait_ge(fold, b + 1)
                    dve.tensor_tensor(top[:, 0:2], top[:, 0:2], top[:, 4:6], ALU.max).then_inc(fold, 1)
            if rope:
                dve.wait_ge(flag, 1)
                dve.tensor_tensor(top[:, 6:7], top[:, 2:3], top[:, 3:4], ALU.mult).then_inc(flag, 1)
                dve.wait_ge(flag, 2)
                dve.tensor_scalar(top[:, 7:8], top[:, 6:7], (BOUND * 4 / 1.05) ** 2, None, ALU.is_le).then_inc(flag, 1)
                dve.wait_ge(flag, 3)
                dve.tensor_scalar(kn["wide"][:, 1:2], top[:, 7:8], -1.0, 1.0, ALU.mult, ALU.add)


def load_stacks(eng, kn, layer, it, st, sem):
    n = 0

    def load(dst, src):
        nonlocal n
        eng.dma_start(dst, src).then_inc(sem, 16)
        n += 1

    nh = 1 if layer == 0 else 2
    hd = HD // nh
    for s in range(NS):
        for m in range(nh):
            r0 = s * HD + m * hd
            rows = bass.ds(it * HQ * hd + m * (B * H * hd), HQ * hd)
            load(st["q"][r0:r0 + hd], kn["q_d"][SLOTS_A[s], rows, :].rearrange("(h r) t -> r h t", r=hd))
            load(st["k"][r0:r0 + hd], kn["k_d"][SLOTS_B[s], rows, :].rearrange("(h r) t -> r h t", r=hd))
        if layer == 0:
            load(st["f"][s * NF:(s + 1) * NF], kn["f_d"][SLOTS_A[s], bass.ds(it * HQ * NF, HQ * NF), :].rearrange("(h r) t -> r h t", r=NF))
            load(st["g"][s * NF:(s + 1) * NF], kn["g_d"][SLOTS_B[s], bass.ds(it * NF, NF), :])
    return n


def attend_phase(nc, kn, layer):
    U = 2
    steps = [(g, kb) for g in range(GB) for kb in range((g + 1) * (TG // P))]
    NST = len(steps)
    body = [(u, s) for u in range(U) for s in range(NST)]
    NB = len(body)
    R = 4
    assert NB % R == 0
    LAG = 2 if layer == 0 else 1
    W = LAG + TG // P
    QK0, E0, O0 = 0, 4, 6
    RQ = 2 if layer == 0 else 3
    SR, FR = (QROWS, FROWS + 3) if layer == 0 else (QROWS + 3, 0)
    with ExitStack() as ctx:
        ph = Phase(nc, ctx, f"att{layer}")
        ones_in = ph.sem("ones_in")
        stacks_in = [ph.sem(f"stacks_in{u}") for u in range(U)]
        stacks_free = [ph.sem(f"stacks_free{u}") for u in range(U)]
        qk = ph.count("qk")
        th = ph.count("th")
        ex = ph.count("ex")
        sc = ph.count("sc")
        pr = ph.count("pr")
        pv = ph.count("pv")
        o_sb, l_ps, l_sb, o_n = (ph.count(n) for n in ("o_sb", "l_ps", "l_sb", "o_n"))
        o_out = ph.stores("o_out", 2, HQ)
        st = []
        for u in range(U):
            s = {"q": ph.sb(f"q{u}", [SR, HQ, T], BF16), "k": ph.sb(f"k{u}", [SR, HQ, T], BF16),
                 "v": ph.sb(f"v{u}", [P, KB, HQ * VW])}
            if layer == 0:
                s["f"], s["g"] = ph.sb(f"f{u}", [FR, HQ, T], BF16), ph.sb(f"g{u}", [FR, T], BF16)
            st.append(s)
        tanh_s = ph.sb("tanh", [P, 2, 2, TG]) if layer == 0 else None
        prob = ph.sb("prob", [P, R, HQ, TG])
        o_s, l_s, on_s = (ph.sb(n, [P, 2, TG]) for n in ("o", "l", "on"))
        ps = kn["ps"]
        N_LOAD = NS * 4 + 2
        block = ctx.enter_context(nc.Block())

        ring = [q % RQ for q in range(2 * NB)]
        if 2 * NB % RQ == 1:
            ring[-1] = 1

        def banks(q):
            return QK0 + 2 * ring[q % (2 * NB)]

        def had_banks(q):
            return next(x for x in range(q - 1, q - 2 * RQ, -1) if banks(x) == banks(q))

        def set_of(i, k):
            return (i + k // NB) * U + body[k % NB][0]

        def at(k):
            u, s = body[k % NB]
            g, kb = steps[s]
            r = kb - g * (TG // P)
            off = r * P if r > 0 else 0
            return u, s, g, kb, off, r >= 0, kb == (g + 1) * (TG // P) - 1

        @block.sync
        def _(sp):
            N_IT = B * NHQ

            def load(it, u):
                n = load_stacks(sp, kn, layer, it, st[u], stacks_in[u])
                shift = st[u]["f"][FROWS:FROWS + 3] if layer == 0 else st[u]["q"][QROWS:QROWS + 3]
                sp.dma_start(shift, kn["shift_d"][:, bass.ds(it * HQ, HQ), :]).then_inc(stacks_in[u], 16)
                sp.dma_start(st[u]["v"][:], kn["v_d"][bass.ds(it, 1)].rearrange("o p k n -> (o p) k n")).then_inc(stacks_in[u], 16)
                assert n + 2 == N_LOAD

            o_out.start(sp)
            for u in range(U):
                if layer == 0:
                    sp.dma_start(st[u]["g"][FROWS:FROWS + 3], kn["ones_d"][:, 0:T]).then_inc(ones_in, 16)
                else:
                    sp.dma_start(st[u]["k"][QROWS:QROWS + 3], kn["ones_d"].rearrange("p (h t) -> p h t", h=HQ)).then_inc(ones_in, 16)
            load(0, 0)
            with sp.Fori(0, N_IT // U) as i:
                for u in range(U):
                    it = i * U + u
                    wait(sp, stacks_free[1 - u], i + 1 + u, ph.passed)
                    load((it + 1) % N_IT, 1 - u)
                    for g in range(GB):
                        o_n.wait(sp, it * GB + g)
                        for h in range(HQ):
                            o_out.done(sp.dma_start(kn["o_d"][bass.ds(it * HQ * HD + h * HD, HD), g * TG:(g + 1) * TG], on_s[VW * h:VW * h + HD, g % 2]), g % 2)
            for u in range(2):
                o_out.wait(sp, u, B * NHQ * GB // 2 - 1)
            sp.wait_ge(stacks_in[0], 16 * N_LOAD * (N_IT // U + 1))

        @block.tensor
        def _(pe):
            for c in (qk, ex, pv, l_ps):
                c.start(pe)
            for u in range(U):
                pe.sem_inc(stacks_free[u], 1)
            pe.wait_ge(ones_in, 16 * U)

            def program(i):

                def scores(k, pair):
                    u, s, g, kb, off, diag, _ = at(k)
                    S = i * NB + k
                    (th if layer == 0 else pr).wait(pe, i * (2 * NB) + had_banks(2 * k + pair))
                    for h in (2 * pair, 2 * pair + 1):
                        bank = banks(2 * k + pair) + h % 2
                        out = ps[:, bank, off:TG]
                        mask = layer == 1 and diag
                        mm = pe.matmul(out, st[u]["k"][:, h, kb * P:(kb + 1) * P], st[u]["q"][:, h, g * TG + off:(g + 1) * TG], start=True, stop=not mask)
                        if mask:
                            mm = pe.matmul(ps[:, bank, off:off + P], kn["identb"][:], kn["mask_kq"][:], start=False, stop=True)
                    qk.done(mm)

                def extra(k, h):
                    u, s, g, kb, off, diag, _ = at(k)
                    S = i * NB + k
                    sc.wait(pe, S * HQ + h - 2)
                    mm = pe.matmul(ps[:, E0 + h % 2, off:TG], st[u]["g"][:, kb * P:(kb + 1) * P], st[u]["f"][:, h, g * TG + off:(g + 1) * TG], start=True, stop=not diag)
                    if diag:
                        mm = pe.matmul(ps[:, E0 + h % 2, off:off + P], kn["identb"][:], kn["mask_kq"][:], start=False, stop=True)
                    ex.done(mm)

                def weigh(k):
                    u, s, g, kb, off, diag, last = at(k)
                    S = i * NB + k
                    if layer == 0:
                        pr.wait(pe, S)
                    else:
                        pr.wait(pe, S * 2 + 1)
                    if kb == 0:
                        l_sb.wait(pe, set_of(i, k) * GB + g - 2)
                    for h in range(HQ):
                        mm = pe.matmul(ps[VW * h:VW * (h + 1), O0 + g % 2, off:TG], st[u]["v"][:, kb, h * VW:(h + 1) * VW], prob[:, k % R, h, off:TG], start=kb == 0, stop=last)
                    pv.done(mm)

                def row_sums(k):
                    u, s, g, *_ = at(k)
                    G = set_of(i, k) * GB + g
                    o_sb.wait(pe, G)
                    l_ps.done(pe.matmul(ps[:, O0 + g % 2], kn["pick"][:], o_s[:, g % 2], start=True, stop=True))

                def first_pair(k):
                    u, s, *_ = at(k)
                    if s == 0:
                        pe.wait_ge(stacks_in[u], (i + (k // NB + 1)) * (16 * N_LOAD))
                    scores(k, 0)

                def step(k):
                    if layer == 0:
                        scores(k, 1)
                        extra(k, 0)
                        extra(k, 1)
                    else:
                        first_pair(k + 1)
                    if k >= LAG:
                        weigh(k - LAG)
                    if k > LAG and at(k - LAG - 1)[-1]:
                        row_sums(k - LAG - 1)
                    if layer == 0:
                        first_pair(k + 1)
                        extra(k, 2)
                        extra(k, 3)
                    else:
                        scores(k + 1, 1)

                return first_pair, scores, step

            first_pair, scores, step = program(0)
            first_pair(0)
            if layer == 1:
                scores(0, 1)
            for k in range(W):
                step(k)
            with pe.Fori(0, B * NHQ // U) as i:
                *_, step = program(i)
                for k in range(W, NB + W):
                    step(k)

        @block.scalar
        def _(act):
            for c in (th, pr):
                c.start(act)
            def step(i, k):
                u, s, g, kb, off, *_ = at(k)
                S = i * NB + k
                for pair in range(2):
                    qk.wait(act, S * 2 + pair)
                    bank = banks(2 * k + pair)
                    src = ps[:, bank:bank + 2, off:TG]
                    if layer == 0:
                        sc.wait(act, (S - 1) * HQ + 2 * pair + 1)
                        th.done(act.activation(tanh_s[:, pair, :, off:TG], src, ACT.Tanh, scale=kn["rbeta"][:, 0:1]))
                    else:
                        pv.wait(act, S - R)
                        pr.done(act.activation(prob[:, k % R, 2 * pair:2 * pair + 2, off:TG], src, ACT.Exp, scale=float(HD) ** -0.5))
                if k > 0 and layer == 0:
                    u, s, g, kb, off, *_ = at(k - 1)
                    S = i * NB + k - 1
                    sc.wait(act, S * HQ + HQ - 1)
                    pr.done(act.activation(prob[:, (k - 1) % R, :, off:TG], prob[:, (k - 1) % R, :, off:TG], ACT.Exp))

            for k in range(W):
                step(0, k)
            with act.Fori(0, B * NHQ // U) as i:
                for k in range(W, NB + W):
                    step(i, k)

        @block.vector
        def _(dve):
            for c in (sc, o_sb, l_sb):
                c.start(dve)

            def invert(i, due, n):
                for k, part in due[:n]:
                    u, s, g, *_ = at(k)
                    G = set_of(i, k) * GB + g
                    cols = slice(part * TG // 4, (part + 1) * TG // 4)
                    if part == 0:
                        l_ps.wait(dve, G)
                        o_n.wait(dve, G - 2)
                    ins = dve.reciprocal(l_s[:, g % 2, cols], ps[:, O0 + g % 2, cols])
                    if part == 3:
                        l_sb.done(ins)
                del due[:n]

            def step(i, k, due):
                if k > LAG and at(k - LAG - 1)[-1]:
                    u, s, g, *_ = at(k - LAG - 1)
                    G = set_of(i, k - LAG - 1) * GB + g
                    pv.wait(dve, i * NB + k - LAG - 1)
                    o_n.wait(dve, G - 2)
                    o_sb.done(dve.tensor_copy(o_s[:, g % 2], ps[:, O0 + g % 2]))
                if k > LAG + 1 and at(k - LAG - 2)[-1]:
                    due += [(k - LAG - 2, part) for part in range(4)]
                if layer == 1:
                    invert(i, due, len(due))
                    return
                u, s, g, kb, off, *_ = at(k)
                S = i * NB + k
                pv.wait(dve, S - R)
                for h in range(HQ):
                    if h == 2:
                        invert(i, due, 2 if g <= 1 else 1)
                    th.wait(dve, S * 2 + h // 2)
                    ex.wait(dve, S * HQ + h)
                    sc.done(dve.scalar_tensor_tensor(prob[:, k % R, h, off:TG], tanh_s[:, h // 2, h % 2, off:TG], kn["alpha"][:, 0:1],
                                                     ps[:, E0 + h % 2, off:TG], ALU.mult, ALU.add))

            for k in range(W):
                step(0, k, [])
            with dve.Fori(0, B * NHQ // U) as i:
                due = []
                for k in range(W, NB + W):
                    step(i, k, due)
                assert not due

        @block.gpsimd
        def _(pool):
            o_n.start(pool)
            with pool.Fori(0, B * NHQ // U) as i:
                for u in range(U):
                    for g in range(GB):
                        it = i * U + u
                        G = it * GB + g
                        l_sb.wait(pool, G)
                        o_out.wait(pool, g % 2, it * (GB // 2) + g // 2 - 1)
                        o_n.done(pool.tensor_tensor(on_s[:, g % 2], o_s[:, g % 2], l_s[:, g % 2], ALU.mult))
                        if g == GB - 1:
                            pool.sem_inc(stacks_free[u], 1)


def row_max_phase(nc, kn, layer):
    SR, FR = QROWS, FROWS
    with ExitStack() as ctx:
        ph = Phase(nc, ctx, f"max{layer}")
        stacks_in, qk, th, sc, mx, nm, tp, out = (ph.sem(n) for n in ("stacks_in", "qk", "th", "sc", "mx", "nm", "tp", "out"))
        st = {"q": ph.sb("q", [SR, HQ, T], BF16), "k": ph.sb("k", [SR, HQ, T], BF16)}
        if layer == 0:
            st["f"], st["g"] = ph.sb("f", [FR, HQ, T], BF16), ph.sb("g", [FR, T], BF16)
        tanh_s = ph.sb("tanh", [P, TG])
        score = ph.sb("score", [P, TG])
        cmax = ph.sb("cmax", [P, GB])
        nmax = ph.sb("nmax", [P, HQ * KB])
        parts = ph.sb("parts", [HQ * KB, 3, P], BF16)
        rem = ph.sb("rem", [HQ * KB, P])
        flag = ph.sb("flag", [P, 1], I32)
        flagged = ph.sem("flagged")
        ps = kn["ps"]
        N_LOAD = NS * 4
        chunks = [(h, qb, c, min(TG, (qb + 1) * P - c * TG)) for h in range(HQ) for qb in range(KB) for c in range(qb // (TG // P) + 1)]
        NCH = len(chunks)
        NQB = HQ * KB
        with nc.Block() as block:
            @block.vector
            def _(dve):
                dve.tensor_copy(flag[:], kn["wide"][:, layer:layer + 1]).then_inc(flagged, 1)
                dve.wait_ge(flagged, 1)
        block = ctx.enter_context(nc.Block())

        @block.sync
        def _(sp):
            wide = sp.value_load(flag[0:1, 0:1], min_val=0, max_val=1)
            with sp.If(wide == 1):
                with sp.Fori(0, B * NHQ) as it:
                    wait(sp, nm, it + 1, ph.passed)
                    load_stacks(sp, kn, layer, it, st, stacks_in)
                    wait(sp, tp, it * 5 + 5, ph.passed)
                    sp.dma_start(kn["shift_d"][:, bass.ds(it * HQ, HQ), :].rearrange("k h (q p) -> (h q) k p", p=P), parts[:]).then_inc(out, 16)
                    wait(sp, out, (it + 1) * 16, ph.passed)
            sp.nop()

        @block.tensor
        def _(pe):
            wide = pe.value_load(flag[0:1, 0:1], min_val=0, max_val=1)
            with pe.If(wide == 1):
                with pe.Fori(0, B * NHQ) as it:
                    pe.wait_ge(stacks_in, (it + 1) * (16 * N_LOAD))
                    for n, (h, qb, c, w) in enumerate(chunks):
                        pe.wait_ge(mx, it * NCH + n + 1)
                        diag = c == qb // (TG // P)
                        if layer == 1:
                            mm = pe.matmul(ps[:, 0, 0:w], st["q"][:, h, qb * P:(qb + 1) * P], st["k"][:, h, c * TG:c * TG + w], start=True, stop=not diag)
                            if diag:
                                mm = pe.matmul(ps[:, 0, w - P:w], kn["identb"][:], kn["mask_qk"][:], start=False, stop=True)
                        else:
                            pe.matmul(ps[:, 1, 0:w], st["f"][:, h, qb * P:(qb + 1) * P], st["g"][:, c * TG:c * TG + w], start=True, stop=not diag)
                            if diag:
                                pe.matmul(ps[:, 1, w - P:w], kn["identb"][:], kn["mask_qk"][:], start=False, stop=True)
                            mm = pe.matmul(ps[:, 0, 0:w], st["q"][:, h, qb * P:(qb + 1) * P], st["k"][:, h, c * TG:c * TG + w], start=True, stop=True)
                        mm.then_inc(qk, 1)
                    wait(pe, nm, it + 2, ph.passed, apart=True)
                    pe.transpose(ps[0:NQB, 2, 0:P], nmax[:], kn["ident"][:]).then_inc(tp, 1)
            pe.nop()

        @block.scalar
        def _(act):
            wide = act.value_load(flag[0:1, 0:1], min_val=0, max_val=1)
            with act.If(wide == 1):
                if layer == 0:
                    with act.Fori(0, B * NHQ) as it:
                        for n, (h, qb, c, w) in enumerate(chunks):
                            act.wait_ge(qk, it * NCH + n + 1)
                            act.activation(tanh_s[:, 0:w], ps[:, 0, 0:w], ACT.Tanh, scale=kn["rbeta"][:, 0:1]).then_inc(th, 1)
                else:
                    act.nop()
            act.nop()

        @block.vector
        def _(dve):
            wide = dve.value_load(flag[0:1, 0:1], min_val=0, max_val=1)
            with dve.If(wide == 1):
                dve.sem_inc(mx, 1)
                dve.sem_inc(nm, 1)
                with dve.Fori(0, B * NHQ) as it:
                    n_row = 0
                    for n, (h, qb, c, w) in enumerate(chunks):
                        if layer == 0:
                            dve.wait_ge(th, it * NCH + n + 1)
                            dve.scalar_tensor_tensor(score[:, 0:w], tanh_s[:, 0:w], kn["alpha"][:, 0:1], ps[:, 1, 0:w], ALU.mult, ALU.add).then_inc(sc, 1)
                            dve.wait_ge(sc, it * (NCH + NQB) + n_row + n + 1)
                            src = score[:, 0:w]
                        else:
                            dve.wait_ge(qk, it * NCH + n + 1)
                            src = ps[:, 0, 0:w]
                        dve.tensor_reduce(cmax[:, c:c + 1], src, AX.X, ALU.max).then_inc(mx, 1)
                        dve.wait_ge(mx, it * NCH + n + 2)
                        if c == qb // (TG // P):
                            row = h * KB + qb
                            dve.tensor_reduce(nmax[:, row:row + 1], cmax[:, 0:c + 1], AX.X, ALU.max).then_inc(sc, 1)
                            n_row += 1
                            dve.wait_ge(sc, it * ((NCH if layer == 0 else 0) + NQB) + n_row + (n + 1 if layer == 0 else 0))
                    dve.tensor_scalar(nmax[:], nmax[:], -1.0, None, ALU.mult).then_inc(nm, 1)
                    dve.wait_ge(tp, it * 5 + 1)
                    ptile = ps[0:NQB, 2, 0:P]
                    dve.tensor_copy(parts[:, 0], ptile).then_inc(tp, 1)
                    dve.wait_ge(tp, it * 5 + 2)
                    dve.tensor_tensor(rem[:], ptile, parts[:, 0], ALU.subtract).then_inc(tp, 1)
                    dve.wait_ge(tp, it * 5 + 3)
                    dve.tensor_copy(parts[:, 1], rem[:]).then_inc(tp, 1)
                    dve.wait_ge(tp, it * 5 + 4)
                    dve.tensor_tensor(parts[:, 2], rem[:], parts[:, 1], ALU.subtract).then_inc(tp, 1)
            dve.nop()


class Norm:

    def __init__(self, ph, name, slots=2):
        self.slots = slots
        self.st = ph.sb(f"{name}_st", [P, slots, TT, 6])
        self.mv = ph.sb(f"{name}_mv", [P, slots, TT, 2])
        self.sd = ph.sb(f"{name}_sd", [P, slots, TT])
        self.rs = ph.sb(f"{name}_rs", [P, slots, TT])
        self.nb = ph.sb(f"{name}_nb", [P, slots, TT])
        self.stats, self.agg, self.root, self.inv, self.shift, self.out = (
            ph.count(f"{name}_{n}") for n in ("stats", "agg", "root", "inv", "shift", "out"))

    def start(self, dve=None, act=None):
        for eng, counts in ((dve, (self.stats, self.agg, self.inv, self.shift, self.out)), (act, (self.root,))):
            if eng is not None:
                for c in counts:
                    c.start(eng)

    def take(self, dve, g, u, rows, wait_row):
        self.out.wait(dve, g - self.slots)
        for t in range(TT):
            wait_row(t)
            ins = dve.bn_stats(self.st[:, u, t], rows(t))
        self.stats.done(ins)
        self.stats.wait(dve, g, apart=True)
        for t in range(TT):
            ins = dve.bn_aggr(self.mv[:, u, t], self.st[:, u, t])
        self.agg.done(ins)

    def take_root(self, act, g, u, eps):
        self.agg.wait(act, g)
        self.root.done(act.activation(self.sd[:, u], self.mv[:, u, :, 1], ACT.Sqrt, bias=eps))

    def invert(self, dve, g, u):
        self.root.wait(dve, g)
        self.inv.done(dve.reciprocal(self.rs[:, u], self.sd[:, u]))
        self.inv.wait(dve, g)
        self.shift.done(dve.scalar_tensor_tensor(self.nb[:, u], self.mv[:, u, :, 0], -1.0, self.rs[:, u], ALU.mult, ALU.mult))

    def apply(self, dve, g, u, dst, src):
        self.shift.wait(dve, g)
        for t in range(TT):
            ins = dve.tensor_scalar(dst(t), src(t), self.rs[:, u, t:t + 1], self.nb[:, u, t:t + 1], ALU.mult, ALU.add)
        self.out.done(ins)


def over_groups(eng, order, do):
    ahead = 3

    def groups(i, at, inside):
        for step in order:
            n = at - int(step[0])
            if inside(n):
                do(step[1:], i + n // GB, n % GB, i * GB + n)

    for at in range(ahead):
        groups(0, at, lambda n: n >= 0)
    with eng.Fori(0, B - 1) as i:
        for at in range(ahead, ahead + GB):
            groups(i, at, lambda n: True)
    for at in range(ahead, ahead + GB):
        groups(B - 1, at, lambda n: n < GB)


def post0_phase(nc, kn, w, x_d, out_d):
    Y1, XT0, Y2 = 0, 2, 4
    with ExitStack() as ctx:
        ph = Phase(nc, ctx, "post0")
        w_in, o_in, x_in = ph.sem("w_in"), [ph.sem(f"o_in{i}") for i in range(GB)], [ph.sem(f"x_in{i}") for i in range(GB)]
        y1, r1, y2, r2 = (ph.count(n) for n in ("y1", "r1", "y2", "r2"))
        xt_ps, xt_sb = ph.count("xt_ps"), ph.count("xt_sb")
        ab_ps, w_ffn = ph.sem("ab_ps"), ph.sem("w_ffn")
        xb = ph.count("xb")
        out = ph.stores("out_dma", 2)
        n1, n2 = Norm(ph, "n1"), Norm(ph, "n2")
        wo = ph.sb("wo", [P, DC, D])
        a_s = ph.sb("a", [16, D])
        b_s = ph.sb("b", [16, D])
        wf = ph.sb("wf", [P, DC, D])
        bias = ph.sb("bias", [P, D])
        o_s = ph.sb("o", [P, GB, DC, TG])
        xs = ph.sb("x", [P, GB, TT, D])
        rr = ph.sb("rr", [P, 2, TT, D])
        x1 = ph.sb("x1", [P, 2, TT, D])
        x1b = ph.sb("x1b", [P, 2, TT, D])
        xt = ph.sb("xt", [P, 2, DC, TG])
        rr2 = ph.sb("rr2", [P, 2, TT, D])
        x2 = ph.sb("x2", [P, 2, TT, D])
        ps = kn["ps"]
        block = ctx.enter_context(nc.Block())

        def rows(d, b, gq):
            return d[bass.ds(b * T + gq * TG, TG), :].rearrange("(t p) d -> p t d", p=P)

        def load(sp, b, gq):
            sp.dma_start(o_s[:, gq], kn["o_d"][bass.ds(b * D, D), gq * TG:(gq + 1) * TG].rearrange("(c p) t -> p c t", p=P)).then_inc(o_in[gq], 16)
            sp.dma_start(xs[:, gq], rows(x_d, b, gq)).then_inc(x_in[gq], 16)

        @block.sync
        def _(sp):
            for dst, src in ((wo, w["wo"]), (a_s, w["a"]), (b_s, w["b"]), (bias, w["bias"])):
                sp.dma_start(dst[:], src).then_inc(w_in, 16)
            for gq in range(GB):
                load(sp, 0, gq)
            out.start(sp)

            def do(step, b, gq, g):
                if step == "load":
                    r1.wait(sp, g * 2 + 1)
                    load(sp, (b + 1) % B, gq)
                else:
                    n2.out.wait(sp, g)
                    out.done(sp.dma_start(rows(out_d, b, gq), x2[:, gq % 2]), gq % 2)

            over_groups(sp, ("0load", "3store"), do)
            for u in range(2):
                out.wait(sp, u, B * GB // 2 - 1)
            for gq in range(GB):
                sp.wait_ge(x_in[gq], 16 * (B + 1))
                sp.wait_ge(o_in[gq], 16 * (B + 1))

        @block.tensor
        def _(pe):
            for c in (y1, xt_ps, y2):
                c.start(pe)
            pe.wait_ge(w_in, 64)
            for c in range(DC):
                pe.matmul(ps[:, Y2 + c, 0:D], a_s[:, c * P:(c + 1) * P], b_s[:], start=True, stop=True).then_inc(ab_ps, 1)
            pe.wait_ge(w_ffn, DC)
            def do(step, b, gq, g):
                u = gq % 2
                if step == "o":
                    pe.wait_ge(o_in[gq], 16 * (b + 1))
                    for half in range(2):
                        r1.wait(pe, (g - 1) * 2 + half)
                        for t in range(2 * half, 2 * half + 2):
                            for c in range(DC):
                                mm = pe.matmul(ps[:, Y1 + half, (t % 2) * D:(t % 2 + 1) * D], o_s[:, gq, c, t * P:(t + 1) * P], wo[:, c, :], start=c == 0, stop=c == DC - 1)
                        y1.done(mm)
                elif step == "xt":
                    n1.out.wait(pe, g)
                    for c in range(DC):
                        xt_sb.wait(pe, (g - 1) * DC + c)
                        for t in range(TT):
                            mm = pe.transpose(ps[:, XT0 + c, t * P:(t + 1) * P], x1[:, u, t, c * P:(c + 1) * P], kn["ident"][:])
                        xt_ps.done(mm)
                else:
                    xt_sb.wait(pe, g * DC + DC - 1)
                    for half in range(2):
                        r2.wait(pe, (g - 1) * 2 + half)
                        for t in range(2 * half, 2 * half + 2):
                            y = ps[:, Y2 + half, (t % 2) * D:(t % 2 + 1) * D]
                            for c in range(DC):
                                mm = pe.matmul(y, xt[:, u, c, t * P:(t + 1) * P], wf[:, c, :], start=c == 0, stop=c == DC - 1)
                        y2.done(mm)

            over_groups(pe, ("0o", "1xt", "2ffn"), do)

        @block.scalar
        def _(act):
            xt_sb.start(act)
            n1.start(act=act)
            n2.start(act=act)
            def do(step, b, gq, g):
                u = gq % 2
                if step == "xt":
                    for c in range(DC):
                        xt_ps.wait(act, g * DC + c)
                        y2.wait(act, (g - 2) * 2 + 1)
                        xt_sb.done(act.activation(xt[:, u, c], ps[:, XT0 + c], ACT.Copy))
                elif step == "root1":
                    n1.take_root(act, g, u, kn["eps"][:, 0:1])
                else:
                    n2.take_root(act, g, u, kn["eps"][:, 0:1])

            over_groups(act, ("1xt", "0root1", "2root2"), do)

        @block.vector
        def _(dve):
            for c in (r1, r2):
                c.start(dve)
            n1.start(dve=dve)
            n2.start(dve=dve)
            dve.wait_ge(w_in, 64)
            for c in range(DC):
                dve.wait_ge(ab_ps, c + 1)
                dve.tensor_tensor(wf[:, c], ps[:, Y2 + c, 0:D], kn["w4"][:, c], ALU.add).then_inc(w_ffn, 1)
            def do(step, b, gq, g):
                u = gq % 2
                if step == "sum1":
                    dve.wait_ge(x_in[gq], 16 * (b + 1))
                    for half in range(2):
                        y1.wait(dve, g * 2 + half)
                        ts = slice(2 * half, 2 * half + 2)
                        r1.done(dve.tensor_tensor(rr[:, u, ts], ps[:, Y1 + half].rearrange("p (t d) -> p t d", t=2), xs[:, gq, ts], ALU.add))
                    n1.take(dve, g, u, lambda t: rr[:, u, t], lambda t: r1.wait(dve, g * 2 + t // 2))
                elif step == "norm1":
                    n1.invert(dve, g, u)
                    xt_ps.wait(dve, (g - 2) * DC + DC - 1)
                    xb.wait(dve, g - 2)
                    n1.apply(dve, g, u, lambda t: x1[:, u, t], lambda t: rr[:, u, t])
                elif step == "sum2":
                    xb.wait(dve, g)
                    for half in range(2):
                        y2.wait(dve, g * 2 + half)
                        ts = slice(2 * half, 2 * half + 2)
                        r2.done(dve.tensor_tensor(rr2[:, u, ts], ps[:, Y2 + half].rearrange("p (t d) -> p t d", t=2), x1b[:, u, ts], ALU.add))
                    n2.take(dve, g, u, lambda t: rr2[:, u, t], lambda t: r2.wait(dve, g * 2 + t // 2))
                else:
                    n2.invert(dve, g, u)
                    out.wait(dve, u, b * (GB // 2) + gq // 2 - 1)
                    n2.apply(dve, g, u, lambda t: x2[:, u, t], lambda t: rr2[:, u, t])

            over_groups(dve, ("1norm1", "3norm2", "0sum1", "2sum2"), do)

        @block.gpsimd
        def _(pool):
            xb.start(pool)
            pool.wait_ge(w_in, 64)
            def do(step, b, gq, g):
                u = gq % 2
                n1.out.wait(pool, g)
                r2.wait(pool, (g - 2) * 2 + 1)
                for t in range(TT):
                    ins = pool.tensor_tensor(x1b[:, u, t], x1[:, u, t], bias[:], ALU.add)
                xb.done(ins)

            over_groups(pool, ("1bias",), do)

def post1_phase(nc, kn, w, x_d, out_d):
    Y1, XT0, RB, KV = 0, 2, 4, 6
    with ExitStack() as ctx:
        ph = Phase(nc, ctx, "post1")
        w_in, o_in, x_in = ph.sem("w_in"), [ph.sem(f"o_in{i}") for i in range(GB)], [ph.sem(f"x_in{i}") for i in range(GB)]
        y1, r1 = ph.count("y1"), ph.count("r1")
        xt_ps, xt_sb, edge = ph.count("xt_ps"), ph.count("xt_sb"), ph.count("edge")
        pr_, pk_, mr_, mk_ = (ph.count(n) for n in ("pr", "pk", "mr", "mk"))
        k_ps, k_re, k_sq = (ph.count(n) for n in ("k_ps", "k_re", "k_sq"))
        r_ps, r_sg, v_ps, rv, r2 = (ph.count(n) for n in ("r_ps", "r_sg", "v_ps", "rv", "r2"))
        omitted = ph.sem("one_minus")
        out = ph.stores("out_dma", 2)
        n1, n2 = Norm(ph, "n1"), Norm(ph, "n2")
        wo, wr, wk, wv = (ph.sb(n, [P, DC, D]) for n in ("wo", "wr", "wk", "wv"))
        mu = ph.sb("mu", [P, 2, DC])
        om = ph.sb("om", [P, 2, DC])
        o_s = ph.sb("o", [P, GB, DC, TG])
        xs = ph.sb("x", [P, GB, TT, D])
        rr = ph.sb("rr", [P, 2, TT, D])
        x3 = ph.sb("x3", [P, GB, TT, D])
        xt = ph.sb("xt", [P, 2, DC, TG + 1])
        prev = ph.sb("prev", [P, 2, DC, TG])
        mix = ph.sb("mix", [P, 2, 2, DC, TG])
        kr = ph.sb("kr", [P, DC, TG])
        ka = ph.sb("ka", [P, 2, DC, TG])
        sg = ph.sb("sg", [P, 2, TT, D])
        rr2 = ph.sb("rr2", [P, 2, TT, D])
        x4 = ph.sb("x4", [P, 2, TT, D])
        ps = kn["ps"]
        block = ctx.enter_context(nc.Block())

        def rows(d, b, gq):
            return d[bass.ds(b * T + gq * TG, TG), :].rearrange("(t p) d -> p t d", p=P)

        def load(sp, b, gq):
            sp.dma_start(o_s[:, gq], kn["o_d"][bass.ds(b * D, D), gq * TG:(gq + 1) * TG].rearrange("(c p) t -> p c t", p=P)).then_inc(o_in[gq], 16)
            sp.dma_start(xs[:, gq], rows(x_d, b, gq)).then_inc(x_in[gq], 16)

        @block.sync
        def _(sp):
            for dst, src in ((wo, w["wo"]), (wr, w["wr"]), (wk, w["wk"]), (wv, w["wv"]), (mu, w["mu"])):
                sp.dma_start(dst[:], src).then_inc(w_in, 16)
            for gq in range(GB):
                load(sp, 0, gq)
            out.start(sp)

            def do(step, b, gq, g):
                if step == "load":
                    r1.wait(sp, g * 2 + 1)
                    load(sp, (b + 1) % B, gq)
                else:
                    n2.out.wait(sp, g)
                    out.done(sp.dma_start(rows(out_d, b, gq), x4[:, gq % 2]), gq % 2)

            over_groups(sp, ("0load", "3store"), do)
            for u in range(2):
                out.wait(sp, u, B * GB // 2 - 1)
            for gq in range(GB):
                sp.wait_ge(x_in[gq], 16 * (B + 1))
                sp.wait_ge(o_in[gq], 16 * (B + 1))

        @block.tensor
        def _(pe):
            for c in (y1, xt_ps, k_ps, r_ps, v_ps):
                c.start(pe)
            pe.wait_ge(w_in, 80)

            def token_rows(bank, lhs, rhs):
                for t in range(2):
                    for c in range(DC):
                        mm = pe.matmul(ps[:, bank, t * D:(t + 1) * D], lhs(t, c), rhs[:, c, :], start=c == 0, stop=c == DC - 1)
                return mm

            def do(step, b, gq, g):
                u = gq % 2
                if step == "kr":
                    mk_.wait(pe, g * DC + DC - 1)
                    for m in range(DC):
                        rv.wait(pe, (g - 1) * 2 + m)
                        for c in range(DC):
                            mm = pe.matmul(ps[:, KV + m], wk[:, c, m * P:(m + 1) * P], mix[:, u, 1, c], start=c == 0, stop=c == DC - 1)
                        k_ps.done(mm)
                    mr_.wait(pe, g * DC + DC - 1)
                    for half in range(2):
                        r_sg.wait(pe, (g - 1) * 2 + half)
                        r_ps.done(token_rows(RB + half, lambda t, c: mix[:, u, 0, c, (2 * half + t) * P:(2 * half + t + 1) * P], wr))
                elif step == "xt":
                    n1.out.wait(pe, g)
                    for c in range(DC):
                        xt_sb.wait(pe, (g - 1) * DC + c)
                        for t in range(TT):
                            mm = pe.transpose(ps[:, XT0 + c, t * P:(t + 1) * P], x3[:, gq, t, c * P:(c + 1) * P], kn["ident"][:])
                        xt_ps.done(mm)
                elif step == "y":
                    pe.wait_ge(o_in[gq], 16 * (b + 1))
                    for half in range(2):
                        r1.wait(pe, (g - 1) * 2 + half)
                        y1.done(token_rows(Y1 + half, lambda t, c: o_s[:, gq, c, (2 * half + t) * P:(2 * half + t + 1) * P], wo))
                else:
                    k_sq.wait(pe, g * DC + DC - 1)
                    for half in range(2):
                        v_ps.done(token_rows(KV + half, lambda t, c: ka[:, u, c, (2 * half + t) * P:(2 * half + t + 1) * P], wv))

            over_groups(pe, ("2kr", "1xt", "0y", "2v"), do)

        @block.scalar
        def _(act):
            for c in (xt_sb, k_re, r_sg):
                c.start(act)
            n1.start(act=act)
            n2.start(act=act)
            def do(step, b, gq, g):
                u = gq % 2
                if step == "root1":
                    n1.take_root(act, g, u, kn["eps"][:, 0:1])
                elif step == "xt":
                    mr_.wait(act, (g - 2) * DC + DC - 1)
                    mk_.wait(act, (g - 2) * DC + DC - 1)
                    edge.wait(act, g - 1)
                    for c in range(DC):
                        xt_ps.wait(act, g * DC + c)
                        xt_sb.done(act.activation(xt[:, u, c, 1:TG + 1], ps[:, XT0 + c], ACT.Copy))
                elif step == "relu":
                    for m in range(DC):
                        k_ps.wait(act, g * DC + m)
                        k_sq.wait(act, (g - 1) * DC + m)
                        k_re.done(act.activation(kr[:, m], ps[:, KV + m], ACT.Relu))
                elif step == "sigmoid":
                    for half in range(2):
                        r_ps.wait(act, g * 2 + half)
                        rv.wait(act, (g - 2) * 2 + half)
                        r_sg.done(act.activation(sg[:, u, 2 * half:2 * half + 2], ps[:, RB + half].rearrange("p (t d) -> p t d", t=2), ACT.Sigmoid))
                else:
                    n2.take_root(act, g, u, kn["eps"][:, 0:1])

            over_groups(act, ("2relu", "3root", "2sigmoid", "1xt", "0root1"), do)

        @block.vector
        def _(dve):
            for c in (r1, rv, r2, edge, mr_, mk_):
                c.start(dve)
            n1.start(dve=dve)
            n2.start(dve=dve)
            dve.wait_ge(w_in, 80)
            dve.tensor_scalar(om[:], mu[:], -1.0, 1.0, ALU.mult, ALU.add).then_inc(omitted, 1)
            def do(step, b, gq, g):
                u = gq % 2
                if step == "sum1":
                    dve.wait_ge(x_in[gq], 16 * (b + 1))
                    for half in range(2):
                        y1.wait(dve, g * 2 + half)
                        ts = slice(2 * half, 2 * half + 2)
                        r1.done(dve.tensor_tensor(rr[:, u, ts], ps[:, Y1 + half].rearrange("p (t d) -> p t d", t=2), xs[:, gq, ts], ALU.add))
                    n1.take(dve, g, u, lambda t: rr[:, u, t], lambda t: r1.wait(dve, g * 2 + t // 2))
                elif step == "norm1":
                    n1.invert(dve, g, u)
                    r2.wait(dve, (g - GB) * 2 + 1)
                    n1.apply(dve, g, u, lambda t: x3[:, gq, t], lambda t: rr[:, u, t])
                elif step == "mix":
                    pr_.wait(dve, (g - 2) * DC + DC - 1)
                    pk_.wait(dve, (g - 2) * DC + DC - 1)
                    if gq == 0:
                        ins = dve.memset(xt[:, u, :, 0:1], 0.0)
                    else:
                        xt_sb.wait(dve, g * DC - 1)
                        ins = dve.tensor_copy(xt[:, u, :, 0:1], xt[:, 1 - u, :, TG:TG + 1])
                    edge.done(ins)
                    for c in range(DC):
                        xt_sb.wait(dve, g * DC + c)
                        pk_.wait(dve, g * DC + c)
                        k_ps.wait(dve, (g - 2) * DC + DC - 1)
                        mk_.done(dve.scalar_tensor_tensor(mix[:, u, 1, c], xt[:, u, c, 1:TG + 1], mu[:, 1, c:c + 1], prev[:, 1, c], ALU.mult, ALU.add))
                    for c in range(DC):
                        pr_.wait(dve, g * DC + c)
                        r_ps.wait(dve, (g - 2) * 2 + 1)
                        mr_.done(dve.scalar_tensor_tensor(mix[:, u, 0, c], xt[:, u, c, 1:TG + 1], mu[:, 0, c:c + 1], prev[:, 0, c], ALU.mult, ALU.add))
                elif step == "sum2":
                    for half in range(2):
                        ts = slice(2 * half, 2 * half + 2)
                        v_ps.wait(dve, g * 2 + half)
                        r_sg.wait(dve, g * 2 + half)
                        rv.done(dve.tensor_tensor(rr2[:, u, ts], ps[:, KV + half].rearrange("p (t d) -> p t d", t=2), sg[:, u, ts], ALU.mult))
                        rv.wait(dve, g * 2 + half)
                        r2.done(dve.tensor_tensor(rr2[:, u, ts], rr2[:, u, ts], x3[:, gq, ts], ALU.add))
                    n2.take(dve, g, u, lambda t: rr2[:, u, t], lambda t: r2.wait(dve, g * 2 + t // 2))
                else:
                    n2.invert(dve, g, u)
                    out.wait(dve, u, b * (GB // 2) + gq // 2 - 1)
                    n2.apply(dve, g, u, lambda t: x4[:, u, t], lambda t: rr2[:, u, t])

            over_groups(dve, ("3sum2", "1norm1", "3norm2", "1mix", "0sum1"), do)

        @block.gpsimd
        def _(pool):
            for c in (pr_, pk_, k_sq):
                c.start(pool)
            pool.wait_ge(omitted, 1)
            def do(step, b, gq, g):
                u = gq % 2
                if step == "prev":
                    edge.wait(pool, g)
                    for which, cnt, mixed in ((1, pk_, mk_), (0, pr_, mr_)):
                        for c in range(DC):
                            xt_sb.wait(pool, g * DC + c)
                            mixed.wait(pool, (g - 1) * DC + c)
                            cnt.done(pool.tensor_scalar(prev[:, which, c], xt[:, u, c, 0:TG], om[:, which, c:c + 1], 0.0, ALU.mult, ALU.add))
                else:
                    for m in range(DC):
                        k_re.wait(pool, g * DC + m)
                        v_ps.wait(pool, (g - 2) * 2 + 1)
                        k_sq.done(pool.tensor_tensor(ka[:, u, m], kr[:, m], kr[:, m], ALU.mult))

            over_groups(pool, ("2square", "1prev"), do)

def two_blocks(nc, a, out):
    with ExitStack() as ctx:
        def sb(name, shape, dt=F32):
            return ctx.enter_context(nc.sbuf_tensor(name, shape, dt))

        def dram(name, shape, dt=F32):
            return nc.dram_tensor(name, shape, dt, kind="Internal").ap()

        kn = {
            "ps": ctx.enter_context(nc.psum_tensor("ps", [P, 8, TG], F32)),
            "ident": sb("ident", [P, P]), "ones": sb("ones", [P, P]), 
            "pick": sb("pick", [P, P]), "identb": sb("identb", [P, P], BF16), "headsum": sb("headsum", [P, P], BF16),
            "mask_kq": sb("mask_kq", [P, P], BF16), "mask_qk": sb("mask_qk", [P, P], BF16),
            "C": sb("C", [NF, H, NF]), "w4": sb("w4", [P, DC, D]),
            "alpha": sb("alpha", [P, 1]), "rbeta": sb("rbeta", [P, 1]), "wide": sb("wide", [P, 2]), "eps": sb("eps", [P, 1]),
            "q_d": dram("q_parts", [3, B * D, T], BF16), "k_d": dram("k_parts", [3, B * D, T], BF16),
            "f_d": dram("f_parts", [3, B * H * NF, T], BF16), "g_d": dram("g_parts", [3, B * NHQ * NF, T], BF16),
            "v_d": dram("v_ones", [B * NHQ, P, KB, HQ * VW]), "shift_d": dram("shift", [3, B * H, T], BF16),
            "ones_d": a["ones_rows"], "o_d": dram("o_t", [B * D, T]), "x2_d": dram("x2", [B * T, D]),
        }
        const_in, made = ctx.enter_context(nc.semaphore("const_in")), ctx.enter_context(nc.semaphore("made"))

        def chunked(ap):
            return ap.rearrange("(c p) n -> p c n", p=P)

        with nc.Block() as block:
            @block.sync
            def _(sp):
                for i, name in enumerate(("ident", "ones", "pick")):
                    sp.dma_start(kn[name][:], a["consts"][i]).then_inc(const_in, 16)
                for i, name in enumerate(("identb", "headsum", "mask_kq", "mask_qk")):
                    sp.dma_start(kn[name][:], a["constsb"][i]).then_inc(const_in, 16)
                sp.wait_ge(const_in, 16 * 7)

            @block.vector
            def _(dve):
                dve.memset(kn["eps"][:], EPS).then_inc(made, 1)
                dve.memset(kn["wide"][:], 0.0).then_inc(made, 1)

        setup_phase(nc, kn, {"tw": a["tw"], "tr": a["L0_attn_transforms"], "kernel0": chunked(a["L0_ffn_kernel"]), "scalars": a["scalars"]})
        x0 = a["L0_attn_x"]
        project_phase(nc, kn, 0, {"wq": chunked(a["wq0"]), "wk": chunked(a["wk0"]), "wv": chunked(a["wv0"]), "w12": chunked(a["w12"])}, x0)
        row_max_phase(nc, kn, 0)
        attend_phase(nc, kn, 0)
        post0_phase(nc, kn, {"wo": chunked(a["wo0"]), "a": a["ffn_a_t"], "b": a["L0_ffn_b"], "bias": a["bias"]}, x0, kn["x2_d"])
        project_phase(nc, kn, 1, {"wq": chunked(a["wq1"]), "wk": chunked(a["wk1"]), "wv": chunked(a["wv1"]), "cos": a["cos"], "sin": a["sin"]}, kn["x2_d"])
        row_max_phase(nc, kn, 1)
        attend_phase(nc, kn, 1)
        post1_phase(nc, kn, {"wo": chunked(a["wo1"]), "wr": chunked(a["wr1"]), "wk": chunked(a["wkf1"]), "wv": chunked(a["wvf1"]),
                             "mu": a["mu"]}, kn["x2_d"], out)


def kernel(**inputs):
    import ml_dtypes as _md
    import numpy as _np
    import concourse.bacc as _bacc
    from concourse import mybir as _mybir
    from concourse.bass_utils import run_bass_kernel_spmd as _run

    x = {k: _np.asarray(v) for k, v in inputs.items()}

    eye = _np.eye(P, dtype=_np.float32)
    r = _np.arange(P)
    pick = (r[:, None] == (r[None, :] // VW) * VW + HD).astype(_np.float32)
    headsum = (r[:, None] // (HD // 2) == r[None, :] // (HD // 2)).astype(_np.float32)
    behind = _np.where(r[:, None] > r[None, :], MASKED, 0.0).astype(_np.float32)
    inv_freq = _np.float32(1.0) / _np.power(_np.float32(10000.0), _np.arange(0, HD, 2, dtype=_np.float32) / _np.float32(HD))
    freqs = _np.arange(T, dtype=_np.float32)[:, None] * inv_freq[None, :].astype(_np.float32)
    emb = freqs[:, r % (HD // 2)].T

    def t(a):
        return _np.ascontiguousarray(_np.asarray(a).T)

    def halves(a):
        return a.reshape(H, 2, HD // 2, D).transpose(1, 0, 2, 3).reshape(D, D)

    def spread(a, n):
        return _np.ascontiguousarray(_np.broadcast_to(_np.asarray(a), (n,) + _np.asarray(a).shape))

    qkv = x["L0_attn_qkv_w"]
    arrays = {
        "consts": _np.stack([eye, _np.ones((P, P), _np.float32), pick]),
        "constsb": _np.stack([eye, headsum, behind, behind.T]).astype(_md.bfloat16),
        "ones_rows": _np.ones((3, HQ * T), dtype=_md.bfloat16),
        "cos": _np.cos(emb).astype(_np.float32), "sin": _np.sin(emb).astype(_np.float32),
        "L0_attn_x": _np.ascontiguousarray(x["L0_attn_x"].reshape(B * T, D)),
        "wq0": t(qkv[:D]), "wk0": t(qkv[D:2 * D]), "wv0": t(qkv[2 * D:]), "wo0": t(x["L0_attn_out_w"]),
        "w12": t(_np.concatenate([x["L0_attn_hex_w"], x["L0_attn_q6_w"]])),
        "L0_attn_transforms": x["L0_attn_transforms"],
        "tw": spread(x["L0_attn_transform_weights"], NF),
        "scalars": spread(_np.stack([x["L0_attn_hamming_lambda_logit"].reshape(()), x["L0_attn_scale_logit"].reshape(()),
                                     x["L0_attn_sips_alpha"].reshape(()), x["L0_attn_sips_beta"].reshape(())]), P),
        "L0_ffn_kernel": x["L0_ffn_kernel"], "ffn_a_t": t(x["L0_ffn_a"]), "L0_ffn_b": x["L0_ffn_b"],
        "bias": spread(x["L0_ffn_bias"], P),
        "wq1": t(halves(x["L1_attn_Wq"])), "wk1": t(halves(x["L1_attn_Wk"])), "wv1": t(x["L1_attn_Wv"]), "wo1": t(x["L1_attn_Wo"]),
        "wr1": t(x["L1_ffn_W_r"]), "wkf1": t(x["L1_ffn_W_k"]), "wvf1": t(x["L1_ffn_W_v"]),
        "mu": _np.ascontiguousarray(_np.stack([x["L1_ffn_mu_r"], x["L1_ffn_mu_k"]]).reshape(2, DC, P).transpose(2, 0, 1)),
    }
    nc = _bacc.Bacc("TRN2", target_bir_lowering=False, num_devices=1)
    aps = {n: nc.dram_tensor(f"in_{n}", v.shape, _mybir.dt.from_np(v.dtype), kind="ExternalInput").ap() for n, v in arrays.items()}
    out = nc.dram_tensor("out", (B * T, D), _mybir.dt.float32, kind="ExternalOutput").ap()
    two_blocks(nc, aps, out)
    res = _run(nc, [{f"in_{n}": _np.ascontiguousarray(v) for n, v in arrays.items()}], core_ids=[0])
    return res.results[0]["out"].reshape(B, T, D)
```
